# Optimizing a Trainium2 kernel written in Bass

```python
import numpy as np
import jax
import jax.numpy as jnp

def _softmax(x, axis=-1):
    return jax.nn.softmax(x, axis=axis)

def _gelu(x):
    return jax.nn.gelu(x, approximate=True)

def _silu(x):
    return jax.nn.silu(x)

def _sigmoid(x):
    return jax.nn.sigmoid(x)

def _layernorm(x, axis=-1, eps=1e-05):
    m = jnp.mean(x, axis=axis, keepdims=True)
    v = jnp.var(x, axis=axis, keepdims=True)
    return (x - m) / jnp.sqrt(v + eps)

def _scatter_add(tgt, idx, src, axis=0):
    return tgt.at[idx].add(src)

def _segment_sum(src, seg, n):
    return jax.ops.segment_sum(src, seg, n)
kernel_name = 'mk_early_fusion_d1_tok_img768_r4_1eea0d'

def setup_inputs(seed: int=0):
    np.random.seed(seed)
    _w = jnp.asarray

    def _rec_inputs():
        import jax
        import jax.numpy as jnp
        _rk = jax.random.key(seed)
        x = -0.00040386 + 0.999972 * jax.random.normal(jax.random.fold_in(_rk, 1), (16, 3, 128, 128), jnp.float32)
        txt = 0.198809 + 1.28268 * jax.random.normal(jax.random.fold_in(_rk, 2), (16, 32, 192), jnp.float32)
        return (x, txt)
    x, txt = _rec_inputs()

    def _L0_tok_setup():
        import jax, jax.numpy as jnp
        import numpy as np
        P = 16
        WIN = 64
        NH = 12

        def _layernorm(x, g, b, eps=1e-05):
            m = x.mean(-1, keepdims=True)
            v = ((x - m) ** 2).mean(-1, keepdims=True)
            return (x - m) * jax.lax.rsqrt(v + eps) * g + b

        def _sinusoidal_pe(n, d):
            pos = jnp.arange(n, dtype=jnp.float32)[:, None]
            i = jnp.arange(d // 2, dtype=jnp.float32)[None, :]
            ang = pos / jnp.power(10000.0, 2.0 * i / d)
            pe = jnp.zeros((n, d), jnp.float32)
            pe = pe.at[:, 0::2].set(jnp.sin(ang)).at[:, 1::2].set(jnp.cos(ang))
            return pe
        key = jax.random.key(seed)
        ks = jax.random.split(key, 8)
        B, C, H, W, D, F = (16, 3, 128, 128, 192, 768)
        s = lambda k, shape: jax.random.normal(k, shape, jnp.float32) * 0.02
        return {'input': jax.random.normal(ks[0], (B, C, H, W), jnp.float32), 'patch_w': s(ks[1], (D, C, P, P)), 'patch_b': jnp.zeros((D,), jnp.float32), 'ln_g': jnp.ones((D,), jnp.float32), 'ln_b': jnp.zeros((D,), jnp.float32), 'qkv_w': s(ks[2], (D, 3 * D)), 'qkv_b': jnp.zeros((3 * D,), jnp.float32), 'proj_w': s(ks[3], (D, D)), 'proj_b': jnp.zeros((D,), jnp.float32), 'ff1_w': s(ks[4], (D, F)), 'ff1_b': jnp.zeros((F,), jnp.float32), 'ff2_w': s(ks[5], (F, D)), 'ff2_b': jnp.zeros((D,), jnp.float32)}
    _L0_tok_all = _L0_tok_setup()
    _L0_tok_in = {k: v for k, v in _L0_tok_all.items() if k in ('patch_w', 'patch_b', 'ln_g', 'ln_b', 'qkv_w', 'qkv_b', 'proj_w', 'proj_b', 'ff1_w', 'ff1_b', 'ff2_w', 'ff2_b')}
    del _L0_tok_all

    def _L0_attn_setup():
        import jax, jax.numpy as jnp
        import numpy as np
        D = 192
        H = 12
        D_INNER = 384
        K_CONV = 4
        HIDDEN = 768
        EPS = 1e-05

        def _ln(x, g, b):
            m = x.mean(-1, keepdims=True)
            v = ((x - m) ** 2).mean(-1, keepdims=True)
            return (x - m) * jax.lax.rsqrt(v + EPS) * g + b

        def _ssm(x, in_proj_w, conv_w, conv_b, out_proj_w):
            xz = x @ in_proj_w
            xb, z = jnp.split(xz, 2, axis=-1)
            lhs = xb.transpose(0, 2, 1)
            rhs = conv_w[:, None, :]
            y = jax.lax.conv_general_dilated(lhs, rhs, window_strides=(1,), padding=[(K_CONV - 1, 0)], dimension_numbers=('NCH', 'OIH', 'NCH'), feature_group_count=D_INNER)
            y = (y + conv_b[None, :, None]).transpose(0, 2, 1)
            y = jax.nn.silu(y) * jax.nn.silu(z)
            return y @ out_proj_w

        def _attn(x, qkv_w, qkv_b, num_heads):
            B, N, Dm = x.shape
            hd = Dm // num_heads
            qkv = (x @ qkv_w + qkv_b).reshape(B, N, 3, num_heads, hd)
            q, k, v = (qkv[:, :, 0], qkv[:, :, 1], qkv[:, :, 2])
            scale = hd ** (-0.5)
            scores = jnp.einsum('bqhd,bkhd->bhqk', q, k) * scale
            attn = jax.nn.softmax(scores, axis=-1)
            out = jnp.einsum('bhqk,bkhd->bqhd', attn, v)
            return out.reshape(B, N, Dm)
        key = jax.random.key(seed)
        ks = jax.random.split(key, 20)
        s = 0.02
        inp = {'x': jax.random.normal(ks[0], (2, 512, D), dtype=jnp.float32), 'ln1_g': jnp.ones((D,), jnp.float32), 'ln1_b': jnp.zeros((D,), jnp.float32), 'in_proj_w': jax.random.normal(ks[1], (D, 2 * D_INNER), jnp.float32) * s, 'conv_w': jax.random.normal(ks[2], (D_INNER, K_CONV), jnp.float32) * s, 'conv_b': jnp.zeros((D_INNER,), jnp.float32), 'out_proj_w': jax.random.normal(ks[3], (D_INNER, D), jnp.float32) * s, 'ln2_g': jnp.ones((D,), jnp.float32), 'ln2_b': jnp.zeros((D,), jnp.float32), 'qkv_w': jax.random.normal(ks[4], (D, 3 * D), jnp.float32) * s, 'qkv_b': jnp.zeros((3 * D,), jnp.float32), 'attn_proj_w': jax.random.normal(ks[5], (D, D), jnp.float32) * s, 'attn_proj_b': jnp.zeros((D,), jnp.float32), 'ln3_g': jnp.ones((D,), jnp.float32), 'ln3_b': jnp.zeros((D,), jnp.float32), 'ffn1_w': jax.random.normal(ks[6], (D, HIDDEN), jnp.float32) * s, 'ffn1_b': jnp.zeros((HIDDEN,), jnp.float32), 'ffn2_w': jax.random.normal(ks[7], (HIDDEN, D), jnp.float32) * s, 'ffn2_b': jnp.zeros((D,), jnp.float32)}
        return inp
    _L0_attn_all = _L0_attn_setup()
    _L0_attn_in = {k: v for k, v in _L0_attn_all.items() if k in ('ln1_g', 'ln1_b', 'in_proj_w', 'conv_w', 'conv_b', 'out_proj_w', 'ln2_g', 'ln2_b', 'qkv_w', 'qkv_b', 'attn_proj_w', 'attn_proj_b', 'ln3_g', 'ln3_b', 'ffn1_w', 'ffn1_b', 'ffn2_w', 'ffn2_b')}
    del _L0_attn_all

    def _L0_ffn_setup():
        import jax, jax.numpy as jnp
        import numpy as np
        DIM = 192
        H = 12
        HD = 64
        SHARED = 2
        ROUTED = 2
        E_ROUTED = H - SHARED
        LN_EPS = 1e-05

        def _layernorm(x, w, b):
            m = x.mean(-1, keepdims=True)
            v = ((x - m) ** 2).mean(-1, keepdims=True)
            return (x - m) * jax.lax.rsqrt(v + LN_EPS) * w + b
        key = jax.random.key(seed)
        ks = jax.random.split(key, 12)
        B, N = (4, 512)
        s = 0.02
        return {'x': jax.random.normal(ks[0], (B, N, DIM), jnp.float32), 'qkv_w': jax.random.normal(ks[1], (DIM, 3 * H * HD), jnp.float32) * s, 'qkv_b': jnp.zeros((3 * H * HD,), jnp.float32), 'q_norm_w': jnp.ones((HD,), jnp.float32), 'q_norm_b': jnp.zeros((HD,), jnp.float32), 'k_norm_w': jnp.ones((HD,), jnp.float32), 'k_norm_b': jnp.zeros((HD,), jnp.float32), 'wg_w': jax.random.normal(ks[2], (DIM, E_ROUTED), jnp.float32) * s, 'wg0_w': jax.random.normal(ks[3], (DIM, 2), jnp.float32) * s, 'wg1_w': jax.random.normal(ks[4], (DIM, SHARED), jnp.float32) * s, 'proj_w': jax.random.normal(ks[5], (H * HD, DIM), jnp.float32) * s, 'proj_b': jnp.zeros((DIM,), jnp.float32)}
    _L0_ffn_all = _L0_ffn_setup()
    _L0_ffn_in = {k: v for k, v in _L0_ffn_all.items() if k in ('qkv_w', 'qkv_b', 'q_norm_w', 'q_norm_b', 'k_norm_w', 'k_norm_b', 'wg_w', 'wg0_w', 'wg1_w', 'proj_w', 'proj_b')}
    del _L0_ffn_all
    return {'x': x, 'txt': txt, 'L0_tok_patch_w': _L0_tok_in['patch_w'], 'L0_tok_patch_b': _L0_tok_in['patch_b'], 'L0_tok_ln_g': _L0_tok_in['ln_g'], 'L0_tok_ln_b': _L0_tok_in['ln_b'], 'L0_tok_qkv_w': _L0_tok_in['qkv_w'], 'L0_tok_qkv_b': _L0_tok_in['qkv_b'], 'L0_tok_proj_w': _L0_tok_in['proj_w'], 'L0_tok_proj_b': _L0_tok_in['proj_b'], 'L0_tok_ff1_w': _L0_tok_in['ff1_w'], 'L0_tok_ff1_b': _L0_tok_in['ff1_b'], 'L0_tok_ff2_w': _L0_tok_in['ff2_w'], 'L0_tok_ff2_b': _L0_tok_in['ff2_b'], 'L0_attn_ln1_g': _L0_attn_in['ln1_g'], 'L0_attn_ln1_b': _L0_attn_in['ln1_b'], 'L0_attn_in_proj_w': _L0_attn_in['in_proj_w'], 'L0_attn_conv_w': _L0_attn_in['conv_w'], 'L0_attn_conv_b': _L0_attn_in['conv_b'], 'L0_attn_out_proj_w': _L0_attn_in['out_proj_w'], 'L0_attn_ln2_g': _L0_attn_in['ln2_g'], 'L0_attn_ln2_b': _L0_attn_in['ln2_b'], 'L0_attn_qkv_w': _L0_attn_in['qkv_w'], 'L0_attn_qkv_b': _L0_attn_in['qkv_b'], 'L0_attn_attn_proj_w': _L0_attn_in['attn_proj_w'], 'L0_attn_attn_proj_b': _L0_attn_in['attn_proj_b'], 'L0_attn_ln3_g': _L0_attn_in['ln3_g'], 'L0_attn_ln3_b': _L0_attn_in['ln3_b'], 'L0_attn_ffn1_w': _L0_attn_in['ffn1_w'], 'L0_attn_ffn1_b': _L0_attn_in['ffn1_b'], 'L0_attn_ffn2_w': _L0_attn_in['ffn2_w'], 'L0_attn_ffn2_b': _L0_attn_in['ffn2_b'], 'L0_ffn_qkv_w': _L0_ffn_in['qkv_w'], 'L0_ffn_qkv_b': _L0_ffn_in['qkv_b'], 'L0_ffn_q_norm_w': _L0_ffn_in['q_norm_w'], 'L0_ffn_q_norm_b': _L0_ffn_in['q_norm_b'], 'L0_ffn_k_norm_w': _L0_ffn_in['k_norm_w'], 'L0_ffn_k_norm_b': _L0_ffn_in['k_norm_b'], 'L0_ffn_wg_w': _L0_ffn_in['wg_w'], 'L0_ffn_wg0_w': _L0_ffn_in['wg0_w'], 'L0_ffn_wg1_w': _L0_ffn_in['wg1_w'], 'L0_ffn_proj_w': _L0_ffn_in['proj_w'], 'L0_ffn_proj_b': _L0_ffn_in['proj_b']}

def reference(x, txt, L0_tok_patch_w, L0_tok_patch_b, L0_tok_ln_g, L0_tok_ln_b, L0_tok_qkv_w, L0_tok_qkv_b, L0_tok_proj_w, L0_tok_proj_b, L0_tok_ff1_w, L0_tok_ff1_b, L0_tok_ff2_w, L0_tok_ff2_b, L0_attn_ln1_g, L0_attn_ln1_b, L0_attn_in_proj_w, L0_attn_conv_w, L0_attn_conv_b, L0_attn_out_proj_w, L0_attn_ln2_g, L0_attn_ln2_b, L0_attn_qkv_w, L0_attn_qkv_b, L0_attn_attn_proj_w, L0_attn_attn_proj_b, L0_attn_ln3_g, L0_attn_ln3_b, L0_attn_ffn1_w, L0_attn_ffn1_b, L0_attn_ffn2_w, L0_attn_ffn2_b, L0_ffn_qkv_w, L0_ffn_qkv_b, L0_ffn_q_norm_w, L0_ffn_q_norm_b, L0_ffn_k_norm_w, L0_ffn_k_norm_b, L0_ffn_wg_w, L0_ffn_wg0_w, L0_ffn_wg1_w, L0_ffn_proj_w, L0_ffn_proj_b):
    import jax
    import jax.numpy as jnp

    def _L0_tok_ref(input, patch_w, patch_b, ln_g, ln_b, qkv_w, qkv_b, proj_w, proj_b, ff1_w, ff1_b, ff2_w, ff2_b):
        import jax, jax.numpy as jnp
        import numpy as np
        P = 16
        WIN = 64
        NH = 12

        def _layernorm(x, g, b, eps=1e-05):
            m = x.mean(-1, keepdims=True)
            v = ((x - m) ** 2).mean(-1, keepdims=True)
            return (x - m) * jax.lax.rsqrt(v + eps) * g + b

        def _sinusoidal_pe(n, d):
            pos = jnp.arange(n, dtype=jnp.float32)[:, None]
            i = jnp.arange(d // 2, dtype=jnp.float32)[None, :]
            ang = pos / jnp.power(10000.0, 2.0 * i / d)
            pe = jnp.zeros((n, d), jnp.float32)
            pe = pe.at[:, 0::2].set(jnp.sin(ang)).at[:, 1::2].set(jnp.cos(ang))
            return pe
        B, C, H, W = input.shape
        D = patch_w.shape[0]
        dh = D // NH
        xp = input.reshape(B, C, H // P, P, W // P, P)
        x = jnp.einsum('bchpwq,dcpq->bhwd', xp, patch_w) + patch_b
        x = x.reshape(B, -1, D)
        x = _layernorm(x, ln_g, ln_b)
        N = x.shape[1]
        x = x + _sinusoidal_pe(N, D)

        def ff(y):
            return jax.nn.gelu(y @ ff1_w + ff1_b) @ ff2_w + ff2_b

        def sparse_attn(y):
            nW = N // WIN
            qkv = (y @ qkv_w + qkv_b).reshape(B, nW, WIN, 3, NH, dh)
            q, k, v = (qkv[:, :, :, 0], qkv[:, :, :, 1], qkv[:, :, :, 2])
            scores = jnp.einsum('bwqhd,bwkhd->bwhqk', q, k) * dh ** (-0.5)
            a = jax.nn.softmax(scores, axis=-1)
            o = jnp.einsum('bwhqk,bwkhd->bwqhd', a, v).reshape(B, N, D)
            return o @ proj_w + proj_b
        identity = x
        x = ff(x)
        x = sparse_attn(x)
        x = x + identity
        identity = x
        x = ff(x)
        x = x + identity
        return x

    def _L0_attn_ref(x, ln1_g, ln1_b, in_proj_w, conv_w, conv_b, out_proj_w, ln2_g, ln2_b, qkv_w, qkv_b, attn_proj_w, attn_proj_b, ln3_g, ln3_b, ffn1_w, ffn1_b, ffn2_w, ffn2_b):
        import jax, jax.numpy as jnp
        import numpy as np
        D = 192
        H = 12
        D_INNER = 384
        K_CONV = 4
        HIDDEN = 768
        EPS = 1e-05

        def _ln(x, g, b):
            m = x.mean(-1, keepdims=True)
            v = ((x - m) ** 2).mean(-1, keepdims=True)
            return (x - m) * jax.lax.rsqrt(v + EPS) * g + b

        def _ssm(x, in_proj_w, conv_w, conv_b, out_proj_w):
            xz = x @ in_proj_w
            xb, z = jnp.split(xz, 2, axis=-1)
            lhs = xb.transpose(0, 2, 1)
            rhs = conv_w[:, None, :]
            y = jax.lax.conv_general_dilated(lhs, rhs, window_strides=(1,), padding=[(K_CONV - 1, 0)], dimension_numbers=('NCH', 'OIH', 'NCH'), feature_group_count=D_INNER)
            y = (y + conv_b[None, :, None]).transpose(0, 2, 1)
            y = jax.nn.silu(y) * jax.nn.silu(z)
            return y @ out_proj_w

        def _attn(x, qkv_w, qkv_b, num_heads):
            B, N, Dm = x.shape
            hd = Dm // num_heads
            qkv = (x @ qkv_w + qkv_b).reshape(B, N, 3, num_heads, hd)
            q, k, v = (qkv[:, :, 0], qkv[:, :, 1], qkv[:, :, 2])
            scale = hd ** (-0.5)
            scores = jnp.einsum('bqhd,bkhd->bhqk', q, k) * scale
            attn = jax.nn.softmax(scores, axis=-1)
            out = jnp.einsum('bhqk,bkhd->bqhd', attn, v)
            return out.reshape(B, N, Dm)
        x = x + _ssm(_ln(x, ln1_g, ln1_b), in_proj_w, conv_w, conv_b, out_proj_w)
        a = _attn(_ln(x, ln2_g, ln2_b), qkv_w, qkv_b, H)
        x = x + a @ attn_proj_w + attn_proj_b
        h = jax.nn.gelu(_ln(x, ln3_g, ln3_b) @ ffn1_w + ffn1_b, approximate=False)
        x = x + h @ ffn2_w + ffn2_b
        return x

    def _L0_ffn_ref(x, qkv_w, qkv_b, q_norm_w, q_norm_b, k_norm_w, k_norm_b, wg_w, wg0_w, wg1_w, proj_w, proj_b):
        import jax, jax.numpy as jnp
        import numpy as np
        DIM = 192
        H = 12
        HD = 64
        SHARED = 2
        ROUTED = 2
        E_ROUTED = H - SHARED
        LN_EPS = 1e-05

        def _layernorm(x, w, b):
            m = x.mean(-1, keepdims=True)
            v = ((x - m) ** 2).mean(-1, keepdims=True)
            return (x - m) * jax.lax.rsqrt(v + LN_EPS) * w + b
        B, N, C = x.shape
        scale = HD ** (-0.5)
        gates = jax.nn.softmax(x @ wg_w, axis=-1)
        _, idx = jax.lax.top_k(gates, ROUTED)
        mask = jax.nn.one_hot(idx, E_ROUTED, dtype=gates.dtype).sum(-2)
        rg = gates * mask
        denom = jnp.clip(rg.sum(-1, keepdims=True), jnp.finfo(rg.dtype).eps, None)
        routed_gates = rg / denom * ROUTED
        qkv = (x @ qkv_w + qkv_b).reshape(B, N, 3, H, HD)
        qkv = jnp.transpose(qkv, (2, 0, 3, 1, 4))
        q, k, v = (qkv[0], qkv[1], qkv[2])
        q = _layernorm(q, q_norm_w, q_norm_b)
        k = _layernorm(k, k_norm_w, k_norm_b)
        attn = jax.nn.softmax(jnp.einsum('bhqd,bhkd->bhqk', q * scale, k), axis=-1)
        o = jnp.einsum('bhqk,bhkd->bhqd', attn, v)
        o = jnp.transpose(o, (0, 2, 1, 3))
        shared_gates = jax.nn.softmax(x @ wg1_w, axis=-1) * SHARED
        w0 = jax.nn.softmax(x @ wg0_w, axis=-1) * 2.0
        shared_gates = w0[..., 0:1] * shared_gates
        routed_gates = w0[..., 1:2] * routed_gates
        masked_gates = jnp.concatenate([shared_gates, routed_gates], axis=-1)
        o = (masked_gates[..., None] * o).reshape(B, N, H * HD)
        return o @ proj_w + proj_b
    h = _L0_tok_ref(x, L0_tok_patch_w, L0_tok_patch_b, L0_tok_ln_g, L0_tok_ln_b, L0_tok_qkv_w, L0_tok_qkv_b, L0_tok_proj_w, L0_tok_proj_b, L0_tok_ff1_w, L0_tok_ff1_b, L0_tok_ff2_w, L0_tok_ff2_b)
    h = jnp.concatenate([h, txt], axis=1)
    h = h + _L0_attn_ref(_layernorm(h, axis=-1), L0_attn_ln1_g, L0_attn_ln1_b, L0_attn_in_proj_w, L0_attn_conv_w, L0_attn_conv_b, L0_attn_out_proj_w, L0_attn_ln2_g, L0_attn_ln2_b, L0_attn_qkv_w, L0_attn_qkv_b, L0_attn_attn_proj_w, L0_attn_attn_proj_b, L0_attn_ln3_g, L0_attn_ln3_b, L0_attn_ffn1_w, L0_attn_ffn1_b, L0_attn_ffn2_w, L0_attn_ffn2_b)
    h = h + _L0_ffn_ref(_layernorm(h, axis=-1), L0_ffn_qkv_w, L0_ffn_qkv_b, L0_ffn_q_norm_w, L0_ffn_q_norm_b, L0_ffn_k_norm_w, L0_ffn_k_norm_b, L0_ffn_wg_w, L0_ffn_wg0_w, L0_ffn_wg1_w, L0_ffn_proj_w, L0_ffn_proj_b)
    return h

_drawn_inputs = setup_inputs


def setup_inputs(seed=0):
    import zlib

    import numpy as np

    out = dict(_drawn_inputs(seed))
    spreads = {'L0_tok_patch_b': (0.0, 0.1),
     'L0_tok_ln_g': (1.0, 0.2),
     'L0_tok_ln_b': (0.0, 0.1),
     'L0_tok_qkv_b': (0.0, 0.481),
     'L0_tok_proj_b': (0.0, 0.1),
     'L0_tok_ff1_b': (0.0, 0.392),
     'L0_tok_ff2_b': (0.0, 0.1),
     'L0_attn_ln1_g': (1.0, 0.6),
     'L0_attn_ln1_b': (0.0, 0.8),
     'L0_attn_conv_b': (0.0, 0.8),
     'L0_attn_ln2_g': (1.0, 0.6),
     'L0_attn_ln2_b': (0.0, 0.8),
     'L0_attn_qkv_b': (0.0, 0.62),
     'L0_attn_attn_proj_b': (0.0, 0.386),
     'L0_attn_ln3_g': (1.0, 0.6),
     'L0_attn_ln3_b': (0.0, 2.0),
     'L0_attn_ffn1_b': (0.0, 0.554),
     'L0_attn_ffn2_b': (0.0, 0.433),
     'L0_ffn_qkv_b': (0.0, 0.572),
     'L0_ffn_q_norm_w': (1.0, 0.6),
     'L0_ffn_q_norm_b': (0.0, 0.8),
     'L0_ffn_k_norm_w': (1.0, 0.6),
     'L0_ffn_k_norm_b': (0.0, 2.0),
     'L0_ffn_proj_b': (0.0, 0.641)}
    factors = {'L0_tok_qkv_w': 8.0,
     'L0_tok_proj_w': 3.141,
     'L0_attn_in_proj_w': 8.0,
     'L0_attn_conv_w': 8.0,
     'L0_attn_out_proj_w': 8.0,
     'L0_attn_qkv_w': 5.365,
     'L0_attn_attn_proj_w': 3.449,
     'L0_ffn_qkv_w': 4.669,
     'L0_ffn_wg_w': 4.712,
     'L0_ffn_wg0_w': 8.0,
     'L0_ffn_wg1_w': 8.0,
     'L0_ffn_proj_w': 3.195}
    for name, (base, spread) in spreads.items():
        noise = np.random.default_rng([zlib.crc32(name.encode()), seed]).standard_normal(out[name].shape)
        drawn = base * np.exp(spread * noise) if base else spread * noise
        out[name] = jnp.asarray(drawn.astype(out[name].dtype))
    for name, factor in factors.items():
        out[name] = (out[name] * factor).astype(out[name].dtype)
    return out
```

```python
from contextlib import ExitStack

import numpy as np

import concourse.bass as bass
from concourse import mybir

F32 = mybir.dt.float32
ACT = mybir.ActivationFunctionType
ALU = mybir.AluOpType
AX = mybir.AxisListType

B, CH, IMG, P = 16, 3, 128, 16
D, F, NH = 192, 768, 12
NI, NT = (IMG // P) ** 2, 32
N = NI + NT
GS = 4
NG = B // GS
HC = 96
TA, TB = GS * NI, GS * N
HD, HD2 = D // NH, 64
DI, KC = 2 * D, 4
TILES_A, TILES_B = TA // 128, TB // 128
KP = CH * P * P // 128
EXPERTS = NH - 2
EPS = 1e-5

V96 = {"tok_g": 0, "tok_ff2_b": 2, "ln1_g": 4, "ln1_b": 6, "ln2_g": 8, "ln2_b": 10, "ln3_g": 12, "ln3_b": 14,
       "tok_b": 16, "n": 18}
V128 = {"conv_w": 0, "conv_b": 12, "q_w": 15, "q_b": 16, "k_w": 17, "k_b": 18, "n": 19}

A_STEPS = [[("a_em", 0)], [("a_x0", 0)], [("a_f1", 0)], [("a_f2", 0)], [("a_qk", 0), ("a_v", 0)],
           [("a_s", 0), ("a_s", 1)], [("a_pt", 0), ("a_o", 0), ("a_ot", 0)], [("a_pt", 1), ("a_o", 1), ("a_ot", 1)],
           [("a_pr", 0)], [("a_f1", 1)], [("a_f2", 1)]]
B_ATT = [[("b_s", 0), ("b_s", 1)], [("b_pt", 0), ("b_o", 0), ("b_s", 2), ("b_ot", 0)],
         [("b_pt", 1), ("b_o", 1), ("b_s", 3), ("b_ot", 1)], [("b_pt", 2), ("b_o", 2), ("b_ot", 2)],
         [("b_pt", 3), ("b_o", 3), ("b_ot", 3)]]
C_ATT = [[("c_s", 0), ("c_v", 0), ("c_s", 1)], [("c_pt", 0), ("c_o", 0), ("c_s", 2), ("c_v", 1), ("c_ot", 0)],
         [("c_pt", 1), ("c_o", 1), ("c_s", 3), ("c_v", 2), ("c_ot", 1)], [("c_pt", 2), ("c_o", 2), ("c_v", 3), ("c_ot", 2)],
         [("c_pt", 3), ("c_o", 3), ("c_ot", 3)]]
B_STEPS = [[("b_ht", 0)], [("b_u", 0)], [("b_in", 0), ("b_in", 1)], [("b_out", 0)], [("b_u", 1)],
           [("b_q", 0), ("b_k", 0), ("b_v", 0)], *B_ATT, [("b_pr", 0)], [("b_u", 2)],
           [("b_f1", 0), ("b_f1", 1)], [("b_f2", 0)], [("b_u", 3)], [("c_g", 0), ("c_qk", 0), ("c_qk", 1)],
           [("c_qt", 0), ("c_qk", 2)], [("c_qt", 1), ("c_qt", 2)], *C_ATT, [("c_pr", 0)]]


def flat(steps):
    return [u for part in steps for u in part]


def woven():
    after = [1, 2, 3, 4, 6, 9, 11, 12, 13, 15, 19]
    out = []
    for n, part in enumerate(B_STEPS):
        out += part
        for m, a in enumerate(A_STEPS):
            if after[m] == n + 1:
                out += a
    return out


ORDER = {"first": flat(A_STEPS), "loop": woven(), "last": flat(B_STEPS)}
SLOT_OF = {"a_em": "T", "a_x0": "S", "a_f1": "T", "a_f2": "S", "a_qk": "T", "a_v": "S", "a_s": "T", "a_pt": "T",
           "a_o": "S", "a_ot": "S", "a_pr": "S", "b_ht": "T", "b_u": "T", "b_in": "T", "b_out": "T", "b_q": "T",
           "b_k": "T", "b_v": "T", "b_s": "T", "b_pt": "T", "b_o": "S", "b_ot": "S", "b_pr": "T", "b_f1": "T",
           "b_f2": "T", "c_g": "S", "c_qk": "T", "c_qt": "T", "c_v": "D", "c_s": "T", "c_pt": "T", "c_o": "D",
           "c_ot": "D", "c_pr": "T"}
READ_BY = {
    "a_em": lambda k: [("a_emb", 1)], "a_x0": lambda k: [("x0T", 2)], "a_f1": lambda k: [("a_h", 3 * k + 3)],
    "a_f2": lambda k: [("hT", 2) if k else ("x1T", 2)], "a_qk": lambda k: [("a_qT", 1), ("a_kT", 1)],
    "a_v": lambda k: [("a_vB", 1)], "a_s": lambda k: [("a_sub", k + 1)], "a_pt": lambda k: [("a_pT", k + 1)],
    "a_o": lambda k: [("a_on", k + 1)], "a_ot": lambda k: [("a_oT", k + 1)], "a_pr": lambda k: [("x2T", 1)],
    "b_ht": lambda k: [("h_tm", 1)], "b_u": lambda k: [("lnT", 2 * k + 2)],
    "b_in": lambda k: [("sz", 1) if k else ("xpad", 1)], "b_out": lambda k: [("x1_tm", 1)],
    "b_q": lambda k: [("b_qT", 1)], "b_k": lambda k: [("b_kT", 1)], "b_v": lambda k: [("b_vO", 1)],
    "b_s": lambda k: [("b_sub", k + 1)], "b_pt": lambda k: [("b_pT", k + 1)], "b_o": lambda k: [("b_on", k + 1)],
    "b_ot": lambda k: [("b_oT", k + 1)], "b_pr": lambda k: [("x2_tm", 1)], "b_f1": lambda k: [("b_h", k + 1)],
    "b_f2": lambda k: [("h2_tm", 1)], "c_g": lambda k: [("g_step", 4)], "c_qk": lambda k: [("qkn", k + 1)],
    "c_qt": lambda k: [("c_qkT", k + 1)], "c_v": lambda k: [("c_v", k + 1)], "c_s": lambda k: [("c_sub", k + 1)],
    "c_pt": lambda k: [("c_pT", k + 1)], "c_o": lambda k: [("c_on", k + 1)], "c_ot": lambda k: [("c_oT", k + 1)],
    "c_pr": lambda k: [("out_tm", 1)],
}


class PsumFills:

    def __init__(self):
        self.at, self.start, self.per, self.last = {}, {}, {}, {}
        total = dict.fromkeys(("T0", "T1", "S0", "S1"), 0)
        for section in ("first", "loop", "last"):
            self.start[section] = dict(total)
            count = dict.fromkeys(total, 0)
            turn = {"T": 0, "S": 0}
            holder = {}
            for unit in ORDER[section]:
                kind = SLOT_OF[unit[0]]
                slot = "S0" if kind == "D" else kind + str(turn[kind] % 2)
                if kind != "D":
                    turn[kind] += 1
                taken = ("S0", "S1") if kind == "D" else (slot,)
                before = sorted({holder[bank] for bank in taken if bank in holder})
                for bank in taken:
                    holder[bank] = unit
                count[slot] += 1
                self.at[section, unit] = (slot, before, count[slot])
            self.per[section] = count
            self.last[section] = sorted(set(holder.values()))
            for s in total:
                total[s] += count[s] * (NG - 1 if section == "loop" else 1)


FILLS = PsumFills()

PER_GROUP = {
    "x_in": 16, "txt_in": 16, "a_emb": 1, "a_stats": 2, "a_mv": 2, "a_lnv": 1, "a_rstd": 1, "a_xn": 2, "x0T": 2,
    "a_h": 6, "x1T": 2, "a_qT": 1, "a_kT": 1, "a_kB": 4, "a_vB": 1, "a_max": 2, "a_sub": 2, "a_exp": 2, "a_pT": 2,
    "a_rec": 2, "a_on": 2, "a_oT": 2, "x2T": 1, "hT": 2,
    "h_tm": 1, "ln_stats": 12, "ln_mv": 12, "ln_log": 4, "ln_rstd": 4, "ln1_sq": 1, "ln1_var": 1, "ln1_log": 1,
    "ln1_rstd": 1, "ln1_both": 1, "ln_u": 12, "y_tm": 3, "lnT": 8,
    "xpad": 1, "sz": 1, "conv": 12, "conv_act": 3, "gate": 3, "x1_tm": 1, "b_qT": 1, "b_kT": 1, "b_kB": 8,
    "b_vO": 1, "b_max": 4, "b_sub": 4, "b_exp": 4, "b_pT": 4, "b_rec": 4, "b_on": 4, "b_oT": 4, "x2_tm": 1,
    "hx": 2, "b_h": 2, "h2_tm": 1, "h2b": 1,
    "logits": 1, "g_step": 23, "g_exp": 1, "gates": 2, "sq": 3, "ss": 3, "qk_log": 3, "qk_rstd": 3, "qkn": 3,
    "c_qkT": 3, "c_ones": 1, "c_v": 4, "c_max": 4, "c_sub": 4, "c_exp": 4, "c_pT": 4, "c_rec": 4, "c_gr": 4,
    "c_on": 4, "c_oT": 4, "out_tm": 1, "out_dma": 16, "out_room": 1, "pad": 1,
}


def program(nc, xT, txtT, patchT, ident, peT, mask, prio, vec96, vec128, patch_b, tok_ff1, tok_ff2, tok_qkv, tok_proj,
            in_proj, out_proj, qkv, attn_proj, ffn1, ffn2, ffn2_b, cqkv, cproj, cproj_b, cgate, out):
    ctx = ExitStack()
    with ctx:
        def sb(name, shape):
            return ctx.enter_context(nc.sbuf_tensor(name, shape, F32))

        def sem(name):
            return ctx.enter_context(nc.semaphore(name))

        w_patch = sb("w_patch", [128, KP, D])
        w_ident = sb("w_ident", [128, 128])
        w_pe = sb("w_pe", [HC, 2, NI])
        w_mask = sb("w_mask", [HC, 6])
        w_prio = sb("w_prio", [N, EXPERTS])
        v96 = sb("v96", [HC, V96["n"]])
        v128 = sb("v128", [128, V128["n"]])
        w_patch_b = sb("w_patch_b", [128, D])
        w_tff1 = sb("w_tff1", [HC + 1, 2, F])
        w_tff2 = sb("w_tff2", [128, F // 128, D])
        w_tqkv = sb("w_tqkv", [HC + 1, 2, 3 * D])
        w_tproj = sb("w_tproj", [HC + 1, 2, D])
        w_in = sb("w_in", [HC, 2, 2 * DI])
        w_out = sb("w_out", [128, DI // 128, D])
        w_qkv = sb("w_qkv", [HC + 1, 2, 3 * D])
        w_proj = sb("w_proj", [HC + 1, 2, D])
        w_ff1 = sb("w_ff1", [HC + 1, 2, F])
        w_ff2 = sb("w_ff2", [128, F // 128, D])
        w_ff2_b = sb("w_ff2_b", [128, D])
        w_cqkv = sb("w_cqkv", [HC + 1, 2, 3 * NH * HD2])
        w_cproj = sb("w_cproj", [128, NH * HD2 // 128, D])
        w_cproj_b = sb("w_cproj_b", [128, D])
        w_cgate = sb("w_cgate", [HC, 2, EXPERTS + 4])
        w_mean = sb("w_mean", [HC + 1, 2, 2 * NH])
        eps = sb("eps", [128, 1])
        x_in = sb("x_in", [128, KP, TA])
        a_emb = sb("a_emb", [128, TILES_A, D])
        a_bn = sb("a_bn", [128, TILES_A, 6])
        a_mv = sb("a_mv", [128, TILES_A, 2])
        a_lnv = sb("a_lnv", [128, TILES_A])
        a_rstd = sb("a_rstd", [128, TILES_A])
        x0T = sb("x0T", [HC + 1, 2, TA])
        x1T = sb("x1T", [HC + 1, 2, TA])
        x2T = sb("x2T", [HC + 1, 2, TA])
        a_wide = sb("a_wide", [128, F // 128 * TA])
        a_h = a_wide[:, :].rearrange("p (c t) -> p c t", t=TA)
        a_kB = a_wide[0:HC, :].rearrange("p (c h t) -> p c h t", c=2, h=6)
        a_qT = sb("a_qT", [HC, 2, TA])
        a_kT = sb("a_kT", [HC, 2, TA])
        a_vB = sb("a_vB", [128, GS, NH // 2, 2 * (HD + 1)])
        a_p = sb("a_p", [128, 2, NH * NI])
        a_pT = sb("a_pT", [128, NH // 2, 128])
        a_max = sb("a_max", [128, 2, NH])
        a_rec = sb("a_rec", [128, 2, NH])
        a_on = sb("a_on", [128, D])
        a_oT = sb("a_oT", [HC + 1, 2, TA])
        hT = sb("hT", [HC, 2, GS, N])
        h_tm = sb("h_tm", [128, TILES_B, D])
        xr = sb("xr", [128, TILES_B, D])
        hx = sb("hx", [128, TILES_B, D])
        u = sb("u", [128, TILES_B, D])
        bn = sb("bn", [128, TILES_B, 6])
        mv = sb("mv", [128, TILES_B, 2])
        lnv = sb("lnv", [128, TILES_B])
        seen = sb("seen", [128, TILES_A + TILES_B])
        rstd = sb("rstd", [128, TILES_B])
        ln1 = sb("ln1", [128, 5, TILES_B])
        bT = sb("bT", [HC + 1, 2, TB])
        scratch = sb("scratch", [128, DI // 128 * GS * (N + KC - 1) + 2 * DI // 128 * TB])
        n0, n1 = DI // 128 * GS * (N + KC - 1), DI // 128 * TB
        xpad = scratch[:, 0:n0].rearrange("p (c s t) -> p c s t", c=DI // 128, s=GS)
        cv = scratch[:, n0:n0 + n1].rearrange("p (c s t) -> p c s t", c=DI // 128, s=GS)
        sz = scratch[:, n0 + n1:n0 + 2 * n1].rearrange("p (c t) -> p c t", c=DI // 128)
        qkw = 2 * NH * HD2
        sq = scratch[:, 0:qkw]
        qkn = scratch[:, qkw:2 * qkw]
        heads = sb("heads", [128, 1560 + GS * NH * (HD + 1)])
        b_qT = heads[0:HC, 0:2 * TB].rearrange("p (c t) -> p c t", c=2)
        b_kT = heads[0:HC, 2 * TB:4 * TB].rearrange("p (c t) -> p c t", c=2) if 4 * TB <= 1560 else None
        b_vO = heads[0:N, 1560:].rearrange("p (s h d) -> p s h d", s=GS, h=NH)
        c_v = heads[0:N, 0:1560].rearrange("p (b h d) -> p b h d", b=2, h=NH)
        b_kB = sb("b_kB", [128, 2 * 2 * 6 * N])
        b_kBv = b_kB[0:HC, :].rearrange("p (b c h t) -> p b c h t", b=2, c=2, h=6)
        c_oT = b_kB[:, :].rearrange("p (c t) -> p c t", c=NH * HD2 // 128)
        pr = sb("pr", [N, 2, NH * N])
        pT = sb("pT", [N, NH, N])
        smax = sb("smax", [N, 2, NH])
        rec = sb("rec", [N, 2, NH])
        gr = sb("gr", [N, 2, NH])
        on = sb("on", [N, NH * HD2])
        b_wide = sb("b_wide", [128, F // 128 * TB])
        b_h = b_wide[:, :].rearrange("p (c t) -> p c t", t=TB)
        c_qT = b_h
        c_kB = sb("c_kB", [128, NH // 2, 2, TB])
        gsm = sb("gsm", [N, 12, GS, EXPERTS + 4])
        gates = sb("gates", [N, GS, NH])
        ss = sb("ss", [128, 3, 2 * NH])

        ps = {"T0": ctx.enter_context(nc.psum_tensor("psT0", [128, 3, 512], F32)),
              "T1": ctx.enter_context(nc.psum_tensor("psT1", [128, 3, 512], F32))}
        psS = ctx.enter_context(nc.psum_tensor("psS", [128, 2, 512], F32))

        S = {name: sem(name) for name in PER_GROUP}
        filled = {s: sem("filled_" + s) for s in ("T0", "T1", "S0", "S1")}
        loads = {n: sem("load_" + n) for n in ("patch", "vec", "tff1", "tff2", "tqkv", "tproj", "in", "out", "qkv",
                                               "proj", "ff1", "ff2", "cqkv", "cproj", "ident")}
        n_loads = {"patch": 1, "vec": 8, "tff1": 1, "tff2": 1, "tqkv": 1, "tproj": 1, "in": 1, "out": 1, "qkv": 1,
                   "proj": 1, "ff1": 1, "ff2": 1, "cqkv": 1, "cproj": 2, "ident": 1}
        s_set = sem("constants_set")
        s_mean = sem("weight_mean")
        s_centred = sem("weight_centred")

        class Where:

            def __init__(self, section, step, group_a, group_b):
                self.section, self.step, self.a, self.b = section, step, group_a, group_b

        def upto(name, group, k=None):
            return group * PER_GROUP[name] + (PER_GROUP[name] if k is None else k)

        def slot(w, unit):
            s = FILLS.at[w.section, unit][0]
            if s[0] == "T":
                return ps[s]
            return psS[:, :, :] if SLOT_OF[unit[0]] == "D" else psS[:, int(s[1]), :]

        def reads(w, unit):
            return [(S[name], upto(name, w.a if unit[0][0] == "a" else w.b, k)) for name, k in
                    READ_BY[unit[0]](unit[1])]

        def reads_before(w, unit):
            return [r for before in FILLS.at[w.section, unit][1] for r in reads(w, before)]

        def fill_count(w, unit):
            s, _, n = FILLS.at[w.section, unit]
            return w.step * FILLS.per[w.section][s] + FILLS.start[w.section][s] + n

        def fill_sem(w, unit):
            return filled[FILLS.at[w.section, unit][0]]

        def sections(eng, steps, at_end=lambda w: None):
            for unit in ORDER["first"]:
                if unit[0] in steps:
                    steps[unit[0]](Where("first", 0, 0, None), unit[1])
            at_end(Where("first", 0, 0, None))
            with eng.Fori(0, NG - 1) as i:
                w = Where("loop", i, i + 1, i)
                for unit in ORDER["loop"]:
                    if unit[0] in steps:
                        steps[unit[0]](w, unit[1])
                at_end(w)
            for unit in ORDER["last"]:
                if unit[0] in steps:
                    steps[unit[0]](Where("last", 0, None, NG - 1), unit[1])

        def col96(name, c):
            return v96[:, V96[name] + c:V96[name] + c + 1]

        def col128(name, c=0):
            return v128[:, V128[name] + c:V128[name] + c + 1]

        block = ctx.enter_context(nc.Block())

        @block.sync
        def _(sp):
            def load_x(g):
                sp.dma_start(x_in[:, :, :], xT[g]).then_inc(S["x_in"], 16)

            sp.dma_start(w_patch[:, :, :], patchT).then_inc(loads["patch"], 16)
            load_x(0)
            for dst, src in ((v96, vec96), (v128, vec128), (w_pe, peT), (w_mask, mask), (w_prio, prio),
                             (w_patch_b, patch_b), (w_ff2_b, ffn2_b), (w_cproj_b, cproj_b)):
                sp.dma_start(dst[:], src).then_inc(loads["vec"], 16)
            sp.dma_start(w_ident[:, :], ident).then_inc(loads["ident"], 16)
            for name, dst, src in (("tff1", w_tff1, tok_ff1), ("tff2", w_tff2, tok_ff2), ("tqkv", w_tqkv, tok_qkv),
                                   ("tproj", w_tproj, tok_proj), ("in", w_in, in_proj), ("out", w_out, out_proj),
                                   ("qkv", w_qkv, qkv), ("proj", w_proj, attn_proj), ("ff1", w_ff1, ffn1),
                                   ("ff2", w_ff2, ffn2)):
                sp.dma_start(dst[:], src).then_inc(loads[name], 16)
            sp.dma_start(hT[:, :, :, NI:N], txtT[0]).then_inc(S["txt_in"], 16)
            sp.dma_start(w_cproj[:, :, :], cproj).then_inc(loads["cproj"], 16)
            sp.dma_start(w_cgate[:, :, :], cgate).then_inc(loads["cproj"], 16)
            sp.dma_start(w_cqkv[:, :, :], cqkv).then_inc(loads["cqkv"], 16)

            def b_ht(w, _):
                if w.section == "loop":
                    sp.wait_ge(S["a_emb"], upto("a_emb", w.b))
                    load_x(w.a)
                    sp.wait_ge(fill_sem(w, ("b_ht", 0)), fill_count(w, ("b_ht", 0)))
                    sp.dma_start(hT[:, :, :, NI:N], txtT[w.a]).then_inc(S["txt_in"], 16)

            def c_pr(w, _):
                sp.wait_ge(S["out_tm"], upto("out_tm", w.b))
                sp.dma_start(out[w.b], u[:, :, :]).then_inc(S["out_dma"], 16)
                sp.wait_ge(S["out_dma"], upto("out_dma", w.b))
                sp.sem_inc(S["out_room"], 1)

            sp.sem_inc(S["out_room"], 1)
            sections(sp, {"b_ht": b_ht, "c_pr": c_pr})
            sp.wait_ge(S["out_dma"], 16 * NG)

        @block.tensor
        def _(pe):
            def chunks(out_ap, lhs, rhs, last, bias_row=True):
                k = HC + 1 if bias_row else HC
                pe.matmul(out_ap, lhs(0, k), rhs(0, k), start=True, stop=False)
                m = pe.matmul(out_ap, lhs(1, HC), rhs(1, HC), start=False, stop=True)
                if last is not None:
                    m.then_inc(last, 1)

            def all_read(w):
                for unit in FILLS.last[w.section]:
                    for sem_read, value in reads(w, unit):
                        pe.wait_ge(sem_read, value)

            def a_em(w, _):
                for sem_read, value in reads_before(w, ("a_em", 0)):
                    pe.wait_ge(sem_read, value)
                t = slot(w, ("a_em", 0))
                if w.section == "first":
                    pe.wait_ge(loads["patch"], 16 * n_loads["patch"])
                pe.wait_ge(S["x_in"], upto("x_in", w.a))
                for tile in range(TILES_A):
                    for j in range(KP):
                        m = pe.matmul(t[:, tile, 0:D], x_in[:, j, tile * 128:(tile + 1) * 128], w_patch[:, j, :],
                                      start=(j == 0), stop=(j == KP - 1))
                m.then_inc(fill_sem(w, ("a_em", 0)), 1)

            def a_x0(w, _):
                for sem_read, value in reads_before(w, ("a_x0", 0)):
                    pe.wait_ge(sem_read, value)
                t = slot(w, ("a_x0", 0)).rearrange("p (c t) -> p c t", c=2)
                if w.section == "first":
                    pe.wait_ge(loads["ident"], 16 * n_loads["ident"])
                pe.wait_ge(S["a_xn"], upto("a_xn", w.a))
                for tile in range(TILES_A):
                    for c in range(2):
                        m = pe.transpose(t[0:HC, c, tile * 128:(tile + 1) * 128],
                                         a_emb[:, tile, c * HC:(c + 1) * HC], w_ident[:, :])
                m.then_inc(fill_sem(w, ("a_x0", 0)), 1)

            def a_f1(w, j):
                for sem_read, value in reads_before(w, ("a_f1", j)):
                    pe.wait_ge(sem_read, value)
                t = slot(w, ("a_f1", j))
                if w.section == "first" and j == 0:
                    pe.wait_ge(loads["tff1"], 16 * n_loads["tff1"])
                    pe.wait_ge(s_set, 1)
                src = x0T if j == 0 else x2T
                pe.wait_ge(S["x0T" if j == 0 else "x2T"], upto("x0T" if j == 0 else "x2T", w.a))
                for c in range(F // 128):
                    o = t[:, c // 2, (c % 2) * TA:(c % 2 + 1) * TA]
                    chunks(o, lambda kc, k: w_tff1[0:k, kc, c * 128:(c + 1) * 128], lambda kc, k: src[0:k, kc, :],
                           fill_sem(w, ("a_f1", j)) if c == F // 128 - 1 else None)

            def a_f2(w, j):
                for sem_read, value in reads_before(w, ("a_f2", j)):
                    pe.wait_ge(sem_read, value)
                t = slot(w, ("a_f2", j)).rearrange("p (c t) -> p c t", c=2)
                if w.section == "first" and j == 0:
                    pe.wait_ge(loads["tff2"], 16 * n_loads["tff2"])
                for c in range(2):
                    for kc in range(F // 128):
                        if c == 0 and kc % 2 == 0:
                            pe.wait_ge(S["a_h"], upto("a_h", w.a, 3 * j + kc // 2 + 1))
                        m = pe.matmul(t[0:HC, c, :], w_tff2[:, kc, c * HC:(c + 1) * HC], a_h[:, kc, :],
                                      start=(kc == 0), stop=(kc == F // 128 - 1))
                m.then_inc(fill_sem(w, ("a_f2", j)), 1)

            def a_qk(w, _):
                for sem_read, value in reads_before(w, ("a_qk", 0)):
                    pe.wait_ge(sem_read, value)
                t = slot(w, ("a_qk", 0))
                if w.section == "first":
                    pe.wait_ge(loads["tqkv"], 16 * n_loads["tqkv"])
                pe.wait_ge(S["x1T"], upto("x1T", w.a))
                for n in range(4):
                    o = t[0:HC, n // 2, (n % 2) * TA:(n % 2 + 1) * TA]
                    chunks(o, lambda kc, k: w_tqkv[0:k, kc, n * HC:(n + 1) * HC], lambda kc, k: x1T[0:k, kc, :],
                           fill_sem(w, ("a_qk", 0)) if n == 3 else None)

            def a_v(w, _):
                for sem_read, value in reads_before(w, ("a_v", 0)):
                    pe.wait_ge(sem_read, value)
                t = slot(w, ("a_v", 0))
                wv = w_tqkv[:, :, 2 * D:3 * D].rearrange("p c (n two d) -> p c two n d", two=2, d=HD)
                for s in range(GS):
                    for odd in range(2):
                        chunks(t[64 * odd:64 * odd + NI, s * HC:(s + 1) * HC],
                               lambda kc, k: x1T[0:k, kc, s * NI:(s + 1) * NI], lambda kc, k: wv[0:k, kc, odd],
                               fill_sem(w, ("a_v", 0)) if s == GS - 1 and odd else None)

            def a_s(w, t2):
                for sem_read, value in reads_before(w, ("a_s", t2)):
                    pe.wait_ge(sem_read, value)
                t = slot(w, ("a_s", t2))
                pe.wait_ge(S["a_qT"], upto("a_qT", w.a))
                pe.wait_ge(S["a_kB"], upto("a_kB", w.a, 2 * t2 + 2))
                for half in range(2):
                    s = 2 * t2 + half
                    for c in range(2):
                        m = pe.matmul(t[64 * half:64 * half + NI, c, 0:6 * NI], a_qT[:, c, s * NI:(s + 1) * NI],
                                      a_kB[:, c, :, half * NI:(half + 1) * NI], start=True, stop=True)
                m.then_inc(fill_sem(w, ("a_s", t2)), 1)

            def a_pt(w, t2):
                for sem_read, value in reads_before(w, ("a_pt", t2)):
                    pe.wait_ge(sem_read, value)
                t = slot(w, ("a_pt", t2))
                pe.wait_ge(S["a_exp"], upto("a_exp", w.a, t2 + 1))
                for n in range(NH // 2):
                    m = pe.transpose(t[:, n // 3, (n % 3) * 128:(n % 3 + 1) * 128],
                                     a_p[:, t2, n * 128:(n + 1) * 128], w_ident[:, :])
                m.then_inc(fill_sem(w, ("a_pt", t2)), 1)

            def a_o(w, t2):
                for sem_read, value in reads_before(w, ("a_o", t2)):
                    pe.wait_ge(sem_read, value)
                t = slot(w, ("a_o", t2))
                pe.wait_ge(S["a_pT"], upto("a_pT", w.a, t2 + 1))
                pe.wait_ge(S["a_vB"], upto("a_vB", w.a))
                for half in range(2):
                    for n in range(NH // 2):
                        k = 2 * (HD + 1)
                        m = pe.matmul(t[64 * half:64 * half + NI, n * k:(n + 1) * k],
                                      a_pT[:, n, half * NI:(half + 1) * NI], a_vB[:, 2 * t2 + half, n, :],
                                      start=True, stop=True)
                m.then_inc(fill_sem(w, ("a_o", t2)), 1)

            def a_ot(w, t2):
                for sem_read, value in reads_before(w, ("a_ot", t2)):
                    pe.wait_ge(sem_read, value)
                t = slot(w, ("a_ot", t2))
                pe.wait_ge(S["a_on"], upto("a_on", w.a, t2 + 1))
                for c in range(2):
                    m = pe.transpose(t[0:HC, c * 128:(c + 1) * 128], a_on[:, c * HC:(c + 1) * HC], w_ident[:, :])
                m.then_inc(fill_sem(w, ("a_ot", t2)), 1)

            def a_pr(w, _):
                for sem_read, value in reads_before(w, ("a_pr", 0)):
                    pe.wait_ge(sem_read, value)
                t = slot(w, ("a_pr", 0)).rearrange("p (c t) -> p c t", c=2)
                if w.section == "first":
                    pe.wait_ge(loads["tproj"], 16 * n_loads["tproj"])
                pe.wait_ge(S["a_oT"], upto("a_oT", w.a))
                for c in range(2):
                    chunks(t[0:HC, c, :], lambda kc, k: w_tproj[0:k, kc, c * HC:(c + 1) * HC],
                           lambda kc, k: a_oT[0:k, kc, :], fill_sem(w, ("a_pr", 0)) if c else None)

            def b_ht(w, _):
                for sem_read, value in reads_before(w, ("b_ht", 0)):
                    pe.wait_ge(sem_read, value)
                t = slot(w, ("b_ht", 0))
                pe.wait_ge(S["hT"], upto("hT", w.b))
                pe.wait_ge(S["txt_in"], upto("txt_in", w.b))
                hv = hT[:, :, :, :].rearrange("p c s t -> p c (s t)")
                for tile in range(TILES_B):
                    for c in range(2):
                        m = pe.transpose(t[:, tile, c * HC:(c + 1) * HC], hv[:, c, tile * 128:(tile + 1) * 128],
                                         w_ident[0:HC, 0:HC])
                m.then_inc(fill_sem(w, ("b_ht", 0)), 1)

            def b_u(w, n):
                for sem_read, value in reads_before(w, ("b_u", n)):
                    pe.wait_ge(sem_read, value)
                t = slot(w, ("b_u", n))
                for tile in range(TILES_B):
                    pe.wait_ge(S["ln_u"], upto("ln_u", w.b, 3 * n + tile + 1))
                    for c in range(2):
                        m = pe.transpose(t[0:HC, c, tile * 128:(tile + 1) * 128], u[:, tile, c * HC:(c + 1) * HC],
                                         w_ident[:, :])
                m.then_inc(fill_sem(w, ("b_u", n)), 1)

            def b_in(w, j):
                for sem_read, value in reads_before(w, ("b_in", j)):
                    pe.wait_ge(sem_read, value)
                t = slot(w, ("b_in", j))
                if j == 0:
                    pe.wait_ge(loads["in"], 16 * n_loads["in"])
                pe.wait_ge(S["lnT"], upto("lnT", w.b, 2))
                for c in range(3):
                    f0 = j * DI + c * 128
                    chunks(t[:, c, 0:TB], lambda kc, k: w_in[0:k, kc, f0:f0 + 128], lambda kc, k: bT[0:k, kc, :],
                           fill_sem(w, ("b_in", j)) if c == 2 else None, bias_row=False)

            def tm_product(w, unit, lhs, rhs, n_k):
                t = slot(w, unit)
                for tile in range(TILES_B):
                    for kc in range(n_k):
                        m = pe.matmul(t[:, tile, 0:D], lhs[:, kc, tile * 128:(tile + 1) * 128], rhs[:, kc, :],
                                      start=(kc == 0), stop=(kc == n_k - 1))
                m.then_inc(fill_sem(w, unit), 1)

            def b_out(w, _):
                for sem_read, value in reads_before(w, ("b_out", 0)):
                    pe.wait_ge(sem_read, value)
                pe.wait_ge(loads["out"], 16 * n_loads["out"])
                pe.wait_ge(S["gate"], upto("gate", w.b))
                tm_product(w, ("b_out", 0), cv.rearrange("p c s t -> p c (s t)"), w_out, DI // 128)

            def b_qk(w, name, f0):
                for sem_read, value in reads_before(w, (name, 0)):
                    pe.wait_ge(sem_read, value)
                t = slot(w, (name, 0))
                pe.wait_ge(loads["qkv"], 16 * n_loads["qkv"])
                pe.wait_ge(S["lnT"], upto("lnT", w.b, 4))
                for c in range(2):
                    chunks(t[0:HC, c, 0:TB], lambda kc, k: w_qkv[0:k, kc, f0 + c * HC:f0 + (c + 1) * HC],
                           lambda kc, k: bT[0:k, kc, :], fill_sem(w, (name, 0)) if c else None)

            def b_v(w, _):
                for sem_read, value in reads_before(w, ("b_v", 0)):
                    pe.wait_ge(sem_read, value)
                t = slot(w, ("b_v", 0))
                for s in range(GS):
                    chunks(t[0:N, s // 2, (s % 2) * D:(s % 2 + 1) * D], lambda kc, k: bT[0:k, kc, s * N:(s + 1) * N],
                           lambda kc, k: w_qkv[0:k, kc, 2 * D:3 * D], fill_sem(w, ("b_v", 0)) if s == GS - 1 else None)

            def b_s(w, s):
                for sem_read, value in reads_before(w, ("b_s", s)):
                    pe.wait_ge(sem_read, value)
                t = slot(w, ("b_s", s))
                pe.wait_ge(S["b_qT"], upto("b_qT", w.b))
                pe.wait_ge(S["b_kB"], upto("b_kB", w.b, 2 * s + 2))
                for c, h0, h1, bank, col in ((0, 0, 4, 0, 0), (0, 4, 6, 1, 0), (1, 0, 2, 1, 2), (1, 2, 6, 2, 0)):
                    m = pe.matmul(t[0:N, bank, col * N:(col + h1 - h0) * N], b_qT[:, c, s * N:(s + 1) * N],
                                  b_kBv[:, s % 2, c, h0:h1, :], start=True, stop=True)
                m.then_inc(fill_sem(w, ("b_s", s)), 1)

            def turn_p(w, unit, s):
                t = slot(w, unit)
                for h in range(NH):
                    m = pe.transpose(t[0:N, h // 4, (h % 4) * N:(h % 4 + 1) * N], pr[:, s % 2, h * N:(h + 1) * N],
                                     w_ident[0:N, 0:N])
                m.then_inc(fill_sem(w, unit), 1)

            def b_pt(w, s):
                for sem_read, value in reads_before(w, ("b_pt", s)):
                    pe.wait_ge(sem_read, value)
                pe.wait_ge(S["b_exp"], upto("b_exp", w.b, s + 1))
                turn_p(w, ("b_pt", s), s)

            def b_o(w, s):
                for sem_read, value in reads_before(w, ("b_o", s)):
                    pe.wait_ge(sem_read, value)
                t = slot(w, ("b_o", s))
                pe.wait_ge(S["b_pT"], upto("b_pT", w.b, s + 1))
                pe.wait_ge(S["b_vO"], upto("b_vO", w.b))
                for h in range(NH):
                    m = pe.matmul(t[0:N, h * (HD + 1):(h + 1) * (HD + 1)], pT[:, h, :], b_vO[:, s, h, :],
                                  start=True, stop=True)
                m.then_inc(fill_sem(w, ("b_o", s)), 1)

            def b_ot(w, s):
                for sem_read, value in reads_before(w, ("b_ot", s)):
                    pe.wait_ge(sem_read, value)
                t = slot(w, ("b_ot", s))
                pe.wait_ge(S["b_on"], upto("b_on", w.b, s + 1))
                for c in range(2):
                    m = pe.transpose(t[0:HC, c * N:(c + 1) * N], on[:, c * HC:(c + 1) * HC], w_ident[0:N, 0:N])
                m.then_inc(fill_sem(w, ("b_ot", s)), 1)

            def b_pr(w, _):
                for sem_read, value in reads_before(w, ("b_pr", 0)):
                    pe.wait_ge(sem_read, value)
                t = slot(w, ("b_pr", 0))
                pe.wait_ge(loads["proj"], 16 * n_loads["proj"])
                pe.wait_ge(S["b_oT"], upto("b_oT", w.b))
                for tile in range(TILES_B):
                    chunks(t[:, tile, 0:D], lambda kc, k: bT[0:k, kc, tile * 128:(tile + 1) * 128],
                           lambda kc, k: w_proj[0:k, kc, :], fill_sem(w, ("b_pr", 0)) if tile == TILES_B - 1 else None)

            def b_f1(w, j):
                for sem_read, value in reads_before(w, ("b_f1", j)):
                    pe.wait_ge(sem_read, value)
                t = slot(w, ("b_f1", j))
                pe.wait_ge(loads["ff1"], 16 * n_loads["ff1"])
                pe.wait_ge(S["lnT"], upto("lnT", w.b, 6))
                for c in range(3):
                    f0 = (3 * j + c) * 128
                    chunks(t[:, c, 0:TB], lambda kc, k: w_ff1[0:k, kc, f0:f0 + 128], lambda kc, k: bT[0:k, kc, :],
                           fill_sem(w, ("b_f1", j)) if c == 2 else None)

            def b_f2(w, _):
                for sem_read, value in reads_before(w, ("b_f2", 0)):
                    pe.wait_ge(sem_read, value)
                pe.wait_ge(loads["ff2"], 16 * n_loads["ff2"])
                pe.wait_ge(S["b_h"], upto("b_h", w.b))
                tm_product(w, ("b_f2", 0), b_h, w_ff2, F // 128)

            def c_g(w, _):
                for sem_read, value in reads_before(w, ("c_g", 0)):
                    pe.wait_ge(sem_read, value)
                t = slot(w, ("c_g", 0))
                pe.wait_ge(loads["cproj"], 16 * n_loads["cproj"])
                pe.wait_ge(S["lnT"], upto("lnT", w.b, 8))
                k14 = EXPERTS + 4
                for s in range(GS):
                    chunks(t[0:N, s * k14:(s + 1) * k14], lambda kc, k: bT[0:k, kc, s * N:(s + 1) * N],
                           lambda kc, k: w_cgate[0:k, kc, :], fill_sem(w, ("c_g", 0)) if s == GS - 1 else None,
                           bias_row=False)

            def c_qk(w, tile):
                for sem_read, value in reads_before(w, ("c_qk", tile)):
                    pe.wait_ge(sem_read, value)
                t = slot(w, ("c_qk", tile))
                pe.wait_ge(s_centred, 2)
                for n in range(3):
                    chunks(t[:, n, :], lambda kc, k: bT[0:k, kc, tile * 128:(tile + 1) * 128],
                           lambda kc, k: w_cqkv[0:k, kc, n * 512:(n + 1) * 512],
                           fill_sem(w, ("c_qk", tile)) if n == 2 else None)

            def c_qt(w, tile):
                for sem_read, value in reads_before(w, ("c_qt", tile)):
                    pe.wait_ge(sem_read, value)
                t = slot(w, ("c_qt", tile))
                pe.wait_ge(S["qkn"], upto("qkn", w.b, tile + 1))
                for n in range(NH):
                    m = pe.transpose(t[:, n // 4, (n % 4) * 128:(n % 4 + 1) * 128], qkn[:, n * 128:(n + 1) * 128],
                                     w_ident[:, :])
                m.then_inc(fill_sem(w, ("c_qt", tile)), 1)

            def c_v_(w, s):
                for sem_read, value in reads_before(w, ("c_v", s)):
                    pe.wait_ge(sem_read, value)
                t = slot(w, ("c_v", s))
                half = NH * HD2 // 2
                for n in range(2):
                    f0 = 2 * NH * HD2 + n * half
                    chunks(t[0:N, n, 0:half], lambda kc, k: bT[0:k, kc, s * N:(s + 1) * N],
                           lambda kc, k: w_cqkv[0:k, kc, f0:f0 + half], fill_sem(w, ("c_v", s)) if n else None)

            def c_s(w, s):
                for sem_read, value in reads_before(w, ("c_s", s)):
                    pe.wait_ge(sem_read, value)
                t = slot(w, ("c_s", s))
                pe.wait_ge(S["c_qkT"], upto("c_qkT", w.b))
                for n in range(NH // 2):
                    m = pe.matmul(t[0:N, n // 2, (n % 2) * 2 * N:(n % 2 + 1) * 2 * N], c_qT[:, n, s * N:(s + 1) * N],
                                  c_kB[:, n, :, s * N:(s + 1) * N], start=True, stop=True)
                m.then_inc(fill_sem(w, ("c_s", s)), 1)

            def c_pt(w, s):
                for sem_read, value in reads_before(w, ("c_pt", s)):
                    pe.wait_ge(sem_read, value)
                pe.wait_ge(S["c_exp"], upto("c_exp", w.b, s + 1))
                turn_p(w, ("c_pt", s), s)

            def c_o(w, s):
                for sem_read, value in reads_before(w, ("c_o", s)):
                    pe.wait_ge(sem_read, value)
                t = slot(w, ("c_o", s))
                pe.wait_ge(S["c_pT"], upto("c_pT", w.b, s + 1))
                pe.wait_ge(S["c_v"], upto("c_v", w.b, s + 1))
                pe.wait_ge(S["c_ones"], upto("c_ones", w.b))
                k = HD2 + 1
                for h in range(NH):
                    m = pe.matmul(t[0:N, h // 6, (h % 6) * k:(h % 6 + 1) * k], pT[:, h, :], c_v[:, s % 2, h, :],
                                  start=True, stop=True)
                m.then_inc(fill_sem(w, ("c_o", s)), 1)

            def c_ot(w, s):
                for sem_read, value in reads_before(w, ("c_ot", s)):
                    pe.wait_ge(sem_read, value)
                t = slot(w, ("c_ot", s))
                pe.wait_ge(S["c_on"], upto("c_on", w.b, s + 1))
                for n in range(NH // 2):
                    m = pe.transpose(t[:, n // 3, (n % 3) * N:(n % 3 + 1) * N], on[:, n * 128:(n + 1) * 128],
                                     w_ident[0:N, 0:N])
                m.then_inc(fill_sem(w, ("c_ot", s)), 1)

            def c_pr(w, _):
                for sem_read, value in reads_before(w, ("c_pr", 0)):
                    pe.wait_ge(sem_read, value)
                pe.wait_ge(S["c_oT"], upto("c_oT", w.b))
                tm_product(w, ("c_pr", 0), c_oT, w_cproj, NH * HD2 // 128)

            sections(pe, {"a_em": a_em, "a_x0": a_x0, "a_f1": a_f1, "a_f2": a_f2, "a_qk": a_qk, "a_v": a_v, "a_s": a_s,
                          "a_pt": a_pt, "a_o": a_o, "a_ot": a_ot, "a_pr": a_pr, "b_ht": b_ht, "b_u": b_u,
                          "b_in": b_in, "b_out": b_out, "b_q": lambda w, n: b_qk(w, "b_q", 0),
                          "b_k": lambda w, n: b_qk(w, "b_k", D), "b_v": b_v, "b_s": b_s, "b_pt": b_pt, "b_o": b_o,
                          "b_ot": b_ot, "b_pr": b_pr, "b_f1": b_f1, "b_f2": b_f2, "c_g": c_g, "c_qk": c_qk,
                          "c_qt": c_qt, "c_v": c_v_, "c_s": c_s, "c_pt": c_pt, "c_o": c_o, "c_ot": c_ot,
                          "c_pr": c_pr}, at_end=all_read)

        @block.scalar
        def _(act):
            act.wait_ge(s_set, 1)
            act.wait_ge(loads["vec"], 16 * n_loads["vec"])

            def rsqrt(log_out, out_ap, in_ap, log_sem, out_sem, log_name, group, k, scale=1.0):
                act.activation(log_out, in_ap, ACT.Ln, bias=eps[0:log_out.shape[0], :], scale=scale).then_inc(log_sem, 1)
                act.wait_ge(S[log_name], upto(log_name, group, k))
                act.activation(out_ap, log_out, ACT.Exp, scale=-0.5).then_inc(out_sem, 1)

            def a_em(w, _):
                act.wait_ge(S["a_mv"], upto("a_mv", w.a))
                rsqrt(a_lnv[:, :], a_rstd[:, :], a_mv[:, :, 1], S["a_lnv"], S["a_rstd"], "a_lnv", w.a, 1)

            def a_f1(w, j):
                act.wait_ge(fill_sem(w, ("a_f1", j)), fill_count(w, ("a_f1", j)))
                t = slot(w, ("a_f1", j))
                for n in range(3):
                    m = act.activation(a_h[:, 2 * n:2 * n + 2, :], t[:, n, :].rearrange("p (c t) -> p c t", c=2),
                                       ACT.Gelu_apprx_tanh).then_inc(S["a_h"], 1)

            def a_qk(w, _):
                act.wait_ge(fill_sem(w, ("a_qk", 0)), fill_count(w, ("a_qk", 0)))
                t = slot(w, ("a_qk", 0))
                act.activation(a_qT[:, :, :], t[0:HC, 0, :].rearrange("p (c t) -> p c t", c=2), ACT.Copy)\
                   .then_inc(S["a_qT"], 1)

            def a_v(w, _):
                act.wait_ge(fill_sem(w, ("a_v", 0)), fill_count(w, ("a_v", 0)))
                t = slot(w, ("a_v", 0))
                for odd in range(2):
                    r = slice(64 * odd, 64 * odd + 64)
                    src = t[r, 0:GS * HC].rearrange("p (s n d) -> p s n d", s=GS, d=HD)
                    m = act.activation(a_vB[r, :, :, odd * (HD + 1):odd * (HD + 1) + HD], src, ACT.Copy)
                m.then_inc(S["a_vB"], 1)

            def a_s(w, t2):
                act.wait_ge(S["a_sub"], upto("a_sub", w.a, t2 + 1))
                act.activation(a_p[:, t2, :], a_p[:, t2, :], ACT.Exp, scale=HD ** -0.5).then_inc(S["a_exp"], 1)

            def a_pt(w, t2):
                act.wait_ge(fill_sem(w, ("a_pt", t2)), fill_count(w, ("a_pt", t2)))
                t = slot(w, ("a_pt", t2))
                act.activation(a_pT[:, :, :].rearrange("p (b n) t -> p b (n t)", b=2), t[:, 0:2, 0:384], ACT.Copy)\
                   .then_inc(S["a_pT"], 1)

            def a_ot(w, t2):
                act.wait_ge(fill_sem(w, ("a_ot", t2)), fill_count(w, ("a_ot", t2)))
                t = slot(w, ("a_ot", t2))
                act.activation(a_oT[0:HC, :, t2 * 128:(t2 + 1) * 128],
                               t[0:HC, 0:256].rearrange("p (c t) -> p c t", c=2), ACT.Copy)\
                   .then_inc(S["a_oT"], 1)

            def b_ht(w, _):
                act.wait_ge(fill_sem(w, ("b_ht", 0)), fill_count(w, ("b_ht", 0)))
                t = slot(w, ("b_ht", 0))
                act.activation(h_tm[:, :, :], t[:, :, 0:D], ACT.Copy)\
                   .then_inc(S["h_tm"], 1)
                norm(w, 0)
                act.wait_ge(S["ln1_var"], upto("ln1_var", w.b))
                rsqrt(ln1[:, 2, :], ln1[:, 3, :], ln1[:, 1, :], S["ln1_log"], S["ln1_rstd"], "ln1_log", w.b, 1)

            def norm(w, n):
                act.wait_ge(S["ln_mv"], upto("ln_mv", w.b, 3 * n + 3))
                rsqrt(lnv[:, :], rstd[:, :], mv[:, :, 1], S["ln_log"], S["ln_rstd"], "ln_log", w.b, n + 1)

            def b_u(w, n):
                act.wait_ge(fill_sem(w, ("b_u", n)), fill_count(w, ("b_u", n)))
                t = slot(w, ("b_u", n))
                if n < 3:
                    act.activation(bT[0:HC, 0, :], t[0:HC, 0, 0:TB], ACT.Identity, scale=col96(f"ln{n + 1}_g", 0),
                                   bias=col96(f"ln{n + 1}_b", 0))\
                       .then_inc(S["lnT"], 1)
                else:
                    act.activation(bT[0:HC, 0, :], t[0:HC, 0, 0:TB], ACT.Copy)\
                       .then_inc(S["lnT"], 1)

            def b_in(w, j):
                act.wait_ge(fill_sem(w, ("b_in", j)), fill_count(w, ("b_in", j)))
                t = slot(w, ("b_in", j))
                if j == 0:
                    for c in range(3):
                        m = act.activation(xpad[:, c, :, KC - 1:], t[:, c, 0:TB].rearrange("p (s t) -> p s t", s=GS),
                                           ACT.Copy)
                    m.then_inc(S["xpad"], 1)
                    return
                act.activation(sz, t[:, :, 0:TB], ACT.Silu).then_inc(S["sz"], 1)
                for c in range(3):
                    act.wait_ge(S["conv"], upto("conv", w.b, 10 + c))
                    act.activation(cv[:, c], cv[:, c], ACT.Silu).then_inc(S["conv_act"], 1)

            def b_out(w, _):
                norm(w, 1)

            def b_q(w, _):
                act.wait_ge(fill_sem(w, ("b_q", 0)), fill_count(w, ("b_q", 0)))
                t = slot(w, ("b_q", 0))
                act.activation(b_qT, t[0:HC, 0:2, 0:TB], ACT.Copy)\
                   .then_inc(S["b_qT"], 1)

            def b_v(w, _):
                act.wait_ge(fill_sem(w, ("b_v", 0)), fill_count(w, ("b_v", 0)))
                t = slot(w, ("b_v", 0))
                for n in range(2):
                    m = act.activation(b_vO[:, 2 * n:2 * n + 2, :, 0:HD],
                                       t[0:N, n, 0:2 * D].rearrange("p (s h d) -> p s h d", s=2, d=HD), ACT.Copy)
                m.then_inc(S["b_vO"], 1)

            def numerators(w, stage, s, head):
                act.wait_ge(S[stage + "_sub"], upto(stage + "_sub", w.b, s + 1))
                act.activation(pr[:, s % 2, :], pr[:, s % 2, :], ACT.Exp, scale=head ** -0.5)\
                   .then_inc(S[stage + "_exp"], 1)

            def turned(w, stage, s):
                act.wait_ge(fill_sem(w, (stage + "_pt", s)), fill_count(w, (stage + "_pt", s)))
                t = slot(w, (stage + "_pt", s))
                act.activation(pT[:, :, :].rearrange("p (b h) t -> p b (h t)", b=3), t[0:N, :, 0:4 * N], ACT.Copy)\
                   .then_inc(S[stage + "_pT"], 1)

            def b_ot(w, s):
                act.wait_ge(fill_sem(w, ("b_ot", s)), fill_count(w, ("b_ot", s)))
                t = slot(w, ("b_ot", s))
                act.activation(bT[0:HC, :, s * N:(s + 1) * N], t[0:HC, 0:2 * N].rearrange("p (c t) -> p c t", c=2),
                               ACT.Copy).then_inc(S["b_oT"], 1)

            def b_pr(w, _):
                norm(w, 2)

            def b_f1(w, j):
                act.wait_ge(fill_sem(w, ("b_f1", j)), fill_count(w, ("b_f1", j)))
                t = slot(w, ("b_f1", j))
                act.activation(b_h[:, 3 * j:3 * j + 3, :], t[:, :, 0:TB], ACT.Gelu)\
                   .then_inc(S["b_h"], 1)

            def b_f2(w, _):
                norm(w, 3)

            def c_g(w, _):
                act.wait_ge(S["g_step"], upto("g_step", w.b, 4))
                act.activation(gsm[:, 1], gsm[:, 1], ACT.Exp).then_inc(S["g_exp"], 1)

            def c_qk(w, tile):
                act.wait_ge(fill_sem(w, ("c_qk", tile)), fill_count(w, ("c_qk", tile)))
                t = slot(w, ("c_qk", tile))
                act.activation(sq.rearrange("p (b n) -> p b n", b=3), t[:, :, :], ACT.Square).then_inc(S["sq"], 1)
                act.wait_ge(S["ss"], upto("ss", w.b, tile + 1))
                rsqrt(ss[:, 1, :], ss[:, 2, :], ss[:, 0, :], S["qk_log"], S["qk_rstd"], "qk_log", w.b, tile + 1,
                      scale=1.0 / HD2)

            def c_qt(w, tile):
                act.wait_ge(fill_sem(w, ("c_qt", tile)), fill_count(w, ("c_qt", tile)))
                t = slot(w, ("c_qt", tile))
                tv = t[:, :, :].rearrange("p b (n t) -> p (b n) t", t=128)
                cols = slice(tile * 128, (tile + 1) * 128)
                act.activation(c_qT[:, :, cols], tv[:, 0:6, :], ACT.Identity, scale=col128("q_w"), bias=col128("q_b"))
                for par in range(2):
                    r = slice(64 * par, 64 * par + 64)
                    m = act.activation(c_kB[r, :, par, cols], tv[r, 6:12, :], ACT.Identity, scale=col128("k_w")[r, :],
                                       bias=col128("k_b")[r, :])
                m.then_inc(S["c_qkT"], 1)

            def c_v_(w, s):
                act.wait_ge(fill_sem(w, ("c_v", s)), fill_count(w, ("c_v", s)))
                t = slot(w, ("c_v", s))
                if s == 0:
                    act.wait_ge(S["c_ones"], upto("c_ones", w.b))
                if s >= 2:
                    act.wait_ge(S["c_rec"], upto("c_rec", w.b, s - 1))
                half = NH * HD2 // 2
                act.activation(c_v[:, s % 2, :, 0:HD2].rearrange("p (b h) d -> p b h d", b=2),
                               t[0:N, :, 0:half].rearrange("p b (h d) -> p b h d", d=HD2), ACT.Copy)\
                   .then_inc(S["c_v"], 1)

            def c_ot(w, s):
                act.wait_ge(fill_sem(w, ("c_ot", s)), fill_count(w, ("c_ot", s)))
                t = slot(w, ("c_ot", s))
                act.activation(c_oT[:, :, s * N:(s + 1) * N].rearrange("p (b n) t -> p b n t", b=2),
                               t[:, :, 0:3 * N].rearrange("p b (n t) -> p b n t", t=N), ACT.Copy)\
                   .then_inc(S["c_oT"], 1)

            sections(act, {"a_em": a_em, "a_f1": a_f1, "a_qk": a_qk, "a_v": a_v, "a_s": a_s, "a_pt": a_pt,
                           "a_ot": a_ot, "b_ht": b_ht, "b_u": b_u, "b_in": b_in, "b_out": b_out, "b_q": b_q,
                           "b_v": b_v, "b_s": lambda w, s: numerators(w, "b", s, HD),
                           "b_pt": lambda w, s: turned(w, "b", s), "b_ot": b_ot, "b_pr": b_pr, "b_f1": b_f1,
                           "b_f2": b_f2, "c_g": c_g, "c_qk": c_qk, "c_qt": c_qt, "c_v": c_v_,
                           "c_s": lambda w, s: numerators(w, "c", s, HD2), "c_pt": lambda w, s: turned(w, "c", s),
                           "c_ot": c_ot})

        @block.vector
        def _(dve):
            dve.memset(eps[:, :], EPS)
            for t in (x0T, x1T, x2T, a_oT, bT):
                dve.memset(t[HC:HC + 1, 0, :], 1.0)
            dve.memset(a_vB[:, :, :, :], 0.0)
            dve.memset(b_vO[:, :, :, HD:HD + 1], 1.0)
            dve.memset(c_kB[:, :, :, :], 0.0).then_inc(s_set, 1)
            dve.wait_ge(s_set, 1)
            for odd in range(2):
                c = odd * (HD + 1) + HD
                m = dve.memset(a_vB[64 * odd:64 * odd + 64, :, :, c:c + 1], 1.0)
            m.then_inc(s_set, 1)
            dve.wait_ge(loads["vec"], 16 * n_loads["vec"])
            for c in range(2):
                dve.tensor_scalar(w_pe[:, c, :], w_pe[:, c, :], col96("tok_b", c), None, ALU.add).then_inc(s_set, 1)
            dve.wait_ge(s_set, 4)

            def a_em(w, _):
                dve.wait_ge(fill_sem(w, ("a_em", 0)), fill_count(w, ("a_em", 0)))
                t = slot(w, ("a_em", 0))
                pb = w_patch_b[:, :].unsqueeze(1).to_broadcast([128, TILES_A, D])
                dve.tensor_tensor(a_emb[:, :, :], t[:, 0:TILES_A, 0:D], pb, ALU.add)\
                   .then_inc(S["a_emb"], 1)
                dve.wait_ge(S["a_emb"], upto("a_emb", w.a))
                for n in range(TILES_A):
                    dve.bn_stats(a_bn[:, n, :], a_emb[:, n, :]).then_inc(S["a_stats"], 1)
                dve.wait_ge(S["a_stats"], upto("a_stats", w.a))
                dve.tensor_copy(seen[:, 0:TILES_A], a_bn[:, :, 0])
                for n in range(TILES_A):
                    dve.bn_aggr(a_mv[:, n, :], a_bn[:, n, :]).then_inc(S["a_mv"], 1)
                dve.wait_ge(S["a_mv"], upto("a_mv", w.a))
                dve.wait_ge(S["a_rstd"], upto("a_rstd", w.a))
                for n in range(TILES_A):
                    dve.tensor_scalar(a_emb[:, n, :], a_emb[:, n, :], a_mv[:, n, 0:1], a_rstd[:, n:n + 1],
                                      ALU.subtract, ALU.mult).then_inc(S["a_xn"], 1)

            def a_x0(w, _):
                dve.wait_ge(fill_sem(w, ("a_x0", 0)), fill_count(w, ("a_x0", 0)))
                t = slot(w, ("a_x0", 0)).rearrange("p (c s t) -> p c s t", c=2, s=GS)
                for c in range(2):
                    pe_c = w_pe[:, c, :].unsqueeze(1).to_broadcast([HC, GS, NI])
                    m = dve.scalar_tensor_tensor(out=x0T[0:HC, c, :].rearrange("p (s t) -> p s t", s=GS),
                                                 in0=t[0:HC, c], scalar=col96("tok_g", c), in1=pe_c, op0=ALU.mult,
                                                 op1=ALU.add).then_inc(S["x0T"], 1)

            def a_f2(w, j):
                dve.wait_ge(fill_sem(w, ("a_f2", j)), fill_count(w, ("a_f2", j)))
                t = slot(w, ("a_f2", j)).rearrange("p (c t) -> p c t", c=2)
                for c in range(2):
                    if j == 0:
                        m = dve.tensor_scalar(x1T[0:HC, c, :], t[0:HC, c, :], col96("tok_ff2_b", c), None, ALU.add)\
                           .then_inc(S["x1T"], 1)
                    else:
                        m = dve.scalar_tensor_tensor(
                            out=hT[:, c, :, 0:NI], in0=t[0:HC, c, :].rearrange("p (s t) -> p s t", s=GS),
                            scalar=col96("tok_ff2_b", c), in1=x2T[0:HC, c, :].rearrange("p (s t) -> p s t", s=GS),
                            op0=ALU.add, op1=ALU.add).then_inc(S["hT"], 1)

            def a_qk(w, _):
                dve.wait_ge(fill_sem(w, ("a_qk", 0)), fill_count(w, ("a_qk", 0)))
                t = slot(w, ("a_qk", 0))
                dve.tensor_copy(a_kT[:, :, :], t[0:HC, 1, :].rearrange("p (c t) -> p c t", c=2))\
                   .then_inc(S["a_kT"], 1)

            def a_s(w, t2):
                dve.wait_ge(fill_sem(w, ("a_s", t2)), fill_count(w, ("a_s", t2)))
                t = slot(w, ("a_s", t2))[:, 0:2, 0:6 * NI].rearrange("p b (h k) -> p b h k", k=NI)
                dve.tensor_reduce(a_max[:, t2, :].rearrange("p (b h) -> p b h", b=2), t, AX.X, ALU.max)\
                   .then_inc(S["a_max"], 1)
                dve.wait_ge(S["a_max"], upto("a_max", w.a, t2 + 1))
                mb = a_max[:, t2, :].rearrange("p (b h) -> p b h", b=2).unsqueeze(3).to_broadcast([128, 2, 6, NI])
                dve.tensor_tensor(a_p[:, t2, :].rearrange("p (b h k) -> p b h k", b=2, k=NI), t, mb, ALU.subtract)\
                   .then_inc(S["a_sub"], 1)

            def a_o(w, t2):
                dve.wait_ge(fill_sem(w, ("a_o", t2)), fill_count(w, ("a_o", t2)))
                t = slot(w, ("a_o", t2))[:, 0:NH * (HD + 1)].rearrange("p (h d) -> p h d", h=NH)
                dve.reciprocal(a_rec[:, t2, :], t[:, :, HD]).then_inc(S["a_rec"], 1)
                dve.wait_ge(S["a_rec"], upto("a_rec", w.a, t2 + 1))
                dve.tensor_tensor(a_on[:, :].rearrange("p (h d) -> p h d", h=NH), t[:, :, 0:HD],
                                  a_rec[:, t2, :].unsqueeze(2).to_broadcast([128, NH, HD]), ALU.mult)\
                   .then_inc(S["a_on"], 1)

            def a_pr(w, _):
                dve.wait_ge(fill_sem(w, ("a_pr", 0)), fill_count(w, ("a_pr", 0)))
                t = slot(w, ("a_pr", 0)).rearrange("p (c t) -> p c t", c=2)
                dve.tensor_tensor(x2T[0:HC, :, :], t[0:HC, :, :], x0T[0:HC, :, :], ALU.add)\
                   .then_inc(S["x2T"], 1)

            def moments(w, n, src):
                for tile in range(TILES_B):
                    dve.bn_stats(bn[:, tile, :], src[:, tile, :]).then_inc(S["ln_stats"], 1)
                dve.wait_ge(S["ln_stats"], upto("ln_stats", w.b, 3 * n + TILES_B))
                dve.tensor_copy(seen[:, TILES_A:TILES_A + TILES_B], bn[:, :, 0])
                for tile in range(TILES_B):
                    dve.bn_aggr(mv[:, tile, :], bn[:, tile, :]).then_inc(S["ln_mv"], 1)
                dve.wait_ge(S["ln_mv"], upto("ln_mv", w.b, 3 * n + 3))

            def normalise(w, n, src, scale):
                for tile in range(TILES_B):
                    dve.tensor_scalar(u[:, tile, :], src[:, tile, :], mv[:, tile, 0:1], scale[:, tile:tile + 1],
                                      ALU.subtract, ALU.mult).then_inc(S["ln_u"], 1)

            def b_ht(w, _):
                dve.wait_ge(S["h_tm"], upto("h_tm", w.b))
                moments(w, 0, h_tm)
                dve.wait_ge(S["ln_rstd"], upto("ln_rstd", w.b, 1))
                dve.tensor_tensor(ln1[:, 0, :], rstd[:, :], rstd[:, :], ALU.mult).then_inc(S["ln1_sq"], 1)
                dve.wait_ge(S["ln1_sq"], upto("ln1_sq", w.b))
                dve.tensor_tensor(ln1[:, 1, :], ln1[:, 0, :], mv[:, :, 1], ALU.mult).then_inc(S["ln1_var"], 1)
                dve.wait_ge(S["ln1_rstd"], upto("ln1_rstd", w.b))
                dve.tensor_tensor(ln1[:, 4, :], ln1[:, 3, :], rstd[:, :], ALU.mult).then_inc(S["ln1_both"], 1)
                dve.wait_ge(S["ln1_both"], upto("ln1_both", w.b))
                dve.wait_ge(S["out_room"], upto("out_room", w.b))
                normalise(w, 0, h_tm, ln1[:, 4, :])
                for tile in range(TILES_B):
                    dve.tensor_scalar(xr[:, tile, :], h_tm[:, tile, :], mv[:, tile, 0:1], rstd[:, tile:tile + 1],
                                      ALU.subtract, ALU.mult).then_inc(S["y_tm"], 1)

            def b_u(w, n):
                dve.wait_ge(fill_sem(w, ("b_u", n)), fill_count(w, ("b_u", n)))
                t = slot(w, ("b_u", n))
                if n < 3:
                    dve.tensor_scalar(bT[0:HC, 1, :], t[0:HC, 1, 0:TB], col96(f"ln{n + 1}_g", 1),
                                      col96(f"ln{n + 1}_b", 1), ALU.mult, ALU.add)\
                       .then_inc(S["lnT"], 1)
                else:
                    dve.tensor_copy(bT[0:HC, 1, :], t[0:HC, 1, 0:TB])\
                       .then_inc(S["lnT"], 1)

            def b_in(w, j):
                if j == 0:
                    dve.wait_ge(fill_sem(w, ("b_in", 0)), fill_count(w, ("b_in", 0)))
                    dve.memset(xpad[:, :, :, 0:KC - 1], 0.0).then_inc(S["pad"], 1)
                    return
                dve.wait_ge(S["xpad"], upto("xpad", w.b))
                dve.wait_ge(S["pad"], upto("pad", w.b))
                for n in range(KC):
                    tap = KC - 1 - n
                    for c in range(3):
                        src = xpad[:, c, :, tap:tap + N]
                        if n == 0:
                            m = dve.tensor_scalar(cv[:, c], src, col128("conv_w", c * KC + tap), col128("conv_b", c),
                                                  ALU.mult, ALU.add)
                        else:
                            dve.wait_ge(S["conv"], upto("conv", w.b, 3 * (n - 1) + c + 1))
                            m = dve.scalar_tensor_tensor(out=cv[:, c], in0=src, scalar=col128("conv_w", c * KC + tap),
                                                         in1=cv[:, c], op0=ALU.mult, op1=ALU.add)
                        m.then_inc(S["conv"], 1)
                dve.wait_ge(S["sz"], upto("sz", w.b))
                for c in range(3):
                    dve.wait_ge(S["conv_act"], upto("conv_act", w.b, c + 1))
                    dve.tensor_tensor(cv[:, c], cv[:, c], sz[:, c, :].rearrange("p (s t) -> p s t", s=GS), ALU.mult)\
                       .then_inc(S["gate"], 1)

            def residual(w, unit, name, out_t, in_t):
                dve.wait_ge(fill_sem(w, unit), fill_count(w, unit))
                t = slot(w, unit)
                dve.tensor_tensor(out_t[:, :, :], t[:, :, 0:D], in_t[:, :, :], ALU.add)\
                   .then_inc(S[name], 1)
                dve.wait_ge(S[name], upto(name, w.b))

            def b_out(w, _):
                dve.wait_ge(S["y_tm"], upto("y_tm", w.b))
                residual(w, ("b_out", 0), "x1_tm", xr, xr)
                moments(w, 1, xr)
                dve.wait_ge(S["ln_rstd"], upto("ln_rstd", w.b, 2))
                normalise(w, 1, xr, rstd)

            def b_k(w, _):
                dve.wait_ge(fill_sem(w, ("b_k", 0)), fill_count(w, ("b_k", 0)))
                t = slot(w, ("b_k", 0))
                dve.tensor_copy(b_kT, t[0:HC, 0:2, 0:TB])\
                   .then_inc(S["b_kT"], 1)

            def less_max(w, stage, s):
                dve.wait_ge(fill_sem(w, (stage + "_s", s)), fill_count(w, (stage + "_s", s)))
                t = slot(w, (stage + "_s", s))[0:N, :, 0:4 * N].rearrange("p b (h k) -> p b h k", k=N)
                mx = smax[:, s % 2, :].rearrange("p (b h) -> p b h", b=3)
                dve.tensor_reduce(mx, t, AX.X, ALU.max).then_inc(S[stage + "_max"], 1)
                dve.wait_ge(S[stage + "_max"], upto(stage + "_max", w.b, s + 1))
                dve.tensor_tensor(pr[:, s % 2, :].rearrange("p (b h k) -> p b h k", b=3, k=N), t,
                                  mx.unsqueeze(3).to_broadcast([N, 3, 4, N]), ALU.subtract)\
                   .then_inc(S[stage + "_sub"], 1)

            def b_o(w, s):
                dve.wait_ge(fill_sem(w, ("b_o", s)), fill_count(w, ("b_o", s)))
                t = slot(w, ("b_o", s))[0:N, 0:NH * (HD + 1)].rearrange("p (h d) -> p h d", h=NH)
                dve.reciprocal(rec[:, s % 2, :], t[:, :, HD]).then_inc(S["b_rec"], 1)
                dve.wait_ge(S["b_rec"], upto("b_rec", w.b, s + 1))
                dve.tensor_tensor(on[:, 0:D].rearrange("p (h d) -> p h d", h=NH), t[:, :, 0:HD],
                                  rec[:, s % 2, :].unsqueeze(2).to_broadcast([N, NH, HD]), ALU.mult)\
                   .then_inc(S["b_on"], 1)

            def b_pr(w, _):
                residual(w, ("b_pr", 0), "x2_tm", xr, xr)
                moments(w, 2, xr)
                dve.wait_ge(S["ln_rstd"], upto("ln_rstd", w.b, 3))
                normalise(w, 2, xr, rstd)

            def b_f2(w, _):
                dve.wait_ge(S["hx"], upto("hx", w.b))
                residual(w, ("b_f2", 0), "h2_tm", hx, hx)
                moments(w, 3, hx)
                dve.wait_ge(S["ln_rstd"], upto("ln_rstd", w.b, 4))
                normalise(w, 3, hx, rstd)

            def c_g(w, _):
                dve.wait_ge(fill_sem(w, ("c_g", 0)), fill_count(w, ("c_g", 0)))
                t = slot(w, ("c_g", 0))[0:N, 0:GS * (EXPERTS + 4)].rearrange("p (s k) -> p s k", s=GS)
                step = [0]

                def ordered(ins):
                    ins.then_inc(S["g_step"], 1)
                    step[0] += 1
                    dve.wait_ge(S["g_step"], upto("g_step", w.b, step[0]))

                def rows(n, lo, hi):
                    return gsm[:, n, :, lo:hi]

                def spread(ap, k):
                    return ap.to_broadcast([N, GS, k])

                pairs = lambda n, at: gsm[:, n, :, at:at + 4].rearrange("p s (a b) -> p s a b", b=2)
                E_ = EXPERTS
                mx = rows(0, 0, 1)
                mx2 = gsm[:, 0, :, 1:3]
                ordered(dve.tensor_reduce(gsm[:, 0, :, 0], t[:, :, 0:E_], AX.X, ALU.max))
                ordered(dve.tensor_reduce(mx2, t[:, :, E_:E_ + 4].rearrange("p s (a b) -> p s a b", b=2), AX.X, ALU.max))
                ordered(dve.tensor_tensor(rows(1, 0, E_), t[:, :, 0:E_], spread(mx, E_), ALU.subtract))
                m = dve.tensor_tensor(pairs(1, E_), t[:, :, E_:E_ + 4].rearrange("p s (a b) -> p s a b", b=2),
                                      mx2.unsqueeze(3).to_broadcast([N, GS, 2, 2]), ALU.subtract)
                ordered(m)
                dve.wait_ge(S["g_exp"], upto("g_exp", w.b))
                e = rows(1, 0, E_)
                prio_b = w_prio[:, :].unsqueeze(1).to_broadcast([N, GS, E_])

                def first_of_largest(values, n):
                    top = gsm[:, n, :, 0:1]
                    ordered(dve.tensor_reduce(gsm[:, n, :, 0], values, AX.X, ALU.max))
                    ordered(dve.tensor_tensor(rows(n + 1, 0, E_), values, spread(top, E_), ALU.is_equal))
                    ordered(dve.tensor_tensor(rows(n + 1, 0, E_), rows(n + 1, 0, E_), prio_b, ALU.mult))
                    ordered(dve.tensor_reduce(gsm[:, n, :, 1], rows(n + 1, 0, E_), AX.X, ALU.max))
                    ordered(dve.tensor_tensor(rows(n + 2, 0, E_), rows(n + 1, 0, E_), spread(gsm[:, n, :, 1:2], E_),
                                              ALU.is_equal))

                first_of_largest(e, 2)
                ordered(dve.scalar_tensor_tensor(out=rows(5, 0, E_), in0=rows(4, 0, E_), scalar=-2.0, in1=e,
                                                 op0=ALU.mult, op1=ALU.add))
                first_of_largest(rows(5, 0, E_), 6)
                ordered(dve.tensor_tensor(rows(9, 0, E_), rows(4, 0, E_), rows(8, 0, E_), ALU.add))
                ordered(dve.tensor_tensor(rows(9, 0, E_), rows(9, 0, E_), e, ALU.mult))
                ordered(dve.tensor_reduce(gsm[:, 10, :, 0], rows(9, 0, E_), AX.X, ALU.add))
                ordered(dve.tensor_reduce(gsm[:, 10, :, 1:3], pairs(1, E_), AX.X, ALU.add))
                ordered(dve.reciprocal(gsm[:, 11, :, 0:3], gsm[:, 10, :, 0:3]))
                ordered(dve.tensor_tensor(gsm[:, 10, :, 4:6], rows(1, E_, E_ + 2), spread(gsm[:, 11, :, 1:2], 2),
                                          ALU.mult))
                ordered(dve.scalar_tensor_tensor(out=gsm[:, 10, :, 6], in0=gsm[:, 10, :, 4], scalar=4.0,
                                                 in1=gsm[:, 11, :, 2], op0=ALU.mult, op1=ALU.mult))
                ordered(dve.scalar_tensor_tensor(out=gsm[:, 10, :, 7], in0=gsm[:, 10, :, 5], scalar=4.0,
                                                 in1=gsm[:, 11, :, 0], op0=ALU.mult, op1=ALU.mult))
                dve.tensor_tensor(gates[:, :, 0:2], rows(1, E_ + 2, E_ + 4), spread(gsm[:, 10, :, 6:7], 2), ALU.mult)\
                   .then_inc(S["gates"], 1)
                dve.tensor_tensor(gates[:, :, 2:NH], rows(9, 0, E_), spread(gsm[:, 10, :, 7:8], E_), ALU.mult)\
                   .then_inc(S["gates"], 1)
                assert step[0] == PER_GROUP["g_step"], step[0]

            def c_qk(w, tile):
                dve.wait_ge(S["sq"], upto("sq", w.b, tile + 1))
                dve.tensor_reduce(ss[:, 0, :], sq.rearrange("p (h d) -> p h d", d=HD2), AX.X, ALU.add)\
                   .then_inc(S["ss"], 1)
                dve.wait_ge(S["qk_rstd"], upto("qk_rstd", w.b, tile + 1))
                t = slot(w, ("c_qk", tile))
                if tile > 0:
                    dve.wait_ge(fill_sem(w, ("c_qt", tile - 1)), fill_count(w, ("c_qt", tile - 1)))
                r = ss[:, 2, :].rearrange("p (b h) -> p b h", b=3).unsqueeze(3).to_broadcast([128, 3, 8, HD2])
                dve.tensor_tensor(qkn.rearrange("p (b h d) -> p b h d", b=3, d=HD2),
                                  t[:, :, :].rearrange("p b (h d) -> p b h d", d=HD2), r, ALU.mult)\
                   .then_inc(S["qkn"], 1)

            def c_o(w, s):
                dve.wait_ge(fill_sem(w, ("c_o", s)), fill_count(w, ("c_o", s)))
                t = slot(w, ("c_o", s))[0:N, :, 0:6 * (HD2 + 1)].rearrange("p b (h d) -> p b h d", h=6)
                split = lambda ap: ap.rearrange("p (b h) -> p b h", b=2)
                dve.reciprocal(split(rec[:, s % 2, :]), t[:, :, :, HD2]).then_inc(S["c_rec"], 1)
                dve.wait_ge(S["c_rec"], upto("c_rec", w.b, s + 1))
                dve.wait_ge(S["gates"], upto("gates", w.b))
                dve.tensor_tensor(gr[:, s % 2, :], rec[:, s % 2, :], gates[:, s, :], ALU.mult).then_inc(S["c_gr"], 1)
                dve.wait_ge(S["c_gr"], upto("c_gr", w.b, s + 1))
                dve.tensor_tensor(on[:, :].rearrange("p (b h d) -> p b h d", b=2, h=6), t[:, :, :, 0:HD2],
                                  split(gr[:, s % 2, :]).unsqueeze(3).to_broadcast([N, 2, 6, HD2]), ALU.mult)\
                   .then_inc(S["c_on"], 1)

            def c_pr(w, _):
                dve.wait_ge(fill_sem(w, ("c_pr", 0)), fill_count(w, ("c_pr", 0)))
                t = slot(w, ("c_pr", 0))
                dve.wait_ge(S["h2b"], upto("h2b", w.b))
                dve.tensor_tensor(u[:, :, :], t[:, :, 0:D], h_tm[:, :, :], ALU.add)\
                   .then_inc(S["out_tm"], 1)

            def centre_weights():
                dve.wait_ge(loads["cqkv"], 16 * n_loads["cqkv"])
                for kc, k in ((0, HC + 1), (1, HC)):
                    wv = w_cqkv[0:k, kc, 0:qkw].rearrange("p (h d) -> p h d", d=HD2)
                    dve.tensor_reduce(w_mean[0:k, kc, :], wv, AX.X, ALU.add).then_inc(s_mean, 1)
                    dve.wait_ge(s_mean, kc + 1)
                    dve.scalar_tensor_tensor(out=wv, in0=w_mean[0:k, kc, :].unsqueeze(2).to_broadcast([k, 2 * NH, HD2]),
                                             scalar=-1.0 / HD2, in1=wv, op0=ALU.mult, op1=ALU.add)\
                       .then_inc(s_centred, 1)

            sections(dve, {"a_em": a_em, "a_x0": a_x0, "a_f2": a_f2, "a_qk": a_qk, "a_s": a_s, "a_o": a_o,
                           "a_pr": a_pr, "b_ht": b_ht, "b_u": b_u, "b_in": b_in, "b_out": b_out, "b_k": b_k,
                           "b_s": lambda w, s: less_max(w, "b", s), "b_o": b_o, "b_pr": b_pr, "b_f2": b_f2,
                           "c_g": c_g, "c_qk": c_qk, "c_s": lambda w, s: less_max(w, "c", s), "c_o": c_o,
                           "c_pr": c_pr,
                           "a_f1": lambda w, j: centre_weights() if w.section == "first" and j == 1 else None})

        @block.gpsimd
        def _(pool):
            pool.wait_ge(loads["vec"], 16 * n_loads["vec"])

            def spread(out_ap, in_ap, k):
                return pool.tensor_tensor(out_ap, in_ap.unsqueeze(1).to_broadcast([HC, 6, k]),
                                          w_mask[:, :].unsqueeze(2).to_broadcast([HC, 6, k]), ALU.mult)

            def a_s(w, t2):
                if t2 == 1:
                    pool.wait_ge(fill_sem(w, ("a_s", 0)), fill_count(w, ("a_s", 0)))
                else:
                    pool.wait_ge(S["a_kT"], upto("a_kT", w.a))
                for c in range(2):
                    spread(a_kB[:, c], a_kT[:, c, t2 * 128:(t2 + 1) * 128], 128).then_inc(S["a_kB"], 1)

            def b_s(w, s):
                if s >= 2:
                    pool.wait_ge(fill_sem(w, ("b_s", s - 2)), fill_count(w, ("b_s", s - 2)))
                else:
                    pool.wait_ge(S["b_kT"], upto("b_kT", w.b))
                for c in range(2):
                    spread(b_kBv[:, s % 2, c], b_kT[:, c, s * N:(s + 1) * N], N).then_inc(S["b_kB"], 1)

            def b_pr(w, _):
                pool.wait_ge(S["x2_tm"], upto("x2_tm", w.b))
                bias = w_ff2_b[:, :].unsqueeze(1).to_broadcast([128, TILES_B, D])
                pool.tensor_tensor(hx[:, :, :], xr[:, :, :], h_tm[:, :, :], ALU.add).then_inc(S["hx"], 1)
                pool.wait_ge(S["hx"], upto("hx", w.b, 1))
                pool.tensor_tensor(hx[:, :, :], hx[:, :, :], bias, ALU.add).then_inc(S["hx"], 1)

            def b_f2(w, _):
                pool.wait_ge(S["h2_tm"], upto("h2_tm", w.b))
                bias = w_cproj_b[:, :].unsqueeze(1).to_broadcast([128, TILES_B, D])
                pool.tensor_tensor(h_tm[:, :, :], hx[:, :, :], bias, ALU.add).then_inc(S["h2b"], 1)
                pool.memset(c_v[:, :, :, HD2:HD2 + 1], 1.0).then_inc(S["c_ones"], 1)

            sections(pool, {"a_s": a_s, "b_s": b_s, "b_pr": b_pr, "b_f2": b_f2})



def positions():
    pos = np.arange(NI, dtype=np.float32)[:, None]
    i = np.arange(D // 2, dtype=np.float32)[None, :]
    ang = pos / np.power(np.float32(10000.0), np.float32(2.0) * i / np.float32(D))
    pe = np.zeros((NI, D), np.float32)
    pe[:, 0::2] = np.sin(ang)
    pe[:, 1::2] = np.cos(ang)
    return pe


def chunked(a, rows):
    return np.ascontiguousarray(a.reshape(-1, rows, a.shape[-1]).transpose(1, 0, 2))


def with_bias(a, b):
    row = np.stack([b, np.zeros_like(b)])[None]
    return np.ascontiguousarray(np.concatenate([chunked(a, HC), row], axis=0))


def kernel(**inputs):
    import concourse.bacc as _bacc
    from concourse.bass_utils import run_bass_kernel_spmd as _run

    v = {k: np.asarray(a) for k, a in inputs.items()}
    tok, att, ffn = (lambda n: v["L0_tok_" + n]), (lambda n: v["L0_attn_" + n]), (lambda n: v["L0_ffn_" + n])
    per96 = lambda b: b.reshape(2, HC).T
    rows = lambda b: np.ascontiguousarray(np.broadcast_to(b, (128, D)))
    pix = v["x"].reshape(NG, GS, CH, IMG // P, P, IMG // P, P).transpose(0, 2, 4, 6, 1, 3, 5)
    arrays = {
        "xT": pix.reshape(NG, KP, 128, TA).transpose(0, 2, 1, 3),
        "txtT": v["txt"].reshape(NG, GS, NT, 2, HC).transpose(0, 4, 3, 1, 2),
        "patchT": chunked(tok("patch_w").reshape(D, -1).T, 128),
        "ident": np.eye(128, dtype=np.float32),
        "peT": positions().T.reshape(2, HC, NI).transpose(1, 0, 2),
        "mask": (np.arange(HC)[:, None] // HD == np.arange(6)[None]).astype(np.float32),
        "prio": np.broadcast_to(np.arange(EXPERTS, 0, -1).astype(np.float32), (N, EXPERTS)),
        "vec96": np.concatenate([per96(tok("ln_g")), per96(tok("ff2_b"))] +
                                [per96(att(f"ln{n}_{k}")) for n in (1, 2, 3) for k in "gb"] +
                                [per96(tok("ln_b"))], axis=1),
        "vec128": np.concatenate([att("conv_w").reshape(3, 128, KC).transpose(1, 0, 2).reshape(128, 3 * KC),
                                  att("conv_b").reshape(3, 128).T] +
                                 [np.concatenate([ffn(n), ffn(n)])[:, None] for n in
                                  ("q_norm_w", "q_norm_b", "k_norm_w", "k_norm_b")], axis=1),
        "patch_b": rows(tok("patch_b")),
        "tok_ff1": with_bias(tok("ff1_w"), tok("ff1_b")),
        "tok_ff2": chunked(tok("ff2_w"), 128),
        "tok_qkv": with_bias(tok("qkv_w"), tok("qkv_b")),
        "tok_proj": with_bias(tok("proj_w"), tok("proj_b")),
        "in_proj": chunked(att("in_proj_w"), HC),
        "out_proj": chunked(att("out_proj_w"), 128),
        "qkv": with_bias(att("qkv_w"), att("qkv_b")),
        "attn_proj": with_bias(att("attn_proj_w"), att("attn_proj_b")),
        "ffn1": with_bias(att("ffn1_w"), att("ffn1_b")),
        "ffn2": chunked(att("ffn2_w"), 128),
        "ffn2_b": rows(att("ffn2_b")),
        "cqkv": with_bias(ffn("qkv_w"), ffn("qkv_b")),
        "cproj": chunked(ffn("proj_w"), 128),
        "cproj_b": rows(ffn("proj_b")),
        "cgate": chunked(np.concatenate([ffn("wg_w"), ffn("wg0_w"), ffn("wg1_w")], axis=1), HC),
    }
    arrays = {k: np.ascontiguousarray(a) for k, a in arrays.items()}
    nc = _bacc.Bacc("TRN2", target_bir_lowering=False, num_devices=1)
    args = {k: nc.dram_tensor(f"in_{k}", a.shape, mybir.dt.from_np(a.dtype), kind="ExternalInput").ap()
            for k, a in arrays.items()}
    res = nc.dram_tensor("out", (B * N, D), F32, kind="ExternalOutput").ap()
    program(nc, **args, out=res.rearrange("(g t p) d -> g p t d", g=NG, p=128))
    r = _run(nc, [{f"in_{k}": a for k, a in arrays.items()}], core_ids=[0])
    return r.results[0]["out"].reshape(B, N, D)
```

```python
from contextlib import ExitStack

import numpy as np

import concourse.bass as bass
from concourse import mybir

F32 = mybir.dt.float32
ACT = mybir.ActivationFunctionType
ALU = mybir.AluOpType
AX = mybir.AxisListType
I32 = mybir.dt.int32

B, CH, IMG, P = 16, 3, 128, 16
D, F, NH = 192, 768, 12
NI, NT = (IMG // P) ** 2, 32
N = NI + NT
GS = 4
NG = B // GS
HC = 96
TA, TB = GS * NI, GS * N
HD, HD2 = D // NH, 64
DI, KC = 2 * D, 4
TILES_A, TILES_B = TA // 128, TB // 128
KP = CH * P * P // 128
EXPERTS = NH - 2
EPS = 1e-5
ROOT_SEED, ROOT_ROUNDS = 0x5F3759DF, 3
ROOT_STEPS = 3 + 3 * ROOT_ROUNDS

V96 = {"tok_g": 0, "tok_ff2_b": 2, "ln1_g": 4, "ln1_b": 6, "ln2_g": 8, "ln2_b": 10, "ln3_g": 12, "ln3_b": 14,
       "tok_b": 16, "n": 18}
V128 = {"conv_w": 0, "conv_b": 12, "q_w": 15, "q_b": 16, "k_w": 17, "k_b": 18, "n": 19}

LOOP_ORDER = """
    b_ht a_em b_u.0 a_en b_in.0 a_x0 b_in.1 a_f1.0 b_out a_f2.0 b_u.1 b_k b_q a_qk
    b_s.0 b_s.1 b_v b_e.0 b_n.0 b_e.1 b_n.1 a_v
    b_pt.0 b_s.2 b_o.0 a_s.0 b_e.2 a_e.0 b_n.2 b_pt.1 b_s.3 b_o.1 a_s.1 b_e.3 a_e.1 b_n.3
    b_pt.2 a_pt.0 b_o.2 a_o.0 b_pt.3 a_ot.0 a_pt.1 b_o.3 a_o.1 b_pr a_ot.1 a_pr b_u.2
    b_f1.0 b_f1.1 b_f2 a_f1.1 b_u.3
    c_g c_qk.0 c_qk.1 c_v.0 c_qt.0 c_v.1 c_s.0 c_qk.2 c_e.0 c_n.0 c_qt.1 a_f2.1 c_s.1 c_qt.2 c_e.1 c_n.1
    c_pt.0 c_s.2 c_o.0 c_e.2 c_n.2 c_pt.1 c_s.3 c_v.2 c_o.1 c_e.3 c_n.3 c_pt.2 c_v.3 c_o.2 c_pt.3 c_o.3 c_pr
"""
LOOP = [(unit.split(".")[0], int(unit.split(".")[1]) if "." in unit else 0) for unit in LOOP_ORDER.split()]
ORDER = {"first": [u for u in LOOP if u[0][0] == "a"], "loop": LOOP, "last": [u for u in LOOP if u[0][0] != "a"]}
SLOT_OF = {"a_em": "S", "a_x0": "S", "a_f1": "T", "a_f2": "S", "a_qk": "D", "a_v": "S", "a_s": "D", "a_pt": "D",
           "a_o": "S", "a_ot": "S", "a_pr": "S", "b_ht": "T", "b_u": "T", "b_in": "T", "b_out": "T", "b_q": "T",
           "b_k": "T", "b_v": "T", "b_s": "T", "b_pt": "T", "b_o": "S", "b_pr": "T", "b_f1": "T",
           "b_f2": "T", "c_g": "S", "c_qk": "T", "c_qt": "T", "c_v": "D", "c_s": "T", "c_pt": "T", "c_o": "D",
           "c_pr": "T"}
FIXED_SLOT = {("c_qk", 0): "T0", ("c_qk", 1): "T1", ("c_qt", 0): "T0", ("c_s", 0): "T0", ("c_qk", 2): "T1",
              ("c_qt", 1): "T0", ("c_s", 1): "T0", ("c_qt", 2): "T1"}
READ_BY = {
    "a_em": lambda k: [("a_emb", 1)], "a_x0": lambda k: [("x0T", 2)], "a_f1": lambda k: [("a_h", 3 * k + 3)],
    "a_f2": lambda k: [("hT", 2) if k else ("x1T", 2)], "a_qk": lambda k: [("a_qT", 1), ("a_kT", 1)],
    "a_v": lambda k: [("a_vB", 1)], "a_s": lambda k: [("a_sub", k + 1)], "a_pt": lambda k: [("a_pT", k + 1)],
    "a_o": lambda k: [("a_on", k + 1)], "a_ot": lambda k: [("a_oT", k + 1)], "a_pr": lambda k: [("x2T", 1)],
    "b_ht": lambda k: [("h_tm", 1)], "b_u": lambda k: [("lnT", 2 * k + 2)],
    "b_in": lambda k: [("sz", 1) if k else ("xpad", 1)], "b_out": lambda k: [("x1_tm", 1)],
    "b_q": lambda k: [("b_qT", 1)], "b_k": lambda k: [("b_kT", 1)], "b_v": lambda k: [("b_vB", 1)],
    "b_s": lambda k: [("b_sub", k + 1)], "b_pt": lambda k: [("b_pT", k + 1)], "b_o": lambda k: [("b_oT", k + 1)],
    "b_pr": lambda k: [("x2_tm", 1)], "b_f1": lambda k: [("b_h", k + 1)],
    "b_f2": lambda k: [("h2_tm", 1)], "c_g": lambda k: [("g_step", 4)], "c_qk": lambda k: [("qk_raw", k + 1)],
    "c_qt": lambda k: [("c_qkT", k + 1)], "c_v": lambda k: [("c_v", k + 1)], "c_s": lambda k: [("c_sub", k + 1)],
    "c_pt": lambda k: [("c_pT", k + 1)], "c_o": lambda k: [("c_oT", k + 1)],
    "c_pr": lambda k: [("out_tm", 1)],
}


class PsumFills:

    def __init__(self):
        self.at, self.start, self.per, self.last = {}, {}, {}, {}
        total = dict.fromkeys(("T0", "T1", "S0", "S1"), 0)
        for section in ("first", "loop", "last"):
            self.start[section] = dict(total)
            count = dict.fromkeys(total, 0)
            turn = {"T": 0, "S": 0}
            holder = {}
            for unit in ORDER[section]:
                if unit[0] not in SLOT_OF:
                    continue
                kind = SLOT_OF[unit[0]]
                slot = "S0" if kind == "D" else FIXED_SLOT.get(unit, kind + str(turn[kind] % 2))
                if kind != "D":
                    turn[kind] = int(slot[1]) + 1
                taken = ("S0", "S1") if kind == "D" else (slot,)
                before = sorted({holder[bank] for bank in taken if bank in holder})
                for bank in taken:
                    holder[bank] = unit
                count[slot] += 1
                self.at[section, unit] = (slot, before, count[slot])
            self.per[section] = count
            self.last[section] = sorted(set(holder.values()))
            for s in total:
                total[s] += count[s] * (NG - 1 if section == "loop" else 1)


FILLS = PsumFills()

PER_GROUP = {
    "x_in": 16, "txt_in": 16, "a_emb": 1, "a_stats": 2, "a_mv": 2, "a_root": ROOT_STEPS, "a_xn": 2, "x0T": 2,
    "a_h": 6, "x1T": 2, "a_qT": 1, "a_kT": 1, "a_kB": 4, "a_vB": 1, "a_max": 2, "a_sub": 2, "a_exp": 2, "a_pT": 2,
    "a_rec": 2, "a_on": 2, "a_oT": 2, "x2T": 1, "hT": 2,
    "h_tm": 1, "ln_stats": 12, "ln_mv": 12, "ln_root": 4 * ROOT_STEPS + 1, "ln_u": 12, "y_tm": 3, "lnT": 8,
    "xpad": 1, "sz": 1, "conv": 12, "conv_act": 3, "gate": 3, "x1_tm": 1, "b_qT": 1, "b_kT": 1, "b_kB": 8,
    "b_vB": 1, "b_max": 4, "b_sub": 4, "b_exp": 4, "b_pT": 4, "b_sum": 4, "b_rec": 4, "b_w": 4, "b_oT": 4, "x2_tm": 1,
    "hx": 2, "b_h": 2, "h2_tm": 1, "h2b": 1,
    "logits": 1, "g_step": 23, "g_exp": 1, "gates": 2, "sq": 3, "qk_raw": 3, "ss": 3, "qk_root": 3 * ROOT_STEPS, "qkn": 3,
    "c_qkT": 3, "c_v": 4, "c_max": 4, "c_sub": 4, "c_exp": 4, "c_pT": 4, "c_sum": 4, "c_rec": 4, "c_gr": 4,
    "c_w": 4, "c_oT": 4, "out_tm": 1, "out_dma": 16, "pad": 1,
}


def program(nc, xT, txtT, patchT, ident, peT, mask, prio, vec96, vec128, patch_b, tok_ff1, tok_ff2, tok_qkv, tok_proj,
            in_proj, out_proj, qkv, attn_proj, ffn1, ffn2, ffn2_b, cqkv, cproj, cproj_b, cgate, out):
    ctx = ExitStack()
    with ctx:
        def sb(name, shape):
            return ctx.enter_context(nc.sbuf_tensor(name, shape, F32))

        def sem(name):
            return ctx.enter_context(nc.semaphore(name))

        w_patch = sb("w_patch", [128, KP, D])
        w_ident = sb("w_ident", [128, 128])
        w_pe = sb("w_pe", [HC, 2, NI])
        w_mask = sb("w_mask", [HC, 6])
        w_prio = sb("w_prio", [N, EXPERTS])
        v96 = sb("v96", [HC, V96["n"]])
        v128 = sb("v128", [128, V128["n"]])
        w_patch_b = sb("w_patch_b", [128, D])
        w_tff1 = sb("w_tff1", [HC + 1, 2, F])
        w_tff2 = sb("w_tff2", [128, F // 128, D])
        w_tqkv = sb("w_tqkv", [HC + 1, 2, 3 * D])
        w_tproj = sb("w_tproj", [HC + 1, 2, D])
        w_in = sb("w_in", [HC, 2, 2 * DI])
        w_out = sb("w_out", [128, DI // 128, D])
        w_qkv = sb("w_qkv", [HC + 1, 2, 3 * D])
        w_proj = sb("w_proj", [HC + 1, 2, D])
        w_ff1 = sb("w_ff1", [HC + 1, 2, F])
        w_ff2 = sb("w_ff2", [128, F // 128, D])
        w_ff2_b = sb("w_ff2_b", [128, D])
        w_cqkv = sb("w_cqkv", [HC + 1, 2, 3 * NH * HD2])
        w_cproj = sb("w_cproj", [128, NH * HD2 // 128, D])
        w_cproj_b = sb("w_cproj_b", [128, D])
        w_cgate = sb("w_cgate", [HC, 2, EXPERTS + 4])
        w_mean = sb("w_mean", [HC + 1, 2, 2 * NH])
        x_in = sb("x_in", [128, KP, TA])
        a_emb = sb("a_emb", [128, TILES_A, D])
        a_bn = sb("a_bn", [128, TILES_A, 6])
        a_mv = sb("a_mv", [128, TILES_A, 2])
        a_root = sb("a_root", [128, 3, TILES_A])
        x0T = sb("x0T", [HC + 1, 2, TA])
        x1T = sb("x1T", [HC + 1, 2, TA])
        x2T = sb("x2T", [HC + 1, 2, TA])
        a_wide = sb("a_wide", [128, F // 128 * TA])
        a_h = a_wide[:, :].rearrange("p (c t) -> p c t", t=TA)
        a_kB = a_wide[0:HC, :].rearrange("p (c h t) -> p c h t", c=2, h=6)
        a_qT = sb("a_qT", [HC, 2, TA])
        a_kT = sb("a_kT", [HC, 2, TA])
        a_vB = sb("a_vB", [128, GS, NH // 2, 2 * (HD + 1)])
        a_p = sb("a_p", [128, 2, NH * NI])
        a_pT = sb("a_pT", [128, NH // 2, 128])
        a_max = sb("a_max", [128, 2, NH])
        a_rec = sb("a_rec", [128, 2, NH])
        a_on = sb("a_on", [128, D])
        a_oT = sb("a_oT", [HC + 1, 2, TA])
        hT = sb("hT", [HC, 2, GS, N])
        h_tm = sb("h_tm", [128, TILES_B, D])
        xr = sb("xr", [128, TILES_B, D])
        hx = sb("hx", [128, TILES_B, D])
        u = sb("u", [128, TILES_B, D])
        bn = sb("bn", [128, TILES_B, 6])
        mv = sb("mv", [128, TILES_B, 2])
        seen = sb("seen", [128, TILES_A + TILES_B])
        root = sb("root", [128, 3, 2 * TILES_B])
        bT = sb("bT", [HC + 1, 2, TB])
        scratch = sb("scratch", [128, DI // 128 * GS * (N + KC - 1) + 2 * DI // 128 * TB])
        n0, n1 = DI // 128 * GS * (N + KC - 1), DI // 128 * TB
        xpad = scratch[:, 0:n0].rearrange("p (c s t) -> p c s t", c=DI // 128, s=GS)
        cv = scratch[:, n0:n0 + n1].rearrange("p (c s t) -> p c s t", c=DI // 128, s=GS)
        sz = scratch[:, n0 + n1:n0 + 2 * n1].rearrange("p (c t) -> p c t", c=DI // 128)
        qkw = 2 * NH * HD2
        sq = scratch[:, 0:qkw]
        qkn = (scratch[:, qkw:2 * qkw], x_in[:, :, :].rearrange("p j t -> p (j t)"))
        heads = sb("heads", [128, 4 * TB + GS * NH * 2 * HD])
        b_qT = heads[0:HC, 0:2 * TB].rearrange("p (c t) -> p c t", c=2)
        b_kT = heads[0:HC, 2 * TB:4 * TB].rearrange("p (c t) -> p c t", c=2)
        b_vB = heads[0:N, 4 * TB:].rearrange("p (s h d) -> p s h d", s=GS, h=NH)
        c_v = heads[0:N, 0:2 * NH * HD2].rearrange("p (b h d) -> p b h d", b=2, h=NH)
        b_kB = sb("b_kB", [128, 2 * 2 * 6 * N])
        b_kBv = b_kB[0:HC, :].rearrange("p (b c h t) -> p b c h t", b=2, c=2, h=6)
        c_oT = b_kB[:, :].rearrange("p (c t) -> p c t", c=NH * HD2 // 128)
        pr = sb("pr", [N, 2, NH * N])
        pT = sb("pT", [N, NH, N])
        smax = sb("smax", [N, 2, NH])
        psum = sb("psum", [N, 2, NH])
        rec = sb("rec", [N, 2, NH])
        gr = sb("gr", [N, 2, NH])
        b_wide = sb("b_wide", [128, F // 128 * TB])
        b_h = b_wide[:, :].rearrange("p (c t) -> p c t", t=TB)
        c_qT = b_h
        c_kB = sb("c_kB", [128, NH // 2, 2, TB])
        gsm = sb("gsm", [N, 12, GS, EXPERTS + 4])
        gates = sb("gates", [N, GS, NH])
        ss = sb("ss", [128, 2 * NH])
        qk_root = sb("qk_root", [128, 3, 2 * NH])

        ps = {"T0": ctx.enter_context(nc.psum_tensor("psT0", [128, 3, 512], F32)),
              "T1": ctx.enter_context(nc.psum_tensor("psT1", [128, 3, 512], F32))}
        psS = ctx.enter_context(nc.psum_tensor("psS", [128, 2, 512], F32))

        S = {name: sem(name) for name in PER_GROUP}
        filled = {s: sem("filled_" + s) for s in ("T0", "T1", "S0", "S1")}
        loads = {n: sem("load_" + n) for n in ("patch", "vec", "tff1", "tff2", "tqkv", "tproj", "in", "out", "qkv",
                                               "proj", "ff1", "ff2", "cqkv", "cproj", "ident")}
        n_loads = {"patch": 1, "vec": 8, "tff1": 1, "tff2": 1, "tqkv": 1, "tproj": 1, "in": 1, "out": 1, "qkv": 1,
                   "proj": 1, "ff1": 1, "ff2": 1, "cqkv": 1, "cproj": 2, "ident": 1}
        s_set = sem("constants_set")
        s_mean = sem("weight_mean")
        s_centred = sem("weight_centred")

        class Where:

            def __init__(self, section, step, group_a, group_b):
                self.section, self.step, self.a, self.b = section, step, group_a, group_b

        def upto(name, group, k=None):
            return group * PER_GROUP[name] + (PER_GROUP[name] if k is None else k)

        def slot(w, unit):
            s = FILLS.at[w.section, unit][0]
            if s[0] == "T":
                return ps[s]
            return psS[:, :, :] if SLOT_OF[unit[0]] == "D" else psS[:, int(s[1]), :]

        def reads(w, units):
            most = {}
            for unit in units:
                for name, k in READ_BY[unit[0]](unit[1]):
                    most[name] = (max(k, most[name][0]) if name in most else k, w.a if unit[0][0] == "a" else w.b)
            return [(S[name], upto(name, group, k)) for name, (k, group) in most.items()]

        def reads_before(w, unit):
            return reads(w, FILLS.at[w.section, unit][1])

        def fill_count(w, unit):
            s, _, n = FILLS.at[w.section, unit]
            return w.step * FILLS.per[w.section][s] + FILLS.start[w.section][s] + n

        def fill_sem(w, unit):
            return filled[FILLS.at[w.section, unit][0]]

        def sections(eng, steps, at_end=lambda w: None):
            for unit in ORDER["first"]:
                if unit[0] in steps:
                    steps[unit[0]](Where("first", 0, 0, None), unit[1])
            at_end(Where("first", 0, 0, None))
            with eng.Fori(0, NG - 1) as i:
                w = Where("loop", i, i + 1, i)
                for unit in ORDER["loop"]:
                    if unit[0] in steps:
                        steps[unit[0]](w, unit[1])
                at_end(w)
            for unit in ORDER["last"]:
                if unit[0] in steps:
                    steps[unit[0]](Where("last", 0, None, NG - 1), unit[1])

        def col96(name, c):
            return v96[:, V96[name] + c:V96[name] + c + 1]

        def col128(name, c=0):
            return v128[:, V128[name] + c:V128[name] + c + 1]

        block = ctx.enter_context(nc.Block())

        @block.sync
        def _(sp):
            sp.dma_start(w_patch[:, :, :], patchT).then_inc(loads["patch"], 16)
            sp.dma_start(x_in[:, :, :], xT[0]).then_inc(S["x_in"], 16)
            for dst, src in ((v96, vec96), (v128, vec128), (w_pe, peT), (w_mask, mask), (w_prio, prio),
                             (w_patch_b, patch_b), (w_ff2_b, ffn2_b), (w_cproj_b, cproj_b)):
                sp.dma_start(dst[:], src).then_inc(loads["vec"], 16)
            sp.dma_start(w_ident[:, :], ident).then_inc(loads["ident"], 16)
            for name, dst, src in (("tff1", w_tff1, tok_ff1), ("tff2", w_tff2, tok_ff2), ("tqkv", w_tqkv, tok_qkv),
                                   ("tproj", w_tproj, tok_proj), ("in", w_in, in_proj), ("out", w_out, out_proj),
                                   ("qkv", w_qkv, qkv), ("proj", w_proj, attn_proj), ("ff1", w_ff1, ffn1),
                                   ("ff2", w_ff2, ffn2)):
                sp.dma_start(dst[:], src).then_inc(loads[name], 16)
            sp.dma_start(hT[:, :, :, NI:N], txtT[0]).then_inc(S["txt_in"], 16)
            sp.dma_start(w_cproj[:, :, :], cproj).then_inc(loads["cproj"], 16)
            sp.dma_start(w_cgate[:, :, :], cgate).then_inc(loads["cproj"], 16)
            sp.dma_start(w_cqkv[:, :, :], cqkv).then_inc(loads["cqkv"], 16)

            def c_pr(w, _):
                sp.wait_ge(S["out_tm"], upto("out_tm", w.b))
                sp.dma_start(out[w.b], u[:, :, :]).then_inc(S["out_dma"], 16)

            sp.sem_inc(S["out_dma"], 16)
            sections(sp, {"c_pr": c_pr})
            sp.wait_ge(S["out_dma"], 16 * (NG + 1))

        @block.tensor
        def _(pe):
            def chunks(out_ap, lhs, rhs, last, bias_row=True):
                k = HC + 1 if bias_row else HC
                pe.matmul(out_ap, lhs(0, k), rhs(0, k), start=True, stop=False)
                m = pe.matmul(out_ap, lhs(1, HC), rhs(1, HC), start=False, stop=True)
                if last is not None:
                    m.then_inc(last, 1)

            def all_read(w):
                for sem_read, value in reads(w, FILLS.last[w.section]):
                    pe.wait_ge(sem_read, value)

            def a_em(w, _):
                for sem_read, value in reads_before(w, ("a_em", 0)):
                    pe.wait_ge(sem_read, value)
                t = slot(w, ("a_em", 0))
                if w.section == "first":
                    pe.wait_ge(loads["patch"], 16 * n_loads["patch"])
                pe.wait_ge(S["x_in"], upto("x_in", w.a))
                for tile in range(TILES_A):
                    for j in range(KP):
                        m = pe.matmul(t[:, tile * D:(tile + 1) * D], x_in[:, j, tile * 128:(tile + 1) * 128], w_patch[:, j, :],
                                      start=(j == 0), stop=(j == KP - 1))
                m.then_inc(fill_sem(w, ("a_em", 0)), 1)

            def a_x0(w, _):
                for sem_read, value in reads_before(w, ("a_x0", 0)):
                    pe.wait_ge(sem_read, value)
                t = slot(w, ("a_x0", 0)).rearrange("p (c t) -> p c t", c=2)
                if w.section == "first":
                    pe.wait_ge(loads["ident"], 16 * n_loads["ident"])
                pe.wait_ge(S["a_xn"], upto("a_xn", w.a))
                for tile in range(TILES_A):
                    for c in range(2):
                        m = pe.transpose(t[0:HC, c, tile * 128:(tile + 1) * 128],
                                         a_emb[:, tile, c * HC:(c + 1) * HC], w_ident[:, :])
                m.then_inc(fill_sem(w, ("a_x0", 0)), 1)

            def a_f1(w, j):
                for sem_read, value in reads_before(w, ("a_f1", j)):
                    pe.wait_ge(sem_read, value)
                t = slot(w, ("a_f1", j))
                if w.section == "first" and j == 0:
                    pe.wait_ge(loads["tff1"], 16 * n_loads["tff1"])
                    pe.wait_ge(s_set, 1)
                src = x0T if j == 0 else x2T
                pe.wait_ge(S["x0T" if j == 0 else "x2T"], upto("x0T" if j == 0 else "x2T", w.a))
                for c in range(F // 128):
                    o = t[:, c // 2, (c % 2) * TA:(c % 2 + 1) * TA]
                    chunks(o, lambda kc, k: w_tff1[0:k, kc, c * 128:(c + 1) * 128], lambda kc, k: src[0:k, kc, :],
                           fill_sem(w, ("a_f1", j)) if c == F // 128 - 1 else None)

            def a_f2(w, j):
                for sem_read, value in reads_before(w, ("a_f2", j)):
                    pe.wait_ge(sem_read, value)
                t = slot(w, ("a_f2", j)).rearrange("p (c t) -> p c t", c=2)
                if w.section == "first" and j == 0:
                    pe.wait_ge(loads["tff2"], 16 * n_loads["tff2"])
                for c in range(2):
                    for kc in range(F // 128):
                        if c == 0 and kc % 2 == 0:
                            pe.wait_ge(S["a_h"], upto("a_h", w.a, 3 * j + kc // 2 + 1))
                        m = pe.matmul(t[0:HC, c, :], w_tff2[:, kc, c * HC:(c + 1) * HC], a_h[:, kc, :],
                                      start=(kc == 0), stop=(kc == F // 128 - 1))
                m.then_inc(fill_sem(w, ("a_f2", j)), 1)

            def a_qk(w, _):
                for sem_read, value in reads_before(w, ("a_qk", 0)):
                    pe.wait_ge(sem_read, value)
                t = slot(w, ("a_qk", 0))
                if w.section == "first":
                    pe.wait_ge(loads["tqkv"], 16 * n_loads["tqkv"])
                pe.wait_ge(S["x1T"], upto("x1T", w.a))
                for n in range(4):
                    o = t[0:HC, n // 2, (n % 2) * TA:(n % 2 + 1) * TA]
                    chunks(o, lambda kc, k: w_tqkv[0:k, kc, n * HC:(n + 1) * HC], lambda kc, k: x1T[0:k, kc, :],
                           fill_sem(w, ("a_qk", 0)) if n == 3 else None)

            def a_v(w, _):
                for sem_read, value in reads_before(w, ("a_v", 0)):
                    pe.wait_ge(sem_read, value)
                t = slot(w, ("a_v", 0))
                wv = w_tqkv[:, :, 2 * D:3 * D].rearrange("p c (n two d) -> p c two n d", two=2, d=HD)
                for s in range(GS):
                    for odd in range(2):
                        chunks(t[64 * odd:64 * odd + NI, s * HC:(s + 1) * HC],
                               lambda kc, k: x1T[0:k, kc, s * NI:(s + 1) * NI], lambda kc, k: wv[0:k, kc, odd],
                               fill_sem(w, ("a_v", 0)) if s == GS - 1 and odd else None)

            def a_s(w, t2):
                for sem_read, value in reads_before(w, ("a_s", t2)):
                    pe.wait_ge(sem_read, value)
                t = slot(w, ("a_s", t2))
                pe.wait_ge(S["a_qT"], upto("a_qT", w.a))
                pe.wait_ge(S["a_kB"], upto("a_kB", w.a, 2 * t2 + 2))
                for half in range(2):
                    s = 2 * t2 + half
                    for c in range(2):
                        m = pe.matmul(t[64 * half:64 * half + NI, c, 0:6 * NI], a_qT[:, c, s * NI:(s + 1) * NI],
                                      a_kB[:, c, :, half * NI:(half + 1) * NI], start=True, stop=True)
                m.then_inc(fill_sem(w, ("a_s", t2)), 1)

            def a_pt(w, t2):
                for sem_read, value in reads_before(w, ("a_pt", t2)):
                    pe.wait_ge(sem_read, value)
                t = slot(w, ("a_pt", t2))
                pe.wait_ge(S["a_exp"], upto("a_exp", w.a, t2 + 1))
                for n in range(NH // 2):
                    m = pe.transpose(t[:, n // 3, (n % 3) * 128:(n % 3 + 1) * 128],
                                     a_p[:, t2, n * 128:(n + 1) * 128], w_ident[:, :])
                m.then_inc(fill_sem(w, ("a_pt", t2)), 1)

            def a_o(w, t2):
                for sem_read, value in reads_before(w, ("a_o", t2)):
                    pe.wait_ge(sem_read, value)
                t = slot(w, ("a_o", t2))
                pe.wait_ge(S["a_pT"], upto("a_pT", w.a, t2 + 1))
                pe.wait_ge(S["a_vB"], upto("a_vB", w.a))
                for half in range(2):
                    for n in range(NH // 2):
                        k = 2 * (HD + 1)
                        m = pe.matmul(t[64 * half:64 * half + NI, n * k:(n + 1) * k],
                                      a_pT[:, n, half * NI:(half + 1) * NI], a_vB[:, 2 * t2 + half, n, :],
                                      start=True, stop=True)
                m.then_inc(fill_sem(w, ("a_o", t2)), 1)

            def a_ot(w, t2):
                for sem_read, value in reads_before(w, ("a_ot", t2)):
                    pe.wait_ge(sem_read, value)
                t = slot(w, ("a_ot", t2))
                pe.wait_ge(S["a_on"], upto("a_on", w.a, t2 + 1))
                for c in range(2):
                    m = pe.transpose(t[0:HC, c * 128:(c + 1) * 128], a_on[:, c * HC:(c + 1) * HC], w_ident[:, :])
                m.then_inc(fill_sem(w, ("a_ot", t2)), 1)

            def a_pr(w, _):
                for sem_read, value in reads_before(w, ("a_pr", 0)):
                    pe.wait_ge(sem_read, value)
                t = slot(w, ("a_pr", 0)).rearrange("p (c t) -> p c t", c=2)
                if w.section == "first":
                    pe.wait_ge(loads["tproj"], 16 * n_loads["tproj"])
                pe.wait_ge(S["a_oT"], upto("a_oT", w.a))
                for c in range(2):
                    chunks(t[0:HC, c, :], lambda kc, k: w_tproj[0:k, kc, c * HC:(c + 1) * HC],
                           lambda kc, k: a_oT[0:k, kc, :], fill_sem(w, ("a_pr", 0)) if c else None)

            def b_ht(w, _):
                for sem_read, value in reads_before(w, ("b_ht", 0)):
                    pe.wait_ge(sem_read, value)
                t = slot(w, ("b_ht", 0))
                pe.wait_ge(S["hT"], upto("hT", w.b))
                pe.wait_ge(S["txt_in"], upto("txt_in", w.b))
                hv = hT[:, :, :, :].rearrange("p c s t -> p c (s t)")
                for tile in range(TILES_B):
                    for c in range(2):
                        m = pe.transpose(t[:, tile, c * HC:(c + 1) * HC], hv[:, c, tile * 128:(tile + 1) * 128],
                                         w_ident[0:HC, 0:HC])
                m.then_inc(fill_sem(w, ("b_ht", 0)), 1)

            def b_u(w, n):
                for sem_read, value in reads_before(w, ("b_u", n)):
                    pe.wait_ge(sem_read, value)
                t = slot(w, ("b_u", n))
                for tile in range(TILES_B):
                    pe.wait_ge(S["ln_u"], upto("ln_u", w.b, 3 * n + tile + 1))
                    for c in range(2):
                        m = pe.transpose(t[0:HC, c, tile * 128:(tile + 1) * 128], u[:, tile, c * HC:(c + 1) * HC],
                                         w_ident[:, :])
                m.then_inc(fill_sem(w, ("b_u", n)), 1)

            def b_in(w, j):
                for sem_read, value in reads_before(w, ("b_in", j)):
                    pe.wait_ge(sem_read, value)
                t = slot(w, ("b_in", j))
                if j == 0:
                    pe.wait_ge(loads["in"], 16 * n_loads["in"])
                pe.wait_ge(S["lnT"], upto("lnT", w.b, 2))
                for c in range(3):
                    f0 = j * DI + c * 128
                    chunks(t[:, c, 0:TB], lambda kc, k: w_in[0:k, kc, f0:f0 + 128], lambda kc, k: bT[0:k, kc, :],
                           fill_sem(w, ("b_in", j)) if c == 2 else None, bias_row=False)

            def tm_product(w, unit, lhs, rhs, n_k):
                t = slot(w, unit)
                for tile in range(TILES_B):
                    for kc in range(n_k):
                        m = pe.matmul(t[:, tile, 0:D], lhs[:, kc, tile * 128:(tile + 1) * 128], rhs[:, kc, :],
                                      start=(kc == 0), stop=(kc == n_k - 1))
                m.then_inc(fill_sem(w, unit), 1)

            def b_out(w, _):
                for sem_read, value in reads_before(w, ("b_out", 0)):
                    pe.wait_ge(sem_read, value)
                pe.wait_ge(loads["out"], 16 * n_loads["out"])
                pe.wait_ge(S["gate"], upto("gate", w.b))
                tm_product(w, ("b_out", 0), cv.rearrange("p c s t -> p c (s t)"), w_out, DI // 128)

            def b_qk(w, name, f0):
                for sem_read, value in reads_before(w, (name, 0)):
                    pe.wait_ge(sem_read, value)
                t = slot(w, (name, 0))
                pe.wait_ge(loads["qkv"], 16 * n_loads["qkv"])
                pe.wait_ge(S["lnT"], upto("lnT", w.b, 4))
                for c in range(2):
                    chunks(t[0:HC, c, 0:TB], lambda kc, k: w_qkv[0:k, kc, f0 + c * HC:f0 + (c + 1) * HC],
                           lambda kc, k: bT[0:k, kc, :], fill_sem(w, (name, 0)) if c else None)

            def b_v(w, _):
                for sem_read, value in reads_before(w, ("b_v", 0)):
                    pe.wait_ge(sem_read, value)
                t = slot(w, ("b_v", 0))
                for s in range(GS):
                    chunks(t[0:N, s // 2, (s % 2) * D:(s % 2 + 1) * D], lambda kc, k: bT[0:k, kc, s * N:(s + 1) * N],
                           lambda kc, k: w_qkv[0:k, kc, 2 * D:3 * D], fill_sem(w, ("b_v", 0)) if s == GS - 1 else None)

            def b_s(w, s):
                for sem_read, value in reads_before(w, ("b_s", s)):
                    pe.wait_ge(sem_read, value)
                t = slot(w, ("b_s", s))
                pe.wait_ge(S["b_qT"], upto("b_qT", w.b))
                pe.wait_ge(S["b_kB"], upto("b_kB", w.b, 2 * s + 2))
                for c, h0, h1, bank, col in ((0, 0, 4, 0, 0), (0, 4, 6, 1, 0), (1, 0, 2, 1, 2), (1, 2, 6, 2, 0)):
                    m = pe.matmul(t[0:N, bank, col * N:(col + h1 - h0) * N], b_qT[:, c, s * N:(s + 1) * N],
                                  b_kBv[:, s % 2, c, h0:h1, :], start=True, stop=True)
                m.then_inc(fill_sem(w, ("b_s", s)), 1)

            def turn_p(w, unit, s):
                t = slot(w, unit)
                for h in range(NH):
                    m = pe.transpose(t[0:N, h // 4, (h % 4) * N:(h % 4 + 1) * N], pr[:, s % 2, h * N:(h + 1) * N],
                                     w_ident[0:N, 0:N])
                m.then_inc(fill_sem(w, unit), 1)

            def b_pt(w, s):
                for sem_read, value in reads_before(w, ("b_pt", s)):
                    pe.wait_ge(sem_read, value)
                pe.wait_ge(S["b_w"], upto("b_w", w.b, s + 1))
                turn_p(w, ("b_pt", s), s)

            def b_o(w, s):
                for sem_read, value in reads_before(w, ("b_o", s)):
                    pe.wait_ge(sem_read, value)
                t = slot(w, ("b_o", s))
                pe.wait_ge(S["b_pT"], upto("b_pT", w.b, s + 1))
                pe.wait_ge(S["b_vB"], upto("b_vB", w.b))
                for h in range(NH):
                    c, row = h // 6, h % 6 // 2 * 2 * HD
                    m = pe.matmul(t[row:row + 2 * HD, c * N:(c + 1) * N], b_vB[:, s, h, :], pT[:, h, :],
                                  start=(h % 2 == 0), stop=(h % 2 == 1))
                m.then_inc(fill_sem(w, ("b_o", s)), 1)

            def b_pr(w, _):
                for sem_read, value in reads_before(w, ("b_pr", 0)):
                    pe.wait_ge(sem_read, value)
                t = slot(w, ("b_pr", 0))
                pe.wait_ge(loads["proj"], 16 * n_loads["proj"])
                pe.wait_ge(S["b_oT"], upto("b_oT", w.b))
                for tile in range(TILES_B):
                    chunks(t[:, tile, 0:D], lambda kc, k: bT[0:k, kc, tile * 128:(tile + 1) * 128],
                           lambda kc, k: w_proj[0:k, kc, :], fill_sem(w, ("b_pr", 0)) if tile == TILES_B - 1 else None)

            def b_f1(w, j):
                for sem_read, value in reads_before(w, ("b_f1", j)):
                    pe.wait_ge(sem_read, value)
                t = slot(w, ("b_f1", j))
                pe.wait_ge(loads["ff1"], 16 * n_loads["ff1"])
                pe.wait_ge(S["lnT"], upto("lnT", w.b, 6))
                for c in range(3):
                    f0 = (3 * j + c) * 128
                    chunks(t[:, c, 0:TB], lambda kc, k: w_ff1[0:k, kc, f0:f0 + 128], lambda kc, k: bT[0:k, kc, :],
                           fill_sem(w, ("b_f1", j)) if c == 2 else None)

            def b_f2(w, _):
                for sem_read, value in reads_before(w, ("b_f2", 0)):
                    pe.wait_ge(sem_read, value)
                pe.wait_ge(loads["ff2"], 16 * n_loads["ff2"])
                pe.wait_ge(S["b_h"], upto("b_h", w.b))
                tm_product(w, ("b_f2", 0), b_h, w_ff2, F // 128)

            def c_g(w, _):
                for sem_read, value in reads_before(w, ("c_g", 0)):
                    pe.wait_ge(sem_read, value)
                t = slot(w, ("c_g", 0))
                pe.wait_ge(loads["cproj"], 16 * n_loads["cproj"])
                pe.wait_ge(S["lnT"], upto("lnT", w.b, 8))
                k14 = EXPERTS + 4
                for s in range(GS):
                    chunks(t[0:N, s * k14:(s + 1) * k14], lambda kc, k: bT[0:k, kc, s * N:(s + 1) * N],
                           lambda kc, k: w_cgate[0:k, kc, :], fill_sem(w, ("c_g", 0)) if s == GS - 1 else None,
                           bias_row=False)

            def c_qk(w, tile):
                for sem_read, value in reads_before(w, ("c_qk", tile)):
                    pe.wait_ge(sem_read, value)
                t = slot(w, ("c_qk", tile))
                pe.wait_ge(s_centred, 2)
                pe.wait_ge(S["lnT"], upto("lnT", w.b, 8))
                for n in range(3):
                    chunks(t[:, n, :], lambda kc, k: bT[0:k, kc, tile * 128:(tile + 1) * 128],
                           lambda kc, k: w_cqkv[0:k, kc, n * 512:(n + 1) * 512],
                           fill_sem(w, ("c_qk", tile)) if n == 2 else None)

            def c_qt(w, tile):
                for sem_read, value in reads_before(w, ("c_qt", tile)):
                    pe.wait_ge(sem_read, value)
                t = slot(w, ("c_qt", tile))
                pe.wait_ge(S["qkn"], upto("qkn", w.b, tile + 1))
                for n in range(NH):
                    m = pe.transpose(t[:, n // 4, (n % 4) * 128:(n % 4 + 1) * 128], qkn[tile % 2][:, n * 128:(n + 1) * 128],
                                     w_ident[:, :])
                m.then_inc(fill_sem(w, ("c_qt", tile)), 1)

            def c_v_(w, s):
                for sem_read, value in reads_before(w, ("c_v", s)):
                    pe.wait_ge(sem_read, value)
                t = slot(w, ("c_v", s))
                half = NH * HD2 // 2
                for n in range(2):
                    f0 = 2 * NH * HD2 + n * half
                    chunks(t[0:N, n, 0:half], lambda kc, k: bT[0:k, kc, s * N:(s + 1) * N],
                           lambda kc, k: w_cqkv[0:k, kc, f0:f0 + half], fill_sem(w, ("c_v", s)) if n else None)

            def c_s(w, s):
                for sem_read, value in reads_before(w, ("c_s", s)):
                    pe.wait_ge(sem_read, value)
                t = slot(w, ("c_s", s))
                pe.wait_ge(S["c_qkT"], upto("c_qkT", w.b, ((s + 1) * N - 1) // 128 + 1))
                for n in range(NH // 2):
                    m = pe.matmul(t[0:N, n // 2, (n % 2) * 2 * N:(n % 2 + 1) * 2 * N], c_qT[:, n, s * N:(s + 1) * N],
                                  c_kB[:, n, :, s * N:(s + 1) * N], start=True, stop=True)
                m.then_inc(fill_sem(w, ("c_s", s)), 1)

            def c_pt(w, s):
                for sem_read, value in reads_before(w, ("c_pt", s)):
                    pe.wait_ge(sem_read, value)
                pe.wait_ge(S["c_w"], upto("c_w", w.b, s + 1))
                turn_p(w, ("c_pt", s), s)

            def c_o(w, s):
                for sem_read, value in reads_before(w, ("c_o", s)):
                    pe.wait_ge(sem_read, value)
                t = slot(w, ("c_o", s))
                pe.wait_ge(S["c_pT"], upto("c_pT", w.b, s + 1))
                pe.wait_ge(S["c_v"], upto("c_v", w.b, min(s + 2, GS)))
                for h in range(NH):
                    n, row = h // 2, h % 2 * HD2
                    m = pe.matmul(t[row:row + HD2, n // 3, (n % 3) * N:(n % 3 + 1) * N], c_v[:, s % 2, h, :],
                                  pT[:, h, :], start=True, stop=True)
                m.then_inc(fill_sem(w, ("c_o", s)), 1)

            def c_pr(w, _):
                for sem_read, value in reads_before(w, ("c_pr", 0)):
                    pe.wait_ge(sem_read, value)
                pe.wait_ge(S["c_oT"], upto("c_oT", w.b))
                tm_product(w, ("c_pr", 0), c_oT, w_cproj, NH * HD2 // 128)

            sections(pe, {"a_em": a_em, "a_x0": a_x0, "a_f1": a_f1, "a_f2": a_f2, "a_qk": a_qk, "a_v": a_v, "a_s": a_s,
                          "a_pt": a_pt, "a_o": a_o, "a_ot": a_ot, "a_pr": a_pr, "b_ht": b_ht, "b_u": b_u,
                          "b_in": b_in, "b_out": b_out, "b_q": lambda w, n: b_qk(w, "b_q", 0),
                          "b_k": lambda w, n: b_qk(w, "b_k", D), "b_v": b_v, "b_s": b_s, "b_pt": b_pt, "b_o": b_o,
                          "b_pr": b_pr, "b_f1": b_f1, "b_f2": b_f2, "c_g": c_g, "c_qk": c_qk,
                          "c_qt": c_qt, "c_v": c_v_, "c_s": c_s, "c_pt": c_pt, "c_o": c_o,
                          "c_pr": c_pr}, at_end=all_read)

        @block.scalar
        def _(act):
            act.wait_ge(s_set, 1)
            act.wait_ge(loads["vec"], 16 * n_loads["vec"])

            def a_f1(w, j):
                act.wait_ge(fill_sem(w, ("a_f1", j)), fill_count(w, ("a_f1", j)))
                t = slot(w, ("a_f1", j))
                for n in range(3):
                    m = act.activation(a_h[:, 2 * n:2 * n + 2, :], t[:, n, :].rearrange("p (c t) -> p c t", c=2),
                                       ACT.Gelu_apprx_tanh).then_inc(S["a_h"], 1)

            def a_qk(w, _):
                act.wait_ge(fill_sem(w, ("a_qk", 0)), fill_count(w, ("a_qk", 0)))
                t = slot(w, ("a_qk", 0))
                act.activation(a_kT[:, :, :], t[0:HC, 1, :].rearrange("p (c t) -> p c t", c=2), ACT.Copy)\
                   .then_inc(S["a_kT"], 1)
                act.activation(a_qT[:, :, :], t[0:HC, 0, :].rearrange("p (c t) -> p c t", c=2), ACT.Copy)\
                   .then_inc(S["a_qT"], 1)

            def a_v(w, _):
                act.wait_ge(fill_sem(w, ("a_v", 0)), fill_count(w, ("a_v", 0)))
                t = slot(w, ("a_v", 0))
                for odd in range(2):
                    r = slice(64 * odd, 64 * odd + 64)
                    src = t[r, 0:GS * HC].rearrange("p (s n d) -> p s n d", s=GS, d=HD)
                    m = act.activation(a_vB[r, :, :, odd * (HD + 1):odd * (HD + 1) + HD], src, ACT.Copy)
                m.then_inc(S["a_vB"], 1)

            def a_e(w, t2):
                act.wait_ge(S["a_sub"], upto("a_sub", w.a, t2 + 1))
                act.activation(a_p[:, t2, :], a_p[:, t2, :], ACT.Exp, scale=HD ** -0.5).then_inc(S["a_exp"], 1)

            def a_pt(w, t2):
                act.wait_ge(fill_sem(w, ("a_pt", t2)), fill_count(w, ("a_pt", t2)))
                t = slot(w, ("a_pt", t2))
                act.activation(a_pT[:, :, :].rearrange("p (b n) t -> p b (n t)", b=2), t[:, 0:2, 0:384], ACT.Copy)\
                   .then_inc(S["a_pT"], 1)

            def a_ot(w, t2):
                act.wait_ge(fill_sem(w, ("a_ot", t2)), fill_count(w, ("a_ot", t2)))
                t = slot(w, ("a_ot", t2))
                act.activation(a_oT[0:HC, :, t2 * 128:(t2 + 1) * 128],
                               t[0:HC, 0:256].rearrange("p (c t) -> p c t", c=2), ACT.Copy)\
                   .then_inc(S["a_oT"], 1)

            def b_ht(w, _):
                if w.section == "loop":
                    act.wait_ge(S["a_emb"], upto("a_emb", w.b))
                    act.dma_start(x_in[:, :, :], xT[w.a]).then_inc(S["x_in"], 16)
                act.wait_ge(fill_sem(w, ("b_ht", 0)), fill_count(w, ("b_ht", 0)))
                t = slot(w, ("b_ht", 0))
                if w.section == "loop":
                    act.dma_start(hT[:, :, :, NI:N], txtT[w.a]).then_inc(S["txt_in"], 16)
                act.activation(h_tm[:, :, :], t[:, :, 0:D], ACT.Copy)\
                   .then_inc(S["h_tm"], 1)

            def b_u(w, n):
                act.wait_ge(fill_sem(w, ("b_u", n)), fill_count(w, ("b_u", n)))
                t = slot(w, ("b_u", n))
                if n < 3:
                    act.activation(bT[0:HC, 0, :], t[0:HC, 0, 0:TB], ACT.Identity, scale=col96(f"ln{n + 1}_g", 0),
                                   bias=col96(f"ln{n + 1}_b", 0))\
                       .then_inc(S["lnT"], 1)
                else:
                    act.activation(bT[0:HC, 0, :], t[0:HC, 0, 0:TB], ACT.Copy)\
                       .then_inc(S["lnT"], 1)

            def b_in(w, j):
                act.wait_ge(fill_sem(w, ("b_in", j)), fill_count(w, ("b_in", j)))
                t = slot(w, ("b_in", j))
                if j == 0:
                    for c in range(3):
                        m = act.activation(xpad[:, c, :, KC - 1:], t[:, c, 0:TB].rearrange("p (s t) -> p s t", s=GS),
                                           ACT.Copy)
                    m.then_inc(S["xpad"], 1)
                    return
                act.activation(sz, t[:, :, 0:TB], ACT.Silu).then_inc(S["sz"], 1)
                for c in range(3):
                    act.wait_ge(S["conv"], upto("conv", w.b, 10 + c))
                    act.activation(cv[:, c], cv[:, c], ACT.Silu).then_inc(S["conv_act"], 1)

            def b_q(w, _):
                act.wait_ge(fill_sem(w, ("b_q", 0)), fill_count(w, ("b_q", 0)))
                t = slot(w, ("b_q", 0))
                act.activation(b_qT, t[0:HC, 0:2, 0:TB], ACT.Copy)\
                   .then_inc(S["b_qT"], 1)

            def b_v(w, _):
                act.wait_ge(fill_sem(w, ("b_v", 0)), fill_count(w, ("b_v", 0)))
                t = slot(w, ("b_v", 0))
                for n in range(2):
                    pairs = b_vB[:, 2 * n:2 * n + 2].rearrange("p s (j two) (half d) -> p (s j) (two half) d",
                                                               two=2, half=2)
                    m = act.activation(pairs[:, :, 0:4:3, :],
                                       t[0:N, n, 0:2 * D].rearrange("p (n two d) -> p n two d", two=2, d=HD), ACT.Copy)
                m.then_inc(S["b_vB"], 1)

            def numerators(w, stage, s, head):
                act.wait_ge(S[stage + "_sub"], upto(stage + "_sub", w.b, s + 1))
                act.activation(pr[:, s % 2, :], pr[:, s % 2, :], ACT.Exp, scale=head ** -0.5)\
                   .then_inc(S[stage + "_exp"], 1)

            def turned(w, stage, s):
                act.wait_ge(fill_sem(w, (stage + "_pt", s)), fill_count(w, (stage + "_pt", s)))
                t = slot(w, (stage + "_pt", s))
                act.activation(pT[:, :, :].rearrange("p (b h) t -> p b (h t)", b=3), t[0:N, :, 0:4 * N], ACT.Copy)\
                   .then_inc(S[stage + "_pT"], 1)

            def b_o(w, s):
                act.wait_ge(fill_sem(w, ("b_o", s)), fill_count(w, ("b_o", s)))
                t = slot(w, ("b_o", s))
                act.activation(bT[0:HC, :, s * N:(s + 1) * N], t[0:HC, 0:2 * N].rearrange("p (c t) -> p c t", c=2),
                               ACT.Copy).then_inc(S["b_oT"], 1)

            def b_f1(w, j):
                act.wait_ge(fill_sem(w, ("b_f1", j)), fill_count(w, ("b_f1", j)))
                t = slot(w, ("b_f1", j))
                act.activation(b_h[:, 3 * j:3 * j + 3, :], t[:, :, 0:TB], ACT.Gelu)\
                   .then_inc(S["b_h"], 1)

            def c_g(w, _):
                act.wait_ge(S["g_step"], upto("g_step", w.b, 4))
                act.activation(gsm[:, 1], gsm[:, 1], ACT.Exp).then_inc(S["g_exp"], 1)

            def c_qk(w, tile):
                act.wait_ge(fill_sem(w, ("c_qk", tile)), fill_count(w, ("c_qk", tile)))
                t = slot(w, ("c_qk", tile))
                if tile > 0:
                    act.wait_ge(S["ss"], upto("ss", w.b, tile))
                act.activation(sq.rearrange("p (b n) -> p b n", b=3), t[:, :, :], ACT.Square).then_inc(S["sq"], 1)
                if tile == 2:
                    act.wait_ge(fill_sem(w, ("c_qt", 0)), fill_count(w, ("c_qt", 0)))
                act.activation(qkn[tile % 2].rearrange("p (b n) -> p b n", b=3), t[:, :, :], ACT.Copy)\
                   .then_inc(S["qk_raw"], 1)

            def c_qt(w, tile):
                act.wait_ge(fill_sem(w, ("c_qt", tile)), fill_count(w, ("c_qt", tile)))
                t = slot(w, ("c_qt", tile))
                tv = t[:, :, :].rearrange("p b (n t) -> p (b n) t", t=128)
                cols = slice(tile * 128, (tile + 1) * 128)
                act.activation(c_qT[:, :, cols], tv[:, 0:6, :], ACT.Identity, scale=col128("q_w"), bias=col128("q_b"))
                for par in range(2):
                    r = slice(64 * par, 64 * par + 64)
                    m = act.activation(c_kB[r, :, par, cols], tv[r, 6:12, :], ACT.Identity, scale=col128("k_w")[r, :],
                                       bias=col128("k_b")[r, :])
                m.then_inc(S["c_qkT"], 1)

            def c_v_(w, s):
                act.wait_ge(fill_sem(w, ("c_v", s)), fill_count(w, ("c_v", s)))
                t = slot(w, ("c_v", s))
                if s >= 2:
                    act.wait_ge(S["c_oT"], upto("c_oT", w.b, s - 1))
                half = NH * HD2 // 2
                act.activation(c_v[:, s % 2, :, :].rearrange("p (b h) d -> p b h d", b=2),
                               t[0:N, :, 0:half].rearrange("p b (h d) -> p b h d", d=HD2), ACT.Copy)\
                   .then_inc(S["c_v"], 1)

            def c_o(w, s):
                act.wait_ge(fill_sem(w, ("c_o", s)), fill_count(w, ("c_o", s)))
                t = slot(w, ("c_o", s))
                act.activation(c_oT[:, :, s * N:(s + 1) * N].rearrange("p (b n) t -> p b n t", b=2),
                               t[:, :, 0:3 * N].rearrange("p b (n t) -> p b n t", t=N), ACT.Copy)\
                   .then_inc(S["c_oT"], 1)

            sections(act, {"a_f1": a_f1, "a_qk": a_qk, "a_v": a_v, "a_e": a_e, "a_pt": a_pt,
                           "a_ot": a_ot, "b_ht": b_ht, "b_u": b_u, "b_in": b_in, "b_q": b_q,
                           "b_v": b_v, "b_e": lambda w, s: numerators(w, "b", s, HD),
                           "b_pt": lambda w, s: turned(w, "b", s), "b_o": b_o, "b_f1": b_f1,
                           "c_qk": c_qk, "c_qt": c_qt, "c_v": c_v_, "c_g": c_g,
                           "c_e": lambda w, s: numerators(w, "c", s, HD2), "c_pt": lambda w, s: turned(w, "c", s),
                           "c_o": c_o})

        @block.vector
        def _(dve):
            for t in (x0T, x1T, x2T, a_oT, bT):
                dve.memset(t[HC:HC + 1, 0, :], 1.0)
            dve.memset(a_vB[:, :, :, :], 0.0)
            dve.memset(b_vB[:, :, :, :], 0.0)
            dve.memset(c_kB[:, :, :, :], 0.0).then_inc(s_set, 1)
            dve.wait_ge(s_set, 1)
            for odd in range(2):
                c = odd * (HD + 1) + HD
                m = dve.memset(a_vB[64 * odd:64 * odd + 64, :, :, c:c + 1], 1.0)
            m.then_inc(s_set, 1)
            dve.wait_ge(loads["vec"], 16 * n_loads["vec"])
            for c in range(2):
                dve.tensor_scalar(w_pe[:, c, :], w_pe[:, c, :], col96("tok_b", c), None, ALU.add).then_inc(s_set, 1)
            dve.wait_ge(s_set, 4)

            def inverse_root(tile, n, name, group, done, starts):
                x, y, t = (tile[:, r, 0:n] for r in range(3))
                count = [done]

                def ordered(ins):
                    ins.then_inc(S[name], 1)
                    count[0] += 1
                    dve.wait_ge(S[name], upto(name, group, count[0]))

                for start in starts:
                    ordered(start())
                ordered(dve.tensor_scalar(y.bitcast(I32), x.bitcast(I32), 1, None, ALU.logical_shift_right))
                ordered(dve.tensor_scalar(y.bitcast(I32), y.bitcast(I32), -1.0, float(ROOT_SEED), ALU.mult, ALU.add))
                for _ in range(ROOT_ROUNDS):
                    ordered(dve.tensor_tensor(t, y, y, ALU.mult))
                    ordered(dve.scalar_tensor_tensor(out=t, in0=t, scalar=-0.5, in1=x, op0=ALU.mult, op1=ALU.mult))
                    ordered(dve.scalar_tensor_tensor(out=y, in0=t, scalar=1.5, in1=y, op0=ALU.add, op1=ALU.mult))

            def a_en(w, _):
                dve.wait_ge(fill_sem(w, ("a_em", 0)), fill_count(w, ("a_em", 0)))
                t = slot(w, ("a_em", 0))
                pb = w_patch_b[:, :].unsqueeze(1).to_broadcast([128, TILES_A, D])
                dve.tensor_tensor(a_emb[:, :, :], t[:, 0:TILES_A * D].rearrange("p (n d) -> p n d", n=TILES_A), pb,
                                  ALU.add)\
                   .then_inc(S["a_emb"], 1)
                dve.wait_ge(S["a_emb"], upto("a_emb", w.a))
                for n in range(TILES_A):
                    dve.bn_stats(a_bn[:, n, :], a_emb[:, n, :]).then_inc(S["a_stats"], 1)
                dve.wait_ge(S["a_stats"], upto("a_stats", w.a))
                dve.tensor_copy(seen[:, 0:TILES_A], a_bn[:, :, 0])
                for n in range(TILES_A):
                    dve.bn_aggr(a_mv[:, n, :], a_bn[:, n, :]).then_inc(S["a_mv"], 1)
                dve.wait_ge(S["a_mv"], upto("a_mv", w.a))
                inverse_root(a_root, TILES_A, "a_root", w.a, 0, [
                    lambda: dve.tensor_scalar(a_root[:, 0, :], a_mv[:, :, 1], EPS, None, ALU.add)])
                for n in range(TILES_A):
                    dve.tensor_scalar(a_emb[:, n, :], a_emb[:, n, :], a_mv[:, n, 0:1], a_root[:, 1, n:n + 1],
                                      ALU.subtract, ALU.mult).then_inc(S["a_xn"], 1)

            def a_x0(w, _):
                dve.wait_ge(fill_sem(w, ("a_x0", 0)), fill_count(w, ("a_x0", 0)))
                t = slot(w, ("a_x0", 0)).rearrange("p (c s t) -> p c s t", c=2, s=GS)
                for c in range(2):
                    pe_c = w_pe[:, c, :].unsqueeze(1).to_broadcast([HC, GS, NI])
                    m = dve.scalar_tensor_tensor(out=x0T[0:HC, c, :].rearrange("p (s t) -> p s t", s=GS),
                                                 in0=t[0:HC, c], scalar=col96("tok_g", c), in1=pe_c, op0=ALU.mult,
                                                 op1=ALU.add).then_inc(S["x0T"], 1)

            def a_f2(w, j):
                dve.wait_ge(fill_sem(w, ("a_f2", j)), fill_count(w, ("a_f2", j)))
                t = slot(w, ("a_f2", j)).rearrange("p (c t) -> p c t", c=2)
                for c in range(2):
                    if j == 0:
                        m = dve.tensor_scalar(x1T[0:HC, c, :], t[0:HC, c, :], col96("tok_ff2_b", c), None, ALU.add)\
                           .then_inc(S["x1T"], 1)
                    else:
                        m = dve.scalar_tensor_tensor(
                            out=hT[:, c, :, 0:NI], in0=t[0:HC, c, :].rearrange("p (s t) -> p s t", s=GS),
                            scalar=col96("tok_ff2_b", c), in1=x2T[0:HC, c, :].rearrange("p (s t) -> p s t", s=GS),
                            op0=ALU.add, op1=ALU.add).then_inc(S["hT"], 1)

            def a_s(w, t2):
                dve.wait_ge(fill_sem(w, ("a_s", t2)), fill_count(w, ("a_s", t2)))
                t = slot(w, ("a_s", t2))[:, 0:2, 0:6 * NI].rearrange("p b (h k) -> p b h k", k=NI)
                dve.tensor_reduce(a_max[:, t2, :].rearrange("p (b h) -> p b h", b=2), t, AX.X, ALU.max)\
                   .then_inc(S["a_max"], 1)
                dve.wait_ge(S["a_max"], upto("a_max", w.a, t2 + 1))
                mb = a_max[:, t2, :].rearrange("p (b h) -> p b h", b=2).unsqueeze(3).to_broadcast([128, 2, 6, NI])
                dve.tensor_tensor(a_p[:, t2, :].rearrange("p (b h k) -> p b h k", b=2, k=NI), t, mb, ALU.subtract)\
                   .then_inc(S["a_sub"], 1)

            def a_o(w, t2):
                dve.wait_ge(fill_sem(w, ("a_o", t2)), fill_count(w, ("a_o", t2)))
                t = slot(w, ("a_o", t2))[:, 0:NH * (HD + 1)].rearrange("p (h d) -> p h d", h=NH)
                dve.reciprocal(a_rec[:, t2, :], t[:, :, HD]).then_inc(S["a_rec"], 1)
                dve.wait_ge(S["a_rec"], upto("a_rec", w.a, t2 + 1))
                dve.tensor_tensor(a_on[:, :].rearrange("p (h d) -> p h d", h=NH), t[:, :, 0:HD],
                                  a_rec[:, t2, :].unsqueeze(2).to_broadcast([128, NH, HD]), ALU.mult)\
                   .then_inc(S["a_on"], 1)

            def a_pr(w, _):
                dve.wait_ge(fill_sem(w, ("a_pr", 0)), fill_count(w, ("a_pr", 0)))
                t = slot(w, ("a_pr", 0)).rearrange("p (c t) -> p c t", c=2)
                dve.tensor_tensor(x2T[0:HC, :, :], t[0:HC, :, :], x0T[0:HC, :, :], ALU.add)\
                   .then_inc(S["x2T"], 1)

            def moments(w, n, src):
                for tile in range(TILES_B):
                    dve.bn_stats(bn[:, tile, :], src[:, tile, :]).then_inc(S["ln_stats"], 1)
                dve.wait_ge(S["ln_stats"], upto("ln_stats", w.b, 3 * n + TILES_B))
                dve.tensor_copy(seen[:, TILES_A:TILES_A + TILES_B], bn[:, :, 0])
                for tile in range(TILES_B):
                    dve.bn_aggr(mv[:, tile, :], bn[:, tile, :]).then_inc(S["ln_mv"], 1)
                dve.wait_ge(S["ln_mv"], upto("ln_mv", w.b, 3 * n + 3))

            def deviations(w, n):
                one = lambda: dve.tensor_scalar(root[:, 0, 0:TILES_B], mv[:, :, 1], EPS, None, ALU.add)
                both = lambda: dve.tensor_scalar(root[:, 0, TILES_B:2 * TILES_B], mv[:, :, 1], 1.0 + EPS, EPS * EPS,
                                                 ALU.mult, ALU.add)
                inverse_root(root, TILES_B * (1 if n else 2), "ln_root", w.b, n * ROOT_STEPS + (1 if n else 0),
                             [one] if n else [one, both])

            def normalise(w, n, src, scale):
                for tile in range(TILES_B):
                    dve.tensor_scalar(u[:, tile, :], src[:, tile, :], mv[:, tile, 0:1], scale[:, tile:tile + 1],
                                      ALU.subtract, ALU.mult).then_inc(S["ln_u"], 1)

            def b_ht(w, _):
                dve.wait_ge(S["h_tm"], upto("h_tm", w.b))
                moments(w, 0, h_tm)
                deviations(w, 0)
                dve.wait_ge(S["out_dma"], upto("out_dma", w.b))
                normalise(w, 0, h_tm, root[:, 1, TILES_B:2 * TILES_B])
                for tile in range(TILES_B):
                    dve.tensor_scalar(xr[:, tile, :], h_tm[:, tile, :], mv[:, tile, 0:1], root[:, 1, tile:tile + 1],
                                      ALU.subtract, ALU.mult).then_inc(S["y_tm"], 1)

            def b_u(w, n):
                dve.wait_ge(fill_sem(w, ("b_u", n)), fill_count(w, ("b_u", n)))
                t = slot(w, ("b_u", n))
                if n < 3:
                    dve.tensor_scalar(bT[0:HC, 1, :], t[0:HC, 1, 0:TB], col96(f"ln{n + 1}_g", 1),
                                      col96(f"ln{n + 1}_b", 1), ALU.mult, ALU.add)\
                       .then_inc(S["lnT"], 1)
                else:
                    dve.tensor_copy(bT[0:HC, 1, :], t[0:HC, 1, 0:TB])\
                       .then_inc(S["lnT"], 1)

            def b_in(w, j):
                if j == 0:
                    dve.wait_ge(fill_sem(w, ("b_in", 0)), fill_count(w, ("b_in", 0)))
                    dve.memset(xpad[:, :, :, 0:KC - 1], 0.0).then_inc(S["pad"], 1)
                    return
                dve.wait_ge(S["xpad"], upto("xpad", w.b))
                dve.wait_ge(S["pad"], upto("pad", w.b))
                for n in range(KC):
                    tap = KC - 1 - n
                    for c in range(3):
                        src = xpad[:, c, :, tap:tap + N]
                        if n == 0:
                            m = dve.tensor_scalar(cv[:, c], src, col128("conv_w", c * KC + tap), col128("conv_b", c),
                                                  ALU.mult, ALU.add)
                        else:
                            dve.wait_ge(S["conv"], upto("conv", w.b, 3 * (n - 1) + c + 1))
                            m = dve.scalar_tensor_tensor(out=cv[:, c], in0=src, scalar=col128("conv_w", c * KC + tap),
                                                         in1=cv[:, c], op0=ALU.mult, op1=ALU.add)
                        m.then_inc(S["conv"], 1)
                dve.wait_ge(S["sz"], upto("sz", w.b))
                for c in range(3):
                    dve.wait_ge(S["conv_act"], upto("conv_act", w.b, c + 1))
                    dve.tensor_tensor(cv[:, c], cv[:, c], sz[:, c, :].rearrange("p (s t) -> p s t", s=GS), ALU.mult)\
                       .then_inc(S["gate"], 1)

            def residual(w, unit, name, out_t, in_t):
                dve.wait_ge(fill_sem(w, unit), fill_count(w, unit))
                t = slot(w, unit)
                dve.tensor_tensor(out_t[:, :, :], t[:, :, 0:D], in_t[:, :, :], ALU.add)\
                   .then_inc(S[name], 1)
                dve.wait_ge(S[name], upto(name, w.b))

            def b_out(w, _):
                dve.wait_ge(S["y_tm"], upto("y_tm", w.b))
                residual(w, ("b_out", 0), "x1_tm", xr, xr)
                moments(w, 1, xr)
                deviations(w, 1)
                normalise(w, 1, xr, root[:, 1, 0:TILES_B])

            def b_k(w, _):
                dve.wait_ge(fill_sem(w, ("b_k", 0)), fill_count(w, ("b_k", 0)))
                t = slot(w, ("b_k", 0))
                dve.tensor_copy(b_kT, t[0:HC, 0:2, 0:TB])\
                   .then_inc(S["b_kT"], 1)

            def less_max(w, stage, s):
                dve.wait_ge(fill_sem(w, (stage + "_s", s)), fill_count(w, (stage + "_s", s)))
                t = slot(w, (stage + "_s", s))[0:N, :, 0:4 * N].rearrange("p b (h k) -> p b h k", k=N)
                mx = smax[:, s % 2, :].rearrange("p (b h) -> p b h", b=3)
                dve.tensor_reduce(mx, t, AX.X, ALU.max).then_inc(S[stage + "_max"], 1)
                dve.wait_ge(S[stage + "_max"], upto(stage + "_max", w.b, s + 1))
                dve.tensor_tensor(pr[:, s % 2, :].rearrange("p (b h k) -> p b h k", b=3, k=N), t,
                                  mx.unsqueeze(3).to_broadcast([N, 3, 4, N]), ALU.subtract)\
                   .then_inc(S[stage + "_sub"], 1)

            def weights(w, stage, s):
                e = pr[:, s % 2, :].rearrange("p (h k) -> p h k", k=N)
                dve.wait_ge(S[stage + "_exp"], upto(stage + "_exp", w.b, s + 1))
                dve.tensor_reduce(psum[:, s % 2, :], e, AX.X, ALU.add).then_inc(S[stage + "_sum"], 1)
                dve.wait_ge(S[stage + "_sum"], upto(stage + "_sum", w.b, s + 1))
                dve.reciprocal(rec[:, s % 2, :], psum[:, s % 2, :]).then_inc(S[stage + "_rec"], 1)
                dve.wait_ge(S[stage + "_rec"], upto(stage + "_rec", w.b, s + 1))
                factor = rec
                if stage == "c":
                    dve.wait_ge(S["gates"], upto("gates", w.b))
                    dve.tensor_tensor(gr[:, s % 2, :], rec[:, s % 2, :], gates[:, s, :], ALU.mult)\
                       .then_inc(S["c_gr"], 1)
                    dve.wait_ge(S["c_gr"], upto("c_gr", w.b, s + 1))
                    factor = gr
                dve.tensor_tensor(e, e, factor[:, s % 2, :].unsqueeze(2).to_broadcast([N, NH, N]), ALU.mult)\
                   .then_inc(S[stage + "_w"], 1)

            def b_pr(w, _):
                residual(w, ("b_pr", 0), "x2_tm", xr, xr)
                moments(w, 2, xr)
                deviations(w, 2)
                normalise(w, 2, xr, root[:, 1, 0:TILES_B])

            def b_f2(w, _):
                dve.wait_ge(S["hx"], upto("hx", w.b))
                residual(w, ("b_f2", 0), "h2_tm", hx, hx)
                moments(w, 3, hx)
                deviations(w, 3)
                normalise(w, 3, hx, root[:, 1, 0:TILES_B])

            def c_g(w, _):
                dve.wait_ge(fill_sem(w, ("c_g", 0)), fill_count(w, ("c_g", 0)))
                t = slot(w, ("c_g", 0))[0:N, 0:GS * (EXPERTS + 4)].rearrange("p (s k) -> p s k", s=GS)
                step = [0]

                def ordered(ins):
                    ins.then_inc(S["g_step"], 1)
                    step[0] += 1
                    dve.wait_ge(S["g_step"], upto("g_step", w.b, step[0]))

                def rows(n, lo, hi):
                    return gsm[:, n, :, lo:hi]

                def spread(ap, k):
                    return ap.to_broadcast([N, GS, k])

                pairs = lambda n, at: gsm[:, n, :, at:at + 4].rearrange("p s (a b) -> p s a b", b=2)
                E_ = EXPERTS
                mx = rows(0, 0, 1)
                mx2 = gsm[:, 0, :, 1:3]
                ordered(dve.tensor_reduce(gsm[:, 0, :, 0], t[:, :, 0:E_], AX.X, ALU.max))
                ordered(dve.tensor_reduce(mx2, t[:, :, E_:E_ + 4].rearrange("p s (a b) -> p s a b", b=2), AX.X, ALU.max))
                ordered(dve.tensor_tensor(rows(1, 0, E_), t[:, :, 0:E_], spread(mx, E_), ALU.subtract))
                m = dve.tensor_tensor(pairs(1, E_), t[:, :, E_:E_ + 4].rearrange("p s (a b) -> p s a b", b=2),
                                      mx2.unsqueeze(3).to_broadcast([N, GS, 2, 2]), ALU.subtract)
                ordered(m)
                dve.wait_ge(S["g_exp"], upto("g_exp", w.b))
                e = rows(1, 0, E_)
                prio_b = w_prio[:, :].unsqueeze(1).to_broadcast([N, GS, E_])

                def first_of_largest(values, n):
                    top = gsm[:, n, :, 0:1]
                    ordered(dve.tensor_reduce(gsm[:, n, :, 0], values, AX.X, ALU.max))
                    ordered(dve.tensor_tensor(rows(n + 1, 0, E_), values, spread(top, E_), ALU.is_equal))
                    ordered(dve.tensor_tensor(rows(n + 1, 0, E_), rows(n + 1, 0, E_), prio_b, ALU.mult))
                    ordered(dve.tensor_reduce(gsm[:, n, :, 1], rows(n + 1, 0, E_), AX.X, ALU.max))
                    ordered(dve.tensor_tensor(rows(n + 2, 0, E_), rows(n + 1, 0, E_), spread(gsm[:, n, :, 1:2], E_),
                                              ALU.is_equal))

                first_of_largest(e, 2)
                ordered(dve.scalar_tensor_tensor(out=rows(5, 0, E_), in0=rows(4, 0, E_), scalar=-2.0, in1=e,
                                                 op0=ALU.mult, op1=ALU.add))
                first_of_largest(rows(5, 0, E_), 6)
                ordered(dve.tensor_tensor(rows(9, 0, E_), rows(4, 0, E_), rows(8, 0, E_), ALU.add))
                ordered(dve.tensor_tensor(rows(9, 0, E_), rows(9, 0, E_), e, ALU.mult))
                ordered(dve.tensor_reduce(gsm[:, 10, :, 0], rows(9, 0, E_), AX.X, ALU.add))
                ordered(dve.tensor_reduce(gsm[:, 10, :, 1:3], pairs(1, E_), AX.X, ALU.add))
                ordered(dve.reciprocal(gsm[:, 11, :, 0:3], gsm[:, 10, :, 0:3]))
                ordered(dve.tensor_tensor(gsm[:, 10, :, 4:6], rows(1, E_, E_ + 2), spread(gsm[:, 11, :, 1:2], 2),
                                          ALU.mult))
                ordered(dve.scalar_tensor_tensor(out=gsm[:, 10, :, 6], in0=gsm[:, 10, :, 4], scalar=4.0,
                                                 in1=gsm[:, 11, :, 2], op0=ALU.mult, op1=ALU.mult))
                ordered(dve.scalar_tensor_tensor(out=gsm[:, 10, :, 7], in0=gsm[:, 10, :, 5], scalar=4.0,
                                                 in1=gsm[:, 11, :, 0], op0=ALU.mult, op1=ALU.mult))
                dve.tensor_tensor(gates[:, :, 0:2], rows(1, E_ + 2, E_ + 4), spread(gsm[:, 10, :, 6:7], 2), ALU.mult)\
                   .then_inc(S["gates"], 1)
                dve.tensor_tensor(gates[:, :, 2:NH], rows(9, 0, E_), spread(gsm[:, 10, :, 7:8], E_), ALU.mult)\
                   .then_inc(S["gates"], 1)
                assert step[0] == PER_GROUP["g_step"], step[0]

            def c_qk(w, tile):
                dve.wait_ge(S["sq"], upto("sq", w.b, tile + 1))
                dve.tensor_reduce(ss[:, :], sq.rearrange("p (h d) -> p h d", d=HD2), AX.X, ALU.add)\
                   .then_inc(S["ss"], 1)
                dve.wait_ge(S["ss"], upto("ss", w.b, tile + 1))
                inverse_root(qk_root, 2 * NH, "qk_root", w.b, tile * ROOT_STEPS, [
                    lambda: dve.tensor_scalar(qk_root[:, 0, :], ss[:, :], 1.0 / HD2, EPS, ALU.mult, ALU.add)])
                dve.wait_ge(S["qk_raw"], upto("qk_raw", w.b, tile + 1))
                qk = qkn[tile % 2].rearrange("p (h d) -> p h d", d=HD2)
                dve.tensor_tensor(qk, qk, qk_root[:, 1, :].unsqueeze(2).to_broadcast([128, 2 * NH, HD2]), ALU.mult)\
                   .then_inc(S["qkn"], 1)

            def c_pr(w, _):
                dve.wait_ge(fill_sem(w, ("c_pr", 0)), fill_count(w, ("c_pr", 0)))
                t = slot(w, ("c_pr", 0))
                dve.wait_ge(S["h2b"], upto("h2b", w.b))
                dve.tensor_tensor(u[:, :, :], t[:, :, 0:D], h_tm[:, :, :], ALU.add)\
                   .then_inc(S["out_tm"], 1)

            def centre_weights():
                dve.wait_ge(loads["cqkv"], 16 * n_loads["cqkv"])
                for kc, k in ((0, HC + 1), (1, HC)):
                    wv = w_cqkv[0:k, kc, 0:qkw].rearrange("p (h d) -> p h d", d=HD2)
                    dve.tensor_reduce(w_mean[0:k, kc, :], wv, AX.X, ALU.add).then_inc(s_mean, 1)
                    dve.wait_ge(s_mean, kc + 1)
                    dve.scalar_tensor_tensor(out=wv, in0=w_mean[0:k, kc, :].unsqueeze(2).to_broadcast([k, 2 * NH, HD2]),
                                             scalar=-1.0 / HD2, in1=wv, op0=ALU.mult, op1=ALU.add)\
                       .then_inc(s_centred, 1)

            sections(dve, {"a_en": a_en, "a_x0": a_x0, "a_f2": a_f2, "a_s": a_s, "a_o": a_o,
                           "a_pr": a_pr, "b_ht": b_ht, "b_u": b_u, "b_in": b_in, "b_out": b_out, "b_k": b_k,
                           "b_s": lambda w, s: less_max(w, "b", s), "b_n": lambda w, s: weights(w, "b", s), "b_pr": b_pr, "b_f2": b_f2,
                           "c_g": c_g, "c_qk": c_qk, "c_s": lambda w, s: less_max(w, "c", s), "c_n": lambda w, s: weights(w, "c", s),
                           "c_pr": c_pr,
                           "a_f1": lambda w, j: centre_weights() if w.section == "first" and j == 1 else None})

        @block.gpsimd
        def _(pool):
            pool.wait_ge(loads["vec"], 16 * n_loads["vec"])

            def spread(out_ap, in_ap, k):
                return pool.tensor_tensor(out_ap, in_ap.unsqueeze(1).to_broadcast([HC, 6, k]),
                                          w_mask[:, :].unsqueeze(2).to_broadcast([HC, 6, k]), ALU.mult)

            def a_s(w, t2):
                if t2 == 1:
                    pool.wait_ge(fill_sem(w, ("a_s", 0)), fill_count(w, ("a_s", 0)))
                else:
                    pool.wait_ge(S["a_kT"], upto("a_kT", w.a))
                for c in range(2):
                    spread(a_kB[:, c], a_kT[:, c, t2 * 128:(t2 + 1) * 128], 128).then_inc(S["a_kB"], 1)

            def b_s(w, s):
                if s >= 2:
                    pool.wait_ge(fill_sem(w, ("b_s", s - 2)), fill_count(w, ("b_s", s - 2)))
                else:
                    pool.wait_ge(S["b_kT"], upto("b_kT", w.b))
                for c in range(2):
                    spread(b_kBv[:, s % 2, c], b_kT[:, c, s * N:(s + 1) * N], N).then_inc(S["b_kB"], 1)

            def b_pr(w, _):
                pool.wait_ge(S["x2_tm"], upto("x2_tm", w.b))
                bias = w_ff2_b[:, :].unsqueeze(1).to_broadcast([128, TILES_B, D])
                pool.tensor_tensor(hx[:, :, :], xr[:, :, :], h_tm[:, :, :], ALU.add).then_inc(S["hx"], 1)
                pool.wait_ge(S["hx"], upto("hx", w.b, 1))
                pool.tensor_tensor(hx[:, :, :], hx[:, :, :], bias, ALU.add).then_inc(S["hx"], 1)

            def b_f2(w, _):
                pool.wait_ge(S["h2_tm"], upto("h2_tm", w.b))
                bias = w_cproj_b[:, :].unsqueeze(1).to_broadcast([128, TILES_B, D])
                pool.tensor_tensor(h_tm[:, :, :], hx[:, :, :], bias, ALU.add).then_inc(S["h2b"], 1)

            sections(pool, {"a_s": a_s, "b_s": b_s, "b_pr": b_pr, "b_f2": b_f2})



def positions():
    pos = np.arange(NI, dtype=np.float32)[:, None]
    i = np.arange(D // 2, dtype=np.float32)[None, :]
    ang = pos / np.power(np.float32(10000.0), np.float32(2.0) * i / np.float32(D))
    pe = np.zeros((NI, D), np.float32)
    pe[:, 0::2] = np.sin(ang)
    pe[:, 1::2] = np.cos(ang)
    return pe


def chunked(a, rows):
    return np.ascontiguousarray(a.reshape(-1, rows, a.shape[-1]).transpose(1, 0, 2))


def with_bias(a, b):
    row = np.stack([b, np.zeros_like(b)])[None]
    return np.ascontiguousarray(np.concatenate([chunked(a, HC), row], axis=0))


def kernel(**inputs):
    import concourse.bacc as _bacc
    from concourse.bass_utils import run_bass_kernel_spmd as _run

    v = {k: np.asarray(a) for k, a in inputs.items()}
    tok, att, ffn = (lambda n: v["L0_tok_" + n]), (lambda n: v["L0_attn_" + n]), (lambda n: v["L0_ffn_" + n])
    per96 = lambda b: b.reshape(2, HC).T
    rows = lambda b: np.ascontiguousarray(np.broadcast_to(b, (128, D)))
    pix = v["x"].reshape(NG, GS, CH, IMG // P, P, IMG // P, P).transpose(0, 2, 4, 6, 1, 3, 5)
    arrays = {
        "xT": pix.reshape(NG, KP, 128, TA).transpose(0, 2, 1, 3),
        "txtT": v["txt"].reshape(NG, GS, NT, 2, HC).transpose(0, 4, 3, 1, 2),
        "patchT": chunked(tok("patch_w").reshape(D, -1).T, 128),
        "ident": np.eye(128, dtype=np.float32),
        "peT": positions().T.reshape(2, HC, NI).transpose(1, 0, 2),
        "mask": (np.arange(HC)[:, None] // HD == np.arange(6)[None]).astype(np.float32),
        "prio": np.broadcast_to(np.arange(EXPERTS, 0, -1).astype(np.float32), (N, EXPERTS)),
        "vec96": np.concatenate([per96(tok("ln_g")), per96(tok("ff2_b"))] +
                                [per96(att(f"ln{n}_{k}")) for n in (1, 2, 3) for k in "gb"] +
                                [per96(tok("ln_b"))], axis=1),
        "vec128": np.concatenate([att("conv_w").reshape(3, 128, KC).transpose(1, 0, 2).reshape(128, 3 * KC),
                                  att("conv_b").reshape(3, 128).T] +
                                 [np.concatenate([ffn(n), ffn(n)])[:, None] for n in
                                  ("q_norm_w", "q_norm_b", "k_norm_w", "k_norm_b")], axis=1),
        "patch_b": rows(tok("patch_b")),
        "tok_ff1": with_bias(tok("ff1_w"), tok("ff1_b")),
        "tok_ff2": chunked(tok("ff2_w"), 128),
        "tok_qkv": with_bias(tok("qkv_w"), tok("qkv_b")),
        "tok_proj": with_bias(tok("proj_w"), tok("proj_b")),
        "in_proj": chunked(att("in_proj_w"), HC),
        "out_proj": chunked(att("out_proj_w"), 128),
        "qkv": with_bias(att("qkv_w"), att("qkv_b")),
        "attn_proj": with_bias(att("attn_proj_w"), att("attn_proj_b")),
        "ffn1": with_bias(att("ffn1_w"), att("ffn1_b")),
        "ffn2": chunked(att("ffn2_w"), 128),
        "ffn2_b": rows(att("ffn2_b")),
        "cqkv": with_bias(ffn("qkv_w"), ffn("qkv_b")),
        "cproj": chunked(ffn("proj_w"), 128),
        "cproj_b": rows(ffn("proj_b")),
        "cgate": chunked(np.concatenate([ffn("wg_w"), ffn("wg0_w"), ffn("wg1_w")], axis=1), HC),
    }
    arrays = {k: np.ascontiguousarray(a) for k, a in arrays.items()}
    nc = _bacc.Bacc("TRN2", target_bir_lowering=False, num_devices=1)
    args = {k: nc.dram_tensor(f"in_{k}", a.shape, mybir.dt.from_np(a.dtype), kind="ExternalInput").ap()
            for k, a in arrays.items()}
    res = nc.dram_tensor("out", (B * N, D), F32, kind="ExternalOutput").ap()
    program(nc, **args, out=res.rearrange("(g t p) d -> g p t d", g=NG, p=128))
    r = _run(nc, [{f"in_{k}": a for k, a in arrays.items()}], core_ids=[0])
    return r.results[0]["out"].reshape(B, N, D)
```

```python
from contextlib import ExitStack

import numpy as np

import concourse.bass as bass
from concourse import mybir

F32 = mybir.dt.float32
ACT = mybir.ActivationFunctionType
ALU = mybir.AluOpType
AX = mybir.AxisListType
I32 = mybir.dt.int32

B, CH, IMG, P = 16, 3, 128, 16
D, F, NH = 192, 768, 12
NI, NT = (IMG // P) ** 2, 32
N = NI + NT
GS = 4
NG = B // GS
HC = 96
TA, TB = GS * NI, GS * N
HD, HD2 = D // NH, 64
DI, KC = 2 * D, 4
TILES_A, TILES_B = TA // 128, TB // 128
KP = CH * P * P // 128
EXPERTS = NH - 2
EPS = 1e-5
ROOT_SEED, ROOT_ROUNDS = 0x5F3759DF, 3
ROOT_STEPS = 3 + 3 * ROOT_ROUNDS

V96 = {"tok_g": 0, "tok_ff2_b": 2, "ln1_g": 4, "ln1_b": 6, "ln2_g": 8, "ln2_b": 10, "ln3_g": 12, "ln3_b": 14,
       "tok_b": 16, "n": 18}
V128 = {"conv_w": 0, "conv_b": 12, "q_w": 15, "q_b": 16, "k_w": 17, "k_b": 18, "n": 19}

STEPS_TEXT = {
    "first": """
    a_en a_em a_x0 a_f1.0 a_g1.0 a_f2.0 a_h2.0 a_qk warm.0 a_v a_s.0 a_s.1 a_e.0 a_pt.0 a_o.0 a_ot.0 a_e.1 a_pt.1
    a_o.1 a_ot.1 warm.1 a_pr a_f1.1=T1 a_g1.1 a_f2.1 a_h2.1
    """,
    "loop": """
    b_ht=T0 a_em b_u.0 a_en b_in.0 a_x0 b_in.1=T1 a_f1.0 a_g1.0 b_out.0 b_out.1 b_out.2 a_f2.0 a_h2.0 b_u.1 a_qk b_k
    b_q=T0 b_s.0 b_s.1 b_e.0 b_v b_e.1 b_n.0 a_v b_pt.0=T0 b_n.1 b_s.2 b_o.0 a_s.0 b_e.2 a_e.0 b_pt.1 b_n.2 b_s.3
    b_o.1 a_s.1 b_e.3 b_n.3 a_e.1 b_pt.2 a_pt.0 b_o.2 a_o.0 a_pt.1 b_pt.3 a_ot.0 b_pr.0 b_o.3 b_pr.1=T0 a_o.1 b_pr.2
    a_ot.1 warm.0 a_pr warm.1 b_u.2 b_f1.0 b_f1.1 b_f2.0 b_f2.1 b_f2.2 a_f1.1 b_u.3 a_g1.1 c_g c_qk.0=T0 c_qk.1=T1
    c_v.0 c_qt.0=T0 c_v.1 c_s.0=T0 c_e.0 c_n.0 c_qk.2=T1 c_qt.1 a_f2.1 c_pt.0 a_h2.1 c_s.1=T0 c_o.0 c_e.1 c_qt.2=T1
    c_n.1 c_v.2 c_s.2=T0 c_e.2 warm.2 c_n.2 c_pt.1=T1 c_s.3 c_o.1 c_n.3 c_e.3 c_pt.2 c_v.3 c_pr.0 c_o.2 c_pt.3
    c_pr.1 c_o.3 c_pr.2=T1
    """,
    "last": """
    b_ht=T0 warm.0 warm.1 warm.2 warm.3 b_u.0 warm.4 b_in.0 b_in.1 warm.5 warm.6 warm.7 b_out.0=T1 b_out.1 b_out.2
    warm.8 warm.9 warm.10 warm.11 warm.12 b_u.1 b_k b_q b_s.0 warm.13 b_s.1 b_e.0 b_v b_e.1 b_n.0 warm.14 warm.15
    warm.16 b_n.1 b_pt.0 b_s.2 b_o.0 b_n.2 b_e.2 b_pt.1 b_s.3 b_o.1 b_e.3 b_pt.2 b_n.3 b_o.2 b_pt.3 b_pr.0 b_o.3
    b_pr.1 b_pr.2 warm.17 warm.18 warm.19 warm.20 b_u.2 b_f1.0 b_f1.1 b_f2.0 b_f2.1 b_f2.2 warm.21 warm.22 warm.23
    warm.24 warm.25 b_u.3 warm.26 c_g c_qk.0=T0 c_qk.1=T1 c_v.0 c_qt.0=T0 c_v.1 c_s.0=T0 c_n.0 c_e.0 c_qk.2=T1
    c_qt.1=T0 c_pt.0=T1 c_s.1=T0 warm.27 c_o.0 c_e.1 c_qt.2=T1 c_v.2 warm.28 c_n.1 c_s.2=T0 c_n.2 c_pt.1=T1 c_e.2
    warm.29 c_s.3 c_o.1 c_e.3 c_n.3 c_pt.2 c_v.3 c_pr.0 c_o.2 c_pt.3 c_pr.1 c_o.3 c_pr.2=T1
    """,
}


def units(text):
    order, fixed = [], {}
    for word in text.split():
        word, _, slot = word.partition("=")
        name, _, k = word.partition(".")
        order.append((name, int(k or 0)))
        if slot:
            fixed[order[-1]] = slot
    return order, fixed


ORDER = {section: units(text)[0] for section, text in STEPS_TEXT.items()}
FIXED_SLOT = {section: units(text)[1] for section, text in STEPS_TEXT.items()}
LAST_FILL = ("c_pr", TILES_B - 1)
SLOT_OF = {"a_em": "S", "a_x0": "S", "a_f1": "T", "a_g1": "S", "a_f2": "S", "a_h2": "S", "a_qk": "D", "a_v": "S",
           "a_s": "D", "a_pt": "D",
           "a_o": "S", "a_ot": "S", "a_pr": "S", "b_ht": "T", "b_u": "T", "b_in": "T", "b_out": "T", "b_q": "T",
           "b_k": "T", "b_v": "T", "b_s": "T", "b_pt": "T", "b_o": "S", "b_pr": "T", "b_f1": "T",
           "b_f2": "T", "c_g": "S", "c_qk": "T", "c_qt": "T", "c_v": "D", "c_s": "T", "c_pt": "T", "c_o": "D",
           "c_pr": "T", "warm": "S"}
READ_BY = {
    "a_em": lambda k: [("a_emb", 1)], "a_x0": lambda k: [("x0T", 2)], "a_f1": lambda k: [("a_h", 3 * k + 2)],
    "a_g1": lambda k: [("a_h", 3 * k + 3)], "a_h2": lambda k: [("hT", 2) if k else ("x1T", 2)],
    "a_f2": lambda k: [("hT", 1) if k else ("x1T", 1)], "a_qk": lambda k: [("a_qT", 1), ("a_kT", 1)],
    "a_v": lambda k: [("a_vB", 1)], "a_s": lambda k: [("a_sub", k + 1)], "a_pt": lambda k: [("a_pT", k + 1)],
    "a_o": lambda k: [("a_on", k + 1)], "a_ot": lambda k: [("a_oT", k + 1)], "a_pr": lambda k: [("x2T", 1)],
    "b_ht": lambda k: [("h_tm", 1)], "b_u": lambda k: [("lnT", 2 * k + 2)],
    "b_in": lambda k: [("sz", 1) if k else ("xpad", 1)], "b_out": lambda k: [("x1_tm", k + 1)],
    "b_q": lambda k: [("b_qT", 1)], "b_k": lambda k: [("b_kT", 1)], "b_v": lambda k: [("b_vB", 1)],
    "b_s": lambda k: [("b_sub", k + 1)], "b_pt": lambda k: [("b_pT", k + 1)], "b_o": lambda k: [("b_oT", k + 1)],
    "b_pr": lambda k: [("x2_tm", k + 1)], "b_f1": lambda k: [("b_h", k + 1)],
    "b_f2": lambda k: [("h2_tm", k + 1)], "c_g": lambda k: [("g_step", 4)], "c_qk": lambda k: [("qk_raw", k + 1)],
    "c_qt": lambda k: [("c_qkT", k + 1)], "c_v": lambda k: [("c_v", k + 1)], "c_s": lambda k: [("c_sub", k + 1)],
    "c_pt": lambda k: [("c_pT", k + 1)], "c_o": lambda k: [("c_oT", k + 1)],
    "c_pr": lambda k: [("out_tm", k + 1)], "warm": lambda k: [],
}


class PsumFills:

    def __init__(self):
        self.at, self.start, self.per, self.last = {}, {}, {}, {}
        total = dict.fromkeys(("T0", "T1", "S0", "S1"), 0)
        for section in ("first", "loop", "last"):
            self.start[section] = dict(total)
            count = dict.fromkeys(total, 0)
            turn = {"T": 0, "S": 0}
            holder = {}
            for unit in ORDER[section]:
                if unit[0] not in SLOT_OF:
                    continue
                kind = SLOT_OF[unit[0]]
                slot = "S0" if kind == "D" else FIXED_SLOT[section].get(unit, kind + str(turn[kind] % 2))
                if kind != "D":
                    turn[kind] = int(slot[1]) + 1
                taken = ("S0", "S1") if kind == "D" else (slot,)
                before = sorted({holder[bank] for bank in taken if bank in holder})
                for bank in taken:
                    holder[bank] = unit
                count[slot] += 1
                self.at[section, unit] = (slot, before, count[slot])
            self.per[section] = count
            self.last[section] = sorted(set(holder.values()))
            for s in total:
                total[s] += count[s] * (NG - 1 if section == "loop" else 1)


FILLS = PsumFills()
assert FILLS.at["loop", ("b_ht", 0)][0] != FILLS.at["loop", LAST_FILL][0] != FILLS.at["last", ("b_ht", 0)][0]

PER_GROUP = {
    "x_in": 16, "txt_in": 16, "a_emb": 1, "a_stats": 2, "a_mv": 2, "a_root": ROOT_STEPS, "a_xn": 2, "x0T": 2,
    "a_h": 6, "x1T": 2, "a_qT": 1, "a_kT": 1, "a_kB": 4, "a_vB": 1, "a_max": 2, "a_sub": 2, "a_exp": 2, "a_pT": 2,
    "a_rec": 2, "a_on": 2, "a_oT": 2, "x2T": 1, "hT": 2,
    "h_tm": 1, "ln_stats": 12, "ln_mv": 12, "ln_root": 4 * ROOT_STEPS + 1, "ln_u": 12, "y_tm": 3, "lnT": 8,
    "xpad": 1, "sz": 1, "conv": 12, "conv_act": 3, "gate": 3, "x1_tm": 3, "b_qT": 1, "b_kT": 1, "b_kB": 8,
    "b_vB": 1, "b_max": 4, "b_sub": 4, "b_exp": 4, "b_pT": 4, "b_sum": 4, "b_rec": 4, "b_w": 4, "b_oT": 4, "x2_tm": 3,
    "hx": 2, "b_h": 2, "h2_tm": 3, "h2b": 1,
    "g_step": 23, "g_exp": 1, "gates": 2, "sq": 3, "qk_raw": 3, "ss": 3, "qk_root": 3 * ROOT_STEPS,
    "qkn": 3,
    "c_qkT": 3, "c_v": 4, "c_max": 4, "c_sub": 4, "c_exp": 4, "c_pT": 4, "c_sum": 4, "c_rec": 4, "c_gr": 4,
    "c_w": 4, "c_oT": 4, "out_tm": 3, "out_dma": 16, "pad": 1,
}


def program(nc, xT, txtT, patchT, ident, peT, mask, prio, vec96, vec128, patch_b, tok_ff1, tok_ff2, tok_qkv, tok_proj,
            in_proj, out_proj, qkv, attn_proj, ffn1, ffn2, ffn2_b, cqkv, cproj, cproj_b, cgate, out):
    ctx = ExitStack()
    with ctx:
        def sb(name, shape):
            return ctx.enter_context(nc.sbuf_tensor(name, shape, F32))

        def sem(name):
            return ctx.enter_context(nc.semaphore(name))

        w_patch = sb("w_patch", [128, KP, D])
        w_ident = sb("w_ident", [128, 128])
        w_pe = sb("w_pe", [HC, 2, NI])
        w_mask = sb("w_mask", [HC, 6])
        w_prio = sb("w_prio", [N, EXPERTS])
        v96 = sb("v96", [HC, V96["n"]])
        v128 = sb("v128", [128, V128["n"]])
        w_patch_b = sb("w_patch_b", [128, D])
        w_tff1 = sb("w_tff1", [HC + 1, 2, F])
        w_tff2 = sb("w_tff2", [128, F // 128, D])
        w_tqkv = sb("w_tqkv", [HC + 1, 2, 3 * D])
        w_tproj = sb("w_tproj", [HC + 1, 2, D])
        w_in = sb("w_in", [HC, 2, 2 * DI])
        w_out = sb("w_out", [128, DI // 128, D])
        w_qkv = sb("w_qkv", [HC + 1, 2, 3 * D])
        w_proj = sb("w_proj", [HC + 1, 2, D])
        w_ff1 = sb("w_ff1", [HC + 1, 2, F])
        w_ff2 = sb("w_ff2", [128, F // 128, D])
        w_ff2_b = sb("w_ff2_b", [128, D])
        w_cqkv = sb("w_cqkv", [HC + 1, 2, 3 * NH * HD2])
        w_cproj = sb("w_cproj", [128, NH * HD2 // 128, D])
        w_cproj_b = sb("w_cproj_b", [128, D])
        w_cgate = sb("w_cgate", [HC, 2, EXPERTS + 4])
        w_mean = sb("w_mean", [HC + 1, 2, 2 * NH])
        x_in = sb("x_in", [128, KP, TA])
        a_emb = sb("a_emb", [128, TILES_A, D])
        a_bn = sb("a_bn", [128, TILES_A, 6])
        a_mv = sb("a_mv", [128, TILES_A, 2])
        a_root = sb("a_root", [128, 3, TILES_A])
        x0T = sb("x0T", [HC + 1, 2, TA])
        x1T = sb("x1T", [HC + 1, 2, TA])
        x2T = sb("x2T", [HC + 1, 2, TA])
        a_wide = sb("a_wide", [128, F // 128 * TA])
        a_h = a_wide[:, :].rearrange("p (c t) -> p c t", t=TA)
        a_kB = a_wide[0:HC, :].rearrange("p (c h t) -> p c h t", c=2, h=6)
        a_qT = sb("a_qT", [HC, 2, TA])
        a_kT = sb("a_kT", [HC, 2, TA])
        a_vB = sb("a_vB", [128, GS, NH // 2, 2 * (HD + 1)])
        a_p = sb("a_p", [128, 2, NH * NI])
        a_pT = sb("a_pT", [128, NH // 2, 128])
        a_max = sb("a_max", [128, 2, NH])
        a_rec = sb("a_rec", [128, 2, NH])
        a_on = sb("a_on", [128, D])
        a_oT = sb("a_oT", [HC + 1, 2, TA])
        hT = sb("hT", [HC, 2, GS, N])
        h_tm = sb("h_tm", [128, TILES_B, D])
        xr = sb("xr", [128, TILES_B, D])
        hx = sb("hx", [128, TILES_B, D])
        u = sb("u", [128, TILES_B, D])
        bn = sb("bn", [128, TILES_B, 6])
        mv = sb("mv", [128, TILES_B, 2])
        seen = sb("seen", [128, TILES_A + TILES_B])
        root = sb("root", [128, 3, 2 * TILES_B])
        bT = sb("bT", [HC + 1, 2, TB])
        scratch = sb("scratch", [128, DI // 128 * GS * (N + KC - 1) + 2 * DI // 128 * TB])
        n0, n1 = DI // 128 * GS * (N + KC - 1), DI // 128 * TB
        xpad = scratch[:, 0:n0].rearrange("p (c s t) -> p c s t", c=DI // 128, s=GS)
        cv = scratch[:, n0:n0 + n1].rearrange("p (c s t) -> p c s t", c=DI // 128, s=GS)
        sz = scratch[:, n0 + n1:n0 + 2 * n1].rearrange("p (c t) -> p c t", c=DI // 128)
        qkw = 2 * NH * HD2
        sq = scratch[:, 0:qkw]
        qkn = (scratch[:, qkw:2 * qkw], x_in[:, :, :].rearrange("p j t -> p (j t)"))
        heads = sb("heads", [128, 4 * TB + GS * NH * 2 * HD])
        b_qT = heads[0:HC, 0:2 * TB].rearrange("p (c t) -> p c t", c=2)
        b_kT = heads[0:HC, 2 * TB:4 * TB].rearrange("p (c t) -> p c t", c=2)
        b_vB = heads[0:N, 4 * TB:].rearrange("p (s h d) -> p s h d", s=GS, h=NH)
        c_v = heads[0:N, 0:2 * NH * HD2].rearrange("p (b h d) -> p b h d", b=2, h=NH)
        b_kB = sb("b_kB", [128, 2 * 2 * 6 * N])
        b_kBv = b_kB[0:HC, :].rearrange("p (b c h t) -> p b c h t", b=2, c=2, h=6)
        c_oT = b_kB[:, :].rearrange("p (c t) -> p c t", c=NH * HD2 // 128)
        pr = sb("pr", [N, 2, NH * N])
        pT = sb("pT", [N, NH, N])
        smax = sb("smax", [N, 2, NH])
        psum = sb("psum", [N, 2, NH])
        rec = sb("rec", [N, 2, NH])
        gr = sb("gr", [N, 2, NH])
        b_wide = sb("b_wide", [128, F // 128 * TB])
        b_h = b_wide[:, :].rearrange("p (c t) -> p c t", t=TB)
        c_qT = b_h
        c_kB = sb("c_kB", [128, NH // 2, 2, TB])
        gsm = sb("gsm", [N, 12, GS, EXPERTS + 4])
        gates = sb("gates", [N, GS, NH])
        ss = sb("ss", [128, 2 * NH])
        qk_root = sb("qk_root", [128, 3, 2 * NH])

        ps = {"T0": ctx.enter_context(nc.psum_tensor("psT0", [128, 3, 512], F32)),
              "T1": ctx.enter_context(nc.psum_tensor("psT1", [128, 3, 512], F32))}
        psS = ctx.enter_context(nc.psum_tensor("psS", [128, 2, 512], F32))

        S = {name: sem(name) for name in PER_GROUP}
        filled = {s: sem("filled_" + s) for s in ("T0", "T1", "S0", "S1")}
        loads = {n: sem("load_" + n) for n in ("patch", "vec", "tff1", "tff2", "tqkv", "tproj", "in", "out", "qkv",
                                               "proj", "ff1", "ff2", "cqkv", "cproj", "ident")}
        n_loads = {"patch": 1, "vec": 8, "tff1": 1, "tff2": 1, "tqkv": 1, "tproj": 1, "in": 1, "out": 1, "qkv": 1,
                   "proj": 1, "ff1": 1, "ff2": 1, "cqkv": 1, "cproj": 2, "ident": 1}
        s_set = sem("constants_set")
        s_mean = sem("weight_mean")
        s_centred = sem("weight_centred")

        AHEAD = ("out_tm",)

        class Where:

            def __init__(self, section, step, group_a, group_b):
                self.section, self.step, self.a, self.b = section, step, group_a, group_b

        def upto(name, group, k=None):
            return (group + (name in AHEAD)) * PER_GROUP[name] + (PER_GROUP[name] if k is None else k)

        def slot(w, unit):
            s = FILLS.at[w.section, unit][0]
            if s[0] == "T":
                return ps[s]
            return psS[:, :, :] if SLOT_OF[unit[0]] == "D" else psS[:, int(s[1]), :]

        def reads(w, units):
            most = {}
            for unit in units:
                for name, k in READ_BY[unit[0]](unit[1]):
                    most[name] = (max(k, most[name][0]) if name in most else k, w.a if unit[0][0] == "a" else w.b)
            return [(S[name], upto(name, group, k)) for name, (k, group) in most.items()]

        def reads_before(w, unit):
            return reads(w, FILLS.at[w.section, unit][1])

        def fill_count(w, unit):
            s, _, n = FILLS.at[w.section, unit]
            return w.step * FILLS.per[w.section][s] + FILLS.start[w.section][s] + n

        def fill_sem(w, unit):
            return filled[FILLS.at[w.section, unit][0]]

        def sections(eng, steps, at_end=lambda w: None):
            for unit in ORDER["first"]:
                if unit[0] in steps:
                    steps[unit[0]](Where("first", 0, 0, None), unit[1])
            at_end(Where("first", 0, 0, None))
            with eng.Fori(0, NG - 1) as i:
                w = Where("loop", i, i + 1, i)
                for unit in ORDER["loop"]:
                    if unit[0] in steps:
                        steps[unit[0]](w, unit[1])
                at_end(w)
            for unit in ORDER["last"]:
                if unit[0] in steps:
                    steps[unit[0]](Where("last", 0, None, NG - 1), unit[1])

        def col96(name, c):
            return v96[:, V96[name] + c:V96[name] + c + 1]

        def col128(name, c=0):
            return v128[:, V128[name] + c:V128[name] + c + 1]

        block = ctx.enter_context(nc.Block())

        @block.sync
        def _(sp):
            sp.sem_inc(S["out_tm"], PER_GROUP["out_tm"])
            sp.dma_start(w_patch[:, :, :], patchT).then_inc(loads["patch"], 16)
            sp.dma_start(x_in[:, :, :], xT[0]).then_inc(S["x_in"], 16)
            for dst, src in ((v96, vec96), (v128, vec128), (w_pe, peT), (w_mask, mask), (w_prio, prio),
                             (w_patch_b, patch_b), (w_ff2_b, ffn2_b), (w_cproj_b, cproj_b)):
                sp.dma_start(dst[:], src).then_inc(loads["vec"], 16)
            sp.dma_start(w_ident[:, :], ident).then_inc(loads["ident"], 16)
            for name, dst, src in (("tff1", w_tff1, tok_ff1), ("tff2", w_tff2, tok_ff2), ("tqkv", w_tqkv, tok_qkv),
                                   ("tproj", w_tproj, tok_proj), ("in", w_in, in_proj), ("out", w_out, out_proj),
                                   ("qkv", w_qkv, qkv), ("proj", w_proj, attn_proj), ("ff1", w_ff1, ffn1),
                                   ("ff2", w_ff2, ffn2)):
                sp.dma_start(dst[:], src).then_inc(loads[name], 16)
            sp.dma_start(hT[:, :, :, NI:N], txtT[0]).then_inc(S["txt_in"], 16)
            sp.dma_start(w_cproj[:, :, :], cproj).then_inc(loads["cproj"], 16)
            sp.dma_start(w_cgate[:, :, :], cgate).then_inc(loads["cproj"], 16)
            sp.dma_start(w_cqkv[:, :, :], cqkv).then_inc(loads["cqkv"], 16)

            def c_pr(w, tile):
                if tile == TILES_B - 1:
                    sp.wait_ge(S["out_tm"], upto("out_tm", w.b))
                    sp.dma_start(out[w.b], hx[:, :, :]).then_inc(S["out_dma"], 16)

            sp.sem_inc(S["out_dma"], 16)
            sections(sp, {"c_pr": c_pr})
            sp.wait_ge(S["out_dma"], 16 * (NG + 1))

        @block.tensor
        def _(pe):
            def chunks(out_ap, lhs, rhs, last, bias_row=True):
                k = HC + 1 if bias_row else HC
                pe.matmul(out_ap, lhs(0, k), rhs(0, k), start=True, stop=False)
                m = pe.matmul(out_ap, lhs(1, HC), rhs(1, HC), start=False, stop=True)
                if last is not None:
                    m.then_inc(last, 1)

            def all_read(w):
                for sem_read, value in reads(w, [unit for unit in FILLS.last[w.section] if unit != LAST_FILL]):
                    pe.wait_ge(sem_read, value)

            def a_em(w, _):
                for sem_read, value in reads_before(w, ("a_em", 0)):
                    pe.wait_ge(sem_read, value)
                t = slot(w, ("a_em", 0))
                if w.section == "first":
                    pe.wait_ge(loads["patch"], 16 * n_loads["patch"])
                pe.wait_ge(S["x_in"], upto("x_in", w.a))
                for tile in range(TILES_A):
                    for j in range(KP):
                        m = pe.matmul(t[:, tile * D:(tile + 1) * D], x_in[:, j, tile * 128:(tile + 1) * 128],
                                      w_patch[:, j, :], start=(j == 0), stop=(j == KP - 1))
                m.then_inc(fill_sem(w, ("a_em", 0)), 1)

            def a_x0(w, _):
                for sem_read, value in reads_before(w, ("a_x0", 0)):
                    pe.wait_ge(sem_read, value)
                t = slot(w, ("a_x0", 0)).rearrange("p (c t) -> p c t", c=2)
                if w.section == "first":
                    pe.wait_ge(loads["ident"], 16 * n_loads["ident"])
                pe.wait_ge(S["a_xn"], upto("a_xn", w.a))
                for tile in range(TILES_A):
                    for c in range(2):
                        m = pe.transpose(t[0:HC, c, tile * 128:(tile + 1) * 128],
                                         a_emb[:, tile, c * HC:(c + 1) * HC], w_ident[:, :])
                m.then_inc(fill_sem(w, ("a_x0", 0)), 1)

            def a_f1(w, j):
                for sem_read, value in reads_before(w, ("a_f1", j)):
                    pe.wait_ge(sem_read, value)
                t = slot(w, ("a_f1", j))
                if w.section == "first" and j == 0:
                    pe.wait_ge(loads["tff1"], 16 * n_loads["tff1"])
                    pe.wait_ge(s_set, 1)
                src = x0T if j == 0 else x2T
                pe.wait_ge(S["x0T" if j == 0 else "x2T"], upto("x0T" if j == 0 else "x2T", w.a))
                for c in range(4):
                    o = t[:, c // 2, (c % 2) * TA:(c % 2 + 1) * TA]
                    chunks(o, lambda kc, k: w_tff1[0:k, kc, c * 128:(c + 1) * 128], lambda kc, k: src[0:k, kc, :],
                           fill_sem(w, ("a_f1", j)) if c == 3 else None)

            def a_g1(w, j):
                for sem_read, value in reads_before(w, ("a_g1", j)):
                    pe.wait_ge(sem_read, value)
                t = slot(w, ("a_g1", j))
                src = x0T if j == 0 else x2T
                for c in range(4, F // 128):
                    chunks(t[:, (c - 4) * TA:(c - 3) * TA], lambda kc, k: w_tff1[0:k, kc, c * 128:(c + 1) * 128],
                           lambda kc, k: src[0:k, kc, :], fill_sem(w, ("a_g1", j)) if c == F // 128 - 1 else None)

            def a_f2(w, j):
                for sem_read, value in reads_before(w, ("a_f2", j)):
                    pe.wait_ge(sem_read, value)
                t = slot(w, ("a_f2", j))
                if w.section == "first" and j == 0:
                    pe.wait_ge(loads["tff2"], 16 * n_loads["tff2"])
                for kc in range(F // 128):
                    if kc % 2 == 0:
                        pe.wait_ge(S["a_h"], upto("a_h", w.a, 3 * j + kc // 2 + 1))
                    m = pe.matmul(t[0:HC, 0:TA], w_tff2[:, kc, 0:HC], a_h[:, kc, :], start=(kc == 0),
                                  stop=(kc == F // 128 - 1))
                m.then_inc(fill_sem(w, ("a_f2", j)), 1)

            def a_h2(w, j):
                for sem_read, value in reads_before(w, ("a_h2", j)):
                    pe.wait_ge(sem_read, value)
                t = slot(w, ("a_h2", j))
                for kc in range(F // 128):
                    m = pe.matmul(t[0:HC, 0:TA], w_tff2[:, kc, HC:D], a_h[:, kc, :], start=(kc == 0),
                                  stop=(kc == F // 128 - 1))
                m.then_inc(fill_sem(w, ("a_h2", j)), 1)

            def a_qk(w, _):
                for sem_read, value in reads_before(w, ("a_qk", 0)):
                    pe.wait_ge(sem_read, value)
                t = slot(w, ("a_qk", 0))
                if w.section == "first":
                    pe.wait_ge(loads["tqkv"], 16 * n_loads["tqkv"])
                pe.wait_ge(S["x1T"], upto("x1T", w.a))
                for n in range(4):
                    o = t[0:HC, n // 2, (n % 2) * TA:(n % 2 + 1) * TA]
                    chunks(o, lambda kc, k: w_tqkv[0:k, kc, n * HC:(n + 1) * HC], lambda kc, k: x1T[0:k, kc, :],
                           fill_sem(w, ("a_qk", 0)) if n == 3 else None)

            def a_v(w, _):
                for sem_read, value in reads_before(w, ("a_v", 0)):
                    pe.wait_ge(sem_read, value)
                t = slot(w, ("a_v", 0))
                wv = w_tqkv[:, :, 2 * D:3 * D].rearrange("p c (n two d) -> p c two n d", two=2, d=HD)
                for s in range(GS):
                    for odd in range(2):
                        chunks(t[64 * odd:64 * odd + NI, s * HC:(s + 1) * HC],
                               lambda kc, k: x1T[0:k, kc, s * NI:(s + 1) * NI], lambda kc, k: wv[0:k, kc, odd],
                               fill_sem(w, ("a_v", 0)) if s == GS - 1 and odd else None)

            def a_s(w, t2):
                for sem_read, value in reads_before(w, ("a_s", t2)):
                    pe.wait_ge(sem_read, value)
                t = slot(w, ("a_s", t2))
                pe.wait_ge(S["a_qT"], upto("a_qT", w.a))
                pe.wait_ge(S["a_kB"], upto("a_kB", w.a, 2 * t2 + 2))
                for half in range(2):
                    s = 2 * t2 + half
                    for c in range(2):
                        m = pe.matmul(t[64 * half:64 * half + NI, c, 0:6 * NI], a_qT[:, c, s * NI:(s + 1) * NI],
                                      a_kB[:, c, :, half * NI:(half + 1) * NI], start=True, stop=True)
                m.then_inc(fill_sem(w, ("a_s", t2)), 1)

            def a_pt(w, t2):
                for sem_read, value in reads_before(w, ("a_pt", t2)):
                    pe.wait_ge(sem_read, value)
                t = slot(w, ("a_pt", t2))
                pe.wait_ge(S["a_exp"], upto("a_exp", w.a, t2 + 1))
                for n in range(NH // 2):
                    m = pe.transpose(t[:, n // 3, (n % 3) * 128:(n % 3 + 1) * 128],
                                     a_p[:, t2, n * 128:(n + 1) * 128], w_ident[:, :])
                m.then_inc(fill_sem(w, ("a_pt", t2)), 1)

            def a_o(w, t2):
                for sem_read, value in reads_before(w, ("a_o", t2)):
                    pe.wait_ge(sem_read, value)
                t = slot(w, ("a_o", t2))
                pe.wait_ge(S["a_pT"], upto("a_pT", w.a, t2 + 1))
                pe.wait_ge(S["a_vB"], upto("a_vB", w.a))
                for half in range(2):
                    for n in range(NH // 2):
                        k = 2 * (HD + 1)
                        m = pe.matmul(t[64 * half:64 * half + NI, n * k:(n + 1) * k],
                                      a_pT[:, n, half * NI:(half + 1) * NI], a_vB[:, 2 * t2 + half, n, :],
                                      start=True, stop=True)
                m.then_inc(fill_sem(w, ("a_o", t2)), 1)

            def a_ot(w, t2):
                for sem_read, value in reads_before(w, ("a_ot", t2)):
                    pe.wait_ge(sem_read, value)
                t = slot(w, ("a_ot", t2))
                pe.wait_ge(S["a_on"], upto("a_on", w.a, t2 + 1))
                for c in range(2):
                    m = pe.transpose(t[0:HC, c * 128:(c + 1) * 128], a_on[:, c * HC:(c + 1) * HC], w_ident[:, :])
                m.then_inc(fill_sem(w, ("a_ot", t2)), 1)

            def a_pr(w, _):
                for sem_read, value in reads_before(w, ("a_pr", 0)):
                    pe.wait_ge(sem_read, value)
                t = slot(w, ("a_pr", 0)).rearrange("p (c t) -> p c t", c=2)
                if w.section == "first":
                    pe.wait_ge(loads["tproj"], 16 * n_loads["tproj"])
                pe.wait_ge(S["a_oT"], upto("a_oT", w.a))
                for c in range(2):
                    chunks(t[0:HC, c, :], lambda kc, k: w_tproj[0:k, kc, c * HC:(c + 1) * HC],
                           lambda kc, k: a_oT[0:k, kc, :], fill_sem(w, ("a_pr", 0)) if c else None)

            def b_ht(w, _):
                for sem_read, value in reads_before(w, ("b_ht", 0)):
                    pe.wait_ge(sem_read, value)
                t = slot(w, ("b_ht", 0))
                pe.wait_ge(S["hT"], upto("hT", w.b))
                pe.wait_ge(S["txt_in"], upto("txt_in", w.b))
                hv = hT[:, :, :, :].rearrange("p c s t -> p c (s t)")
                for tile in range(TILES_B):
                    for c in range(2):
                        m = pe.transpose(t[:, tile, c * HC:(c + 1) * HC], hv[:, c, tile * 128:(tile + 1) * 128],
                                         w_ident[0:HC, 0:HC])
                m.then_inc(fill_sem(w, ("b_ht", 0)), 1)

            def b_u(w, n):
                for sem_read, value in reads_before(w, ("b_u", n)):
                    pe.wait_ge(sem_read, value)
                t = slot(w, ("b_u", n))
                if n == 0:
                    pe.wait_ge(S["out_tm"], upto("out_tm", w.b, 0))
                for tile in range(TILES_B):
                    pe.wait_ge(S["ln_u"], upto("ln_u", w.b, 3 * n + tile + 1))
                    for c in range(2):
                        m = pe.transpose(t[0:HC, c, tile * 128:(tile + 1) * 128], u[:, tile, c * HC:(c + 1) * HC],
                                         w_ident[:, :])
                m.then_inc(fill_sem(w, ("b_u", n)), 1)

            def b_in(w, j):
                for sem_read, value in reads_before(w, ("b_in", j)):
                    pe.wait_ge(sem_read, value)
                t = slot(w, ("b_in", j))
                if j == 0:
                    pe.wait_ge(loads["in"], 16 * n_loads["in"])
                pe.wait_ge(S["lnT"], upto("lnT", w.b, 2))
                for c in range(3):
                    f0 = j * DI + c * 128
                    chunks(t[:, c, 0:TB], lambda kc, k: w_in[0:k, kc, f0:f0 + 128], lambda kc, k: bT[0:k, kc, :],
                           fill_sem(w, ("b_in", j)) if c == 2 else None, bias_row=False)

            def tm_product(w, unit, lhs, rhs, n_k, halves=None):
                t = slot(w, unit)
                tile = unit[1]
                for kc in range(n_k):
                    if halves is not None and kc == n_k // 2:
                        pe.wait_ge(S[halves], upto(halves, w.b))
                    m = pe.matmul(t[:, 0, 0:D], lhs[:, kc, tile * 128:(tile + 1) * 128], rhs[:, kc, :],
                                  start=(kc == 0), stop=(kc == n_k - 1))
                m.then_inc(fill_sem(w, unit), 1)

            def b_out(w, tile):
                for sem_read, value in reads_before(w, ("b_out", tile)):
                    pe.wait_ge(sem_read, value)
                pe.wait_ge(loads["out"], 16 * n_loads["out"])
                pe.wait_ge(S["gate"], upto("gate", w.b))
                tm_product(w, ("b_out", tile), cv.rearrange("p c s t -> p c (s t)"), w_out, DI // 128)

            def b_qk(w, name, f0):
                for sem_read, value in reads_before(w, (name, 0)):
                    pe.wait_ge(sem_read, value)
                t = slot(w, (name, 0))
                pe.wait_ge(loads["qkv"], 16 * n_loads["qkv"])
                pe.wait_ge(S["lnT"], upto("lnT", w.b, 4))
                for c in range(2):
                    chunks(t[0:HC, c, 0:TB], lambda kc, k: w_qkv[0:k, kc, f0 + c * HC:f0 + (c + 1) * HC],
                           lambda kc, k: bT[0:k, kc, :], fill_sem(w, (name, 0)) if c else None)

            def b_v(w, _):
                for sem_read, value in reads_before(w, ("b_v", 0)):
                    pe.wait_ge(sem_read, value)
                t = slot(w, ("b_v", 0))
                for s in range(GS):
                    chunks(t[0:N, s // 2, (s % 2) * D:(s % 2 + 1) * D], lambda kc, k: bT[0:k, kc, s * N:(s + 1) * N],
                           lambda kc, k: w_qkv[0:k, kc, 2 * D:3 * D], fill_sem(w, ("b_v", 0)) if s == GS - 1 else None)

            def b_s(w, s):
                for sem_read, value in reads_before(w, ("b_s", s)):
                    pe.wait_ge(sem_read, value)
                t = slot(w, ("b_s", s))
                pe.wait_ge(S["b_qT"], upto("b_qT", w.b))
                pe.wait_ge(S["b_kB"], upto("b_kB", w.b, 2 * s + 2))
                for c, h0, h1, bank, col in ((0, 0, 4, 0, 0), (0, 4, 6, 1, 0), (1, 0, 2, 1, 2), (1, 2, 6, 2, 0)):
                    m = pe.matmul(t[0:N, bank, col * N:(col + h1 - h0) * N], b_qT[:, c, s * N:(s + 1) * N],
                                  b_kBv[:, s % 2, c, h0:h1, :], start=True, stop=True)
                m.then_inc(fill_sem(w, ("b_s", s)), 1)

            def turn_p(w, unit, s):
                t = slot(w, unit)
                for h in range(NH):
                    m = pe.transpose(t[0:N, h // 4, (h % 4) * N:(h % 4 + 1) * N], pr[:, s % 2, h * N:(h + 1) * N],
                                     w_ident[0:N, 0:N])
                m.then_inc(fill_sem(w, unit), 1)

            def b_pt(w, s):
                for sem_read, value in reads_before(w, ("b_pt", s)):
                    pe.wait_ge(sem_read, value)
                pe.wait_ge(S["b_w"], upto("b_w", w.b, s + 1))
                turn_p(w, ("b_pt", s), s)

            def b_o(w, s):
                for sem_read, value in reads_before(w, ("b_o", s)):
                    pe.wait_ge(sem_read, value)
                t = slot(w, ("b_o", s))
                pe.wait_ge(S["b_pT"], upto("b_pT", w.b, s + 1))
                pe.wait_ge(S["b_vB"], upto("b_vB", w.b))
                for h in range(NH):
                    c, row = h // 6, h % 6 // 2 * 2 * HD
                    m = pe.matmul(t[row:row + 2 * HD, c * N:(c + 1) * N], b_vB[:, s, h, :], pT[:, h, :],
                                  start=(h % 2 == 0), stop=(h % 2 == 1))
                m.then_inc(fill_sem(w, ("b_o", s)), 1)

            def samples_of(tile):
                return -(-(tile + 1) * 128 // N)

            def b_pr(w, tile):
                for sem_read, value in reads_before(w, ("b_pr", tile)):
                    pe.wait_ge(sem_read, value)
                t = slot(w, ("b_pr", tile))
                pe.wait_ge(loads["proj"], 16 * n_loads["proj"])
                pe.wait_ge(S["b_oT"], upto("b_oT", w.b, samples_of(tile)))
                chunks(t[:, 0, 0:D], lambda kc, k: bT[0:k, kc, tile * 128:(tile + 1) * 128],
                       lambda kc, k: w_proj[0:k, kc, :], fill_sem(w, ("b_pr", tile)))

            def b_f1(w, j):
                for sem_read, value in reads_before(w, ("b_f1", j)):
                    pe.wait_ge(sem_read, value)
                t = slot(w, ("b_f1", j))
                pe.wait_ge(loads["ff1"], 16 * n_loads["ff1"])
                pe.wait_ge(S["lnT"], upto("lnT", w.b, 6))
                for c in range(3):
                    f0 = (3 * j + c) * 128
                    chunks(t[:, c, 0:TB], lambda kc, k: w_ff1[0:k, kc, f0:f0 + 128], lambda kc, k: bT[0:k, kc, :],
                           fill_sem(w, ("b_f1", j)) if c == 2 else None)

            def b_f2(w, tile):
                for sem_read, value in reads_before(w, ("b_f2", tile)):
                    pe.wait_ge(sem_read, value)
                pe.wait_ge(loads["ff2"], 16 * n_loads["ff2"])
                pe.wait_ge(S["b_h"], upto("b_h", w.b, 1))
                tm_product(w, ("b_f2", tile), b_h, w_ff2, F // 128, halves="b_h")

            def c_g(w, _):
                for sem_read, value in reads_before(w, ("c_g", 0)):
                    pe.wait_ge(sem_read, value)
                t = slot(w, ("c_g", 0))
                pe.wait_ge(loads["cproj"], 16 * n_loads["cproj"])
                pe.wait_ge(S["lnT"], upto("lnT", w.b, 8))
                k14 = EXPERTS + 4
                for s in range(GS):
                    chunks(t[0:N, s * k14:(s + 1) * k14], lambda kc, k: bT[0:k, kc, s * N:(s + 1) * N],
                           lambda kc, k: w_cgate[0:k, kc, :], fill_sem(w, ("c_g", 0)) if s == GS - 1 else None,
                           bias_row=False)

            def c_qk(w, tile):
                for sem_read, value in reads_before(w, ("c_qk", tile)):
                    pe.wait_ge(sem_read, value)
                t = slot(w, ("c_qk", tile))
                pe.wait_ge(s_centred, 2)
                pe.wait_ge(S["lnT"], upto("lnT", w.b, 8))
                for n in range(3):
                    chunks(t[:, n, :], lambda kc, k: bT[0:k, kc, tile * 128:(tile + 1) * 128],
                           lambda kc, k: w_cqkv[0:k, kc, n * 512:(n + 1) * 512],
                           fill_sem(w, ("c_qk", tile)) if n == 2 else None)

            def c_qt(w, tile):
                for sem_read, value in reads_before(w, ("c_qt", tile)):
                    pe.wait_ge(sem_read, value)
                t = slot(w, ("c_qt", tile))
                pe.wait_ge(S["qkn"], upto("qkn", w.b, tile + 1))
                for n in range(NH):
                    m = pe.transpose(t[:, n // 4, (n % 4) * 128:(n % 4 + 1) * 128],
                                     qkn[tile % 2][:, n * 128:(n + 1) * 128], w_ident[:, :])
                m.then_inc(fill_sem(w, ("c_qt", tile)), 1)

            def c_v_(w, s):
                for sem_read, value in reads_before(w, ("c_v", s)):
                    pe.wait_ge(sem_read, value)
                t = slot(w, ("c_v", s))
                half = NH * HD2 // 2
                for n in range(2):
                    f0 = 2 * NH * HD2 + n * half
                    chunks(t[0:N, n, 0:half], lambda kc, k: bT[0:k, kc, s * N:(s + 1) * N],
                           lambda kc, k: w_cqkv[0:k, kc, f0:f0 + half], fill_sem(w, ("c_v", s)) if n else None)

            def c_s(w, s):
                for sem_read, value in reads_before(w, ("c_s", s)):
                    pe.wait_ge(sem_read, value)
                t = slot(w, ("c_s", s))
                pe.wait_ge(S["c_qkT"], upto("c_qkT", w.b, ((s + 1) * N - 1) // 128 + 1))
                for n in range(NH // 2):
                    m = pe.matmul(t[0:N, n // 2, (n % 2) * 2 * N:(n % 2 + 1) * 2 * N], c_qT[:, n, s * N:(s + 1) * N],
                                  c_kB[:, n, :, s * N:(s + 1) * N], start=True, stop=True)
                m.then_inc(fill_sem(w, ("c_s", s)), 1)

            def c_pt(w, s):
                for sem_read, value in reads_before(w, ("c_pt", s)):
                    pe.wait_ge(sem_read, value)
                pe.wait_ge(S["c_w"], upto("c_w", w.b, s + 1))
                turn_p(w, ("c_pt", s), s)

            def c_o(w, s):
                for sem_read, value in reads_before(w, ("c_o", s)):
                    pe.wait_ge(sem_read, value)
                t = slot(w, ("c_o", s))
                pe.wait_ge(S["c_pT"], upto("c_pT", w.b, s + 1))
                pe.wait_ge(S["c_v"], upto("c_v", w.b, min(s + 2, GS)))
                for h in range(NH):
                    n, row = h // 2, h % 2 * HD2
                    m = pe.matmul(t[row:row + HD2, n // 3, (n % 3) * N:(n % 3 + 1) * N], c_v[:, s % 2, h, :],
                                  pT[:, h, :], start=True, stop=True)
                m.then_inc(fill_sem(w, ("c_o", s)), 1)

            def c_pr(w, tile):
                for sem_read, value in reads_before(w, ("c_pr", tile)):
                    pe.wait_ge(sem_read, value)
                pe.wait_ge(S["c_oT"], upto("c_oT", w.b, samples_of(tile)))
                tm_product(w, ("c_pr", tile), c_oT, w_cproj, NH * HD2 // 128)

            def warm(w, k):
                for sem_read, value in reads_before(w, ("warm", k)):
                    pe.wait_ge(sem_read, value)
                t = slot(w, ("warm", k))
                if w.section == "first":
                    pe.wait_ge(loads["ident"], 16 * n_loads["ident"])
                m = pe.matmul(t[:, 0:2 * D], w_ident[:, :], w_patch[:, 0:2, :], start=True, stop=True)
                m.then_inc(fill_sem(w, ("warm", k)), 1)

            sections(pe, {"warm": warm, "a_em": a_em, "a_x0": a_x0, "a_f1": a_f1, "a_g1": a_g1, "a_h2": a_h2,
                          "a_f2": a_f2, "a_qk": a_qk, "a_v": a_v, "a_s": a_s,
                          "a_pt": a_pt, "a_o": a_o, "a_ot": a_ot, "a_pr": a_pr, "b_ht": b_ht, "b_u": b_u,
                          "b_in": b_in, "b_out": b_out, "b_q": lambda w, n: b_qk(w, "b_q", 0),
                          "b_k": lambda w, n: b_qk(w, "b_k", D), "b_v": b_v, "b_s": b_s, "b_pt": b_pt, "b_o": b_o,
                          "b_pr": b_pr, "b_f1": b_f1, "b_f2": b_f2, "c_g": c_g, "c_qk": c_qk,
                          "c_qt": c_qt, "c_v": c_v_, "c_s": c_s, "c_pt": c_pt, "c_o": c_o,
                          "c_pr": c_pr}, at_end=all_read)

        @block.scalar
        def _(act):
            act.wait_ge(s_set, 1)
            act.wait_ge(loads["vec"], 16 * n_loads["vec"])

            def a_f1(w, j):
                act.wait_ge(fill_sem(w, ("a_f1", j)), fill_count(w, ("a_f1", j)))
                t = slot(w, ("a_f1", j))
                for n in range(2):
                    act.activation(a_h[:, 2 * n:2 * n + 2, :], t[:, n, :].rearrange("p (c t) -> p c t", c=2),
                                   ACT.Gelu_apprx_tanh).then_inc(S["a_h"], 1)

            def a_g1(w, j):
                act.wait_ge(fill_sem(w, ("a_g1", j)), fill_count(w, ("a_g1", j)))
                t = slot(w, ("a_g1", j))
                act.activation(a_h[:, 4:6, :], t.rearrange("p (c t) -> p c t", c=2), ACT.Gelu_apprx_tanh)\
                   .then_inc(S["a_h"], 1)

            def a_qk(w, _):
                act.wait_ge(fill_sem(w, ("a_qk", 0)), fill_count(w, ("a_qk", 0)))
                t = slot(w, ("a_qk", 0))
                act.activation(a_kT[:, :, :], t[0:HC, 1, :].rearrange("p (c t) -> p c t", c=2), ACT.Copy)\
                   .then_inc(S["a_kT"], 1)
                act.activation(a_qT[:, :, :], t[0:HC, 0, :].rearrange("p (c t) -> p c t", c=2), ACT.Copy)\
                   .then_inc(S["a_qT"], 1)

            def a_v(w, _):
                act.wait_ge(fill_sem(w, ("a_v", 0)), fill_count(w, ("a_v", 0)))
                t = slot(w, ("a_v", 0))
                for odd in range(2):
                    r = slice(64 * odd, 64 * odd + 64)
                    src = t[r, 0:GS * HC].rearrange("p (s n d) -> p s n d", s=GS, d=HD)
                    m = act.activation(a_vB[r, :, :, odd * (HD + 1):odd * (HD + 1) + HD], src, ACT.Copy)
                m.then_inc(S["a_vB"], 1)

            def a_e(w, t2):
                act.wait_ge(S["a_sub"], upto("a_sub", w.a, t2 + 1))
                act.activation(a_p[:, t2, :], a_p[:, t2, :], ACT.Exp, scale=HD ** -0.5).then_inc(S["a_exp"], 1)

            def a_pt(w, t2):
                act.wait_ge(fill_sem(w, ("a_pt", t2)), fill_count(w, ("a_pt", t2)))
                t = slot(w, ("a_pt", t2))
                act.activation(a_pT[:, :, :].rearrange("p (b n) t -> p b (n t)", b=2), t[:, 0:2, 0:384], ACT.Copy)\
                   .then_inc(S["a_pT"], 1)

            def a_ot(w, t2):
                act.wait_ge(fill_sem(w, ("a_ot", t2)), fill_count(w, ("a_ot", t2)))
                t = slot(w, ("a_ot", t2))
                act.activation(a_oT[0:HC, :, t2 * 128:(t2 + 1) * 128],
                               t[0:HC, 0:256].rearrange("p (c t) -> p c t", c=2), ACT.Copy)\
                   .then_inc(S["a_oT"], 1)

            def b_ht(w, _):
                if w.section == "loop":
                    act.wait_ge(S["a_emb"], upto("a_emb", w.b))
                    act.dma_start(x_in[:, :, :], xT[w.a]).then_inc(S["x_in"], 16)
                act.wait_ge(fill_sem(w, ("b_ht", 0)), fill_count(w, ("b_ht", 0)))
                t = slot(w, ("b_ht", 0))
                if w.section == "loop":
                    act.dma_start(hT[:, :, :, NI:N], txtT[w.a]).then_inc(S["txt_in"], 16)
                act.wait_ge(S["ln_stats"], upto("ln_stats", w.b, TILES_B))
                act.activation(h_tm[:, :, :], t[:, :, 0:D], ACT.Copy)\
                   .then_inc(S["h_tm"], 1)

            def b_u(w, n):
                act.wait_ge(fill_sem(w, ("b_u", n)), fill_count(w, ("b_u", n)))
                t = slot(w, ("b_u", n))
                if n < 3:
                    act.activation(bT[0:HC, 0, :], t[0:HC, 0, 0:TB], ACT.Identity, scale=col96(f"ln{n + 1}_g", 0),
                                   bias=col96(f"ln{n + 1}_b", 0))\
                       .then_inc(S["lnT"], 1)
                else:
                    act.activation(bT[0:HC, 0, :], t[0:HC, 0, 0:TB], ACT.Copy)\
                       .then_inc(S["lnT"], 1)

            def b_in(w, j):
                act.wait_ge(fill_sem(w, ("b_in", j)), fill_count(w, ("b_in", j)))
                t = slot(w, ("b_in", j))
                if j == 0:
                    for c in range(3):
                        m = act.activation(xpad[:, c, :, KC - 1:], t[:, c, 0:TB].rearrange("p (s t) -> p s t", s=GS),
                                           ACT.Copy)
                    m.then_inc(S["xpad"], 1)
                    return
                act.activation(sz, t[:, :, 0:TB], ACT.Silu).then_inc(S["sz"], 1)
                for c in range(3):
                    act.wait_ge(S["conv"], upto("conv", w.b, 10 + c))
                    act.activation(cv[:, c], cv[:, c], ACT.Silu).then_inc(S["conv_act"], 1)

            def b_q(w, _):
                act.wait_ge(fill_sem(w, ("b_q", 0)), fill_count(w, ("b_q", 0)))
                t = slot(w, ("b_q", 0))
                act.activation(b_qT, t[0:HC, 0:2, 0:TB], ACT.Copy)\
                   .then_inc(S["b_qT"], 1)

            def b_v(w, _):
                act.wait_ge(fill_sem(w, ("b_v", 0)), fill_count(w, ("b_v", 0)))
                t = slot(w, ("b_v", 0))
                for n in range(2):
                    pairs = b_vB[:, 2 * n:2 * n + 2].rearrange("p s (j two) (half d) -> p (s j) (two half) d",
                                                               two=2, half=2)
                    m = act.activation(pairs[:, :, 0:4:3, :],
                                       t[0:N, n, 0:2 * D].rearrange("p (n two d) -> p n two d", two=2, d=HD), ACT.Copy)
                m.then_inc(S["b_vB"], 1)

            def numerators(w, stage, s, head):
                act.wait_ge(S[stage + "_sub"], upto(stage + "_sub", w.b, s + 1))
                act.activation(pr[:, s % 2, :], pr[:, s % 2, :], ACT.Exp, scale=head ** -0.5)\
                   .then_inc(S[stage + "_exp"], 1)

            def turned(w, stage, s):
                act.wait_ge(fill_sem(w, (stage + "_pt", s)), fill_count(w, (stage + "_pt", s)))
                t = slot(w, (stage + "_pt", s))
                act.activation(pT[:, :, :].rearrange("p (b h) t -> p b (h t)", b=3), t[0:N, :, 0:4 * N], ACT.Copy)\
                   .then_inc(S[stage + "_pT"], 1)

            def b_o(w, s):
                act.wait_ge(fill_sem(w, ("b_o", s)), fill_count(w, ("b_o", s)))
                t = slot(w, ("b_o", s))
                act.activation(bT[0:HC, :, s * N:(s + 1) * N], t[0:HC, 0:2 * N].rearrange("p (c t) -> p c t", c=2),
                               ACT.Copy).then_inc(S["b_oT"], 1)

            def b_f1(w, j):
                act.wait_ge(fill_sem(w, ("b_f1", j)), fill_count(w, ("b_f1", j)))
                t = slot(w, ("b_f1", j))
                act.activation(b_h[:, 3 * j:3 * j + 3, :], t[:, :, 0:TB], ACT.Gelu)\
                   .then_inc(S["b_h"], 1)

            def c_g(w, _):
                act.wait_ge(S["g_step"], upto("g_step", w.b, 4))
                act.activation(gsm[:, 1], gsm[:, 1], ACT.Exp).then_inc(S["g_exp"], 1)

            def c_qk(w, tile):
                act.wait_ge(fill_sem(w, ("c_qk", tile)), fill_count(w, ("c_qk", tile)))
                t = slot(w, ("c_qk", tile))
                if tile > 0:
                    act.wait_ge(S["ss"], upto("ss", w.b, tile))
                act.activation(sq.rearrange("p (b n) -> p b n", b=3), t[:, :, :], ACT.Square).then_inc(S["sq"], 1)
                if tile == 2:
                    act.wait_ge(fill_sem(w, ("c_qt", 0)), fill_count(w, ("c_qt", 0)))
                act.activation(qkn[tile % 2].rearrange("p (b n) -> p b n", b=3), t[:, :, :], ACT.Copy)\
                   .then_inc(S["qk_raw"], 1)

            def c_qt(w, tile):
                act.wait_ge(fill_sem(w, ("c_qt", tile)), fill_count(w, ("c_qt", tile)))
                t = slot(w, ("c_qt", tile))
                tv = t[:, :, :].rearrange("p b (n t) -> p (b n) t", t=128)
                cols = slice(tile * 128, (tile + 1) * 128)
                act.activation(c_qT[:, :, cols], tv[:, 0:6, :], ACT.Identity, scale=col128("q_w"), bias=col128("q_b"))
                for par in range(2):
                    r = slice(64 * par, 64 * par + 64)
                    m = act.activation(c_kB[r, :, par, cols], tv[r, 6:12, :], ACT.Identity, scale=col128("k_w")[r, :],
                                       bias=col128("k_b")[r, :])
                m.then_inc(S["c_qkT"], 1)

            def c_v_(w, s):
                act.wait_ge(fill_sem(w, ("c_v", s)), fill_count(w, ("c_v", s)))
                t = slot(w, ("c_v", s))
                if s >= 2:
                    act.wait_ge(S["c_oT"], upto("c_oT", w.b, s - 1))
                half = NH * HD2 // 2
                act.activation(c_v[:, s % 2, :, :].rearrange("p (b h) d -> p b h d", b=2),
                               t[0:N, :, 0:half].rearrange("p b (h d) -> p b h d", d=HD2), ACT.Copy)\
                   .then_inc(S["c_v"], 1)

            def c_o(w, s):
                act.wait_ge(fill_sem(w, ("c_o", s)), fill_count(w, ("c_o", s)))
                t = slot(w, ("c_o", s))
                act.activation(c_oT[:, :, s * N:(s + 1) * N].rearrange("p (b n) t -> p b n t", b=2),
                               t[:, :, 0:3 * N].rearrange("p b (n t) -> p b n t", t=N), ACT.Copy)\
                   .then_inc(S["c_oT"], 1)

            sections(act, {"a_f1": a_f1, "a_g1": a_g1, "a_qk": a_qk, "a_v": a_v, "a_e": a_e, "a_pt": a_pt,
                           "a_ot": a_ot, "b_ht": b_ht, "b_u": b_u, "b_in": b_in, "b_q": b_q,
                           "b_v": b_v, "b_e": lambda w, s: numerators(w, "b", s, HD),
                           "b_pt": lambda w, s: turned(w, "b", s), "b_o": b_o, "b_f1": b_f1,
                           "c_qk": c_qk, "c_qt": c_qt, "c_v": c_v_, "c_g": c_g,
                           "c_e": lambda w, s: numerators(w, "c", s, HD2), "c_pt": lambda w, s: turned(w, "c", s),
                           "c_o": c_o})

        @block.vector
        def _(dve):
            for t in (x0T, x1T, x2T, a_oT, bT):
                dve.memset(t[HC:HC + 1, 0, :], 1.0)
            dve.memset(a_vB[:, :, :, :], 0.0)
            dve.memset(b_vB[:, :, :, :], 0.0)
            dve.memset(c_kB[:, :, :, :], 0.0).then_inc(s_set, 1)
            dve.wait_ge(s_set, 1)
            for odd in range(2):
                c = odd * (HD + 1) + HD
                m = dve.memset(a_vB[64 * odd:64 * odd + 64, :, :, c:c + 1], 1.0)
            m.then_inc(s_set, 1)
            dve.wait_ge(loads["vec"], 16 * n_loads["vec"])
            for c in range(2):
                dve.tensor_scalar(w_pe[:, c, :], w_pe[:, c, :], col96("tok_b", c), None, ALU.add).then_inc(s_set, 1)
            dve.wait_ge(s_set, 4)

            def inverse_root(tile, n, name, group, done, starts):
                x, y, t = (tile[:, r, 0:n] for r in range(3))
                count = [done]

                def ordered(ins):
                    ins.then_inc(S[name], 1)
                    count[0] += 1
                    dve.wait_ge(S[name], upto(name, group, count[0]))

                for start in starts:
                    ordered(start())
                ordered(dve.tensor_scalar(y.bitcast(I32), x.bitcast(I32), 1, None, ALU.logical_shift_right))
                ordered(dve.tensor_scalar(y.bitcast(I32), y.bitcast(I32), -1.0, float(ROOT_SEED), ALU.mult, ALU.add))
                for _ in range(ROOT_ROUNDS):
                    ordered(dve.tensor_tensor(t, y, y, ALU.mult))
                    ordered(dve.scalar_tensor_tensor(out=t, in0=t, scalar=-0.5, in1=x, op0=ALU.mult, op1=ALU.mult))
                    ordered(dve.scalar_tensor_tensor(out=y, in0=t, scalar=1.5, in1=y, op0=ALU.add, op1=ALU.mult))

            def a_en(w, _):
                dve.wait_ge(fill_sem(w, ("a_em", 0)), fill_count(w, ("a_em", 0)))
                t = slot(w, ("a_em", 0))
                pb = w_patch_b[:, :].unsqueeze(1).to_broadcast([128, TILES_A, D])
                dve.tensor_tensor(a_emb[:, :, :], t[:, 0:TILES_A * D].rearrange("p (n d) -> p n d", n=TILES_A), pb,
                                  ALU.add)\
                   .then_inc(S["a_emb"], 1)
                dve.wait_ge(S["a_emb"], upto("a_emb", w.a))
                for n in range(TILES_A):
                    dve.bn_stats(a_bn[:, n, :], a_emb[:, n, :]).then_inc(S["a_stats"], 1)
                dve.wait_ge(S["a_stats"], upto("a_stats", w.a))
                dve.tensor_copy(seen[:, 0:TILES_A], a_bn[:, :, 0])
                for n in range(TILES_A):
                    dve.bn_aggr(a_mv[:, n, :], a_bn[:, n, :]).then_inc(S["a_mv"], 1)
                dve.wait_ge(S["a_mv"], upto("a_mv", w.a))
                inverse_root(a_root, TILES_A, "a_root", w.a, 0, [
                    lambda: dve.tensor_scalar(a_root[:, 0, :], a_mv[:, :, 1], EPS, None, ALU.add)])
                for n in range(TILES_A):
                    dve.tensor_scalar(a_emb[:, n, :], a_emb[:, n, :], a_mv[:, n, 0:1], a_root[:, 1, n:n + 1],
                                      ALU.subtract, ALU.mult).then_inc(S["a_xn"], 1)

            def a_x0(w, _):
                dve.wait_ge(fill_sem(w, ("a_x0", 0)), fill_count(w, ("a_x0", 0)))
                t = slot(w, ("a_x0", 0)).rearrange("p (c s t) -> p c s t", c=2, s=GS)
                for c in range(2):
                    pe_c = w_pe[:, c, :].unsqueeze(1).to_broadcast([HC, GS, NI])
                    m = dve.scalar_tensor_tensor(out=x0T[0:HC, c, :].rearrange("p (s t) -> p s t", s=GS),
                                                 in0=t[0:HC, c], scalar=col96("tok_g", c), in1=pe_c, op0=ALU.mult,
                                                 op1=ALU.add).then_inc(S["x0T"], 1)

            def a_f2_chunk(w, name, j, c):
                dve.wait_ge(fill_sem(w, (name, j)), fill_count(w, (name, j)))
                t = slot(w, (name, j))[0:HC, 0:TA]
                if j == 0:
                    dve.tensor_scalar(x1T[0:HC, c, :], t, col96("tok_ff2_b", c), None, ALU.add).then_inc(S["x1T"], 1)
                else:
                    dve.scalar_tensor_tensor(
                        out=hT[:, c, :, 0:NI], in0=t.rearrange("p (s t) -> p s t", s=GS),
                        scalar=col96("tok_ff2_b", c), in1=x2T[0:HC, c, :].rearrange("p (s t) -> p s t", s=GS),
                        op0=ALU.add, op1=ALU.add).then_inc(S["hT"], 1)

            def a_s(w, t2):
                dve.wait_ge(fill_sem(w, ("a_s", t2)), fill_count(w, ("a_s", t2)))
                t = slot(w, ("a_s", t2))[:, 0:2, 0:6 * NI].rearrange("p b (h k) -> p b h k", k=NI)
                dve.tensor_reduce(a_max[:, t2, :].rearrange("p (b h) -> p b h", b=2), t, AX.X, ALU.max)\
                   .then_inc(S["a_max"], 1)
                dve.wait_ge(S["a_max"], upto("a_max", w.a, t2 + 1))
                mb = a_max[:, t2, :].rearrange("p (b h) -> p b h", b=2).unsqueeze(3).to_broadcast([128, 2, 6, NI])
                dve.tensor_tensor(a_p[:, t2, :].rearrange("p (b h k) -> p b h k", b=2, k=NI), t, mb, ALU.subtract)\
                   .then_inc(S["a_sub"], 1)

            def a_o(w, t2):
                dve.wait_ge(fill_sem(w, ("a_o", t2)), fill_count(w, ("a_o", t2)))
                t = slot(w, ("a_o", t2))[:, 0:NH * (HD + 1)].rearrange("p (h d) -> p h d", h=NH)
                dve.reciprocal(a_rec[:, t2, :], t[:, :, HD]).then_inc(S["a_rec"], 1)
                dve.wait_ge(S["a_rec"], upto("a_rec", w.a, t2 + 1))
                dve.tensor_tensor(a_on[:, :].rearrange("p (h d) -> p h d", h=NH), t[:, :, 0:HD],
                                  a_rec[:, t2, :].unsqueeze(2).to_broadcast([128, NH, HD]), ALU.mult)\
                   .then_inc(S["a_on"], 1)

            def a_pr(w, _):
                dve.wait_ge(fill_sem(w, ("a_pr", 0)), fill_count(w, ("a_pr", 0)))
                t = slot(w, ("a_pr", 0)).rearrange("p (c t) -> p c t", c=2)
                dve.tensor_tensor(x2T[0:HC, :, :], t[0:HC, :, :], x0T[0:HC, :, :], ALU.add)\
                   .then_inc(S["x2T"], 1)

            def statistics(w, n, src, tile):
                dve.bn_stats(bn[:, tile, :], src[:, tile, :]).then_inc(S["ln_stats"], 1)

            def moments(w, n):
                dve.wait_ge(S["ln_stats"], upto("ln_stats", w.b, 3 * n + TILES_B))
                dve.tensor_copy(seen[:, TILES_A:TILES_A + TILES_B], bn[:, :, 0])
                for tile in range(TILES_B):
                    dve.bn_aggr(mv[:, tile, :], bn[:, tile, :]).then_inc(S["ln_mv"], 1)
                dve.wait_ge(S["ln_mv"], upto("ln_mv", w.b, 3 * n + 3))

            def deviations(w, n):
                one = lambda: dve.tensor_scalar(root[:, 0, 0:TILES_B], mv[:, :, 1], EPS, None, ALU.add)
                both = lambda: dve.tensor_scalar(root[:, 0, TILES_B:2 * TILES_B], mv[:, :, 1], 1.0 + EPS, EPS * EPS,
                                                 ALU.mult, ALU.add)
                inverse_root(root, TILES_B * (1 if n else 2), "ln_root", w.b, n * ROOT_STEPS + (1 if n else 0),
                             [one] if n else [one, both])

            def normalise(w, n, src, scale):
                for tile in range(TILES_B):
                    dve.tensor_scalar(u[:, tile, :], src[:, tile, :], mv[:, tile, 0:1], scale[:, tile:tile + 1],
                                      ALU.subtract, ALU.mult).then_inc(S["ln_u"], 1)

            def b_ht(w, _):
                dve.wait_ge(fill_sem(w, ("b_ht", 0)), fill_count(w, ("b_ht", 0)))
                t = slot(w, ("b_ht", 0))[:, :, 0:D]
                for tile in range(TILES_B):
                    statistics(w, 0, t, tile)
                moments(w, 0)
                deviations(w, 0)
                dve.wait_ge(S["h_tm"], upto("h_tm", w.b))
                normalise(w, 0, h_tm, root[:, 1, TILES_B:2 * TILES_B])
                for tile in range(TILES_B):
                    dve.tensor_scalar(xr[:, tile, :], h_tm[:, tile, :], mv[:, tile, 0:1], root[:, 1, tile:tile + 1],
                                      ALU.subtract, ALU.mult).then_inc(S["y_tm"], 1)

            def b_u(w, n):
                dve.wait_ge(fill_sem(w, ("b_u", n)), fill_count(w, ("b_u", n)))
                t = slot(w, ("b_u", n))
                if n < 3:
                    dve.tensor_scalar(bT[0:HC, 1, :], t[0:HC, 1, 0:TB], col96(f"ln{n + 1}_g", 1),
                                      col96(f"ln{n + 1}_b", 1), ALU.mult, ALU.add)\
                       .then_inc(S["lnT"], 1)
                else:
                    dve.tensor_copy(bT[0:HC, 1, :], t[0:HC, 1, 0:TB])\
                       .then_inc(S["lnT"], 1)

            def b_in(w, j):
                if j == 0:
                    dve.wait_ge(fill_sem(w, ("b_in", 0)), fill_count(w, ("b_in", 0)))
                    dve.memset(xpad[:, :, :, 0:KC - 1], 0.0).then_inc(S["pad"], 1)
                    return
                dve.wait_ge(S["xpad"], upto("xpad", w.b))
                dve.wait_ge(S["pad"], upto("pad", w.b))
                for n in range(KC):
                    tap = KC - 1 - n
                    for c in range(3):
                        src = xpad[:, c, :, tap:tap + N]
                        if n == 0:
                            m = dve.tensor_scalar(cv[:, c], src, col128("conv_w", c * KC + tap), col128("conv_b", c),
                                                  ALU.mult, ALU.add)
                        else:
                            dve.wait_ge(S["conv"], upto("conv", w.b, 3 * (n - 1) + c + 1))
                            m = dve.scalar_tensor_tensor(out=cv[:, c], in0=src, scalar=col128("conv_w", c * KC + tap),
                                                         in1=cv[:, c], op0=ALU.mult, op1=ALU.add)
                        m.then_inc(S["conv"], 1)
                dve.wait_ge(S["sz"], upto("sz", w.b))
                for c in range(3):
                    dve.wait_ge(S["conv_act"], upto("conv_act", w.b, c + 1))
                    dve.tensor_tensor(cv[:, c], cv[:, c], sz[:, c, :].rearrange("p (s t) -> p s t", s=GS), ALU.mult)\
                       .then_inc(S["gate"], 1)

            def residual(w, unit, name, out_t, in_t):
                dve.wait_ge(fill_sem(w, unit), fill_count(w, unit))
                t = slot(w, unit)
                tile = unit[1]
                dve.tensor_tensor(out_t[:, tile, :], t[:, 0, 0:D], in_t[:, tile, :], ALU.add).then_inc(S[name], 1)
                dve.wait_ge(S[name], upto(name, w.b, tile + 1))

            def sum_and_norm(w, unit, name, x, n):
                residual(w, unit, name, x, x)
                statistics(w, n, x, unit[1])
                if unit[1] == TILES_B - 1:
                    moments(w, n)
                    deviations(w, n)
                    normalise(w, n, x, root[:, 1, 0:TILES_B])

            def b_out(w, tile):
                dve.wait_ge(S["y_tm"], upto("y_tm", w.b, tile + 1))
                sum_and_norm(w, ("b_out", tile), "x1_tm", xr, 1)

            def b_k(w, _):
                dve.wait_ge(fill_sem(w, ("b_k", 0)), fill_count(w, ("b_k", 0)))
                t = slot(w, ("b_k", 0))
                dve.tensor_copy(b_kT, t[0:HC, 0:2, 0:TB])\
                   .then_inc(S["b_kT"], 1)

            def less_max(w, stage, s):
                dve.wait_ge(fill_sem(w, (stage + "_s", s)), fill_count(w, (stage + "_s", s)))
                t = slot(w, (stage + "_s", s))[0:N, :, 0:4 * N].rearrange("p b (h k) -> p b h k", k=N)
                mx = smax[:, s % 2, :].rearrange("p (b h) -> p b h", b=3)
                dve.tensor_reduce(mx, t, AX.X, ALU.max).then_inc(S[stage + "_max"], 1)
                dve.wait_ge(S[stage + "_max"], upto(stage + "_max", w.b, s + 1))
                dve.tensor_tensor(pr[:, s % 2, :].rearrange("p (b h k) -> p b h k", b=3, k=N), t,
                                  mx.unsqueeze(3).to_broadcast([N, 3, 4, N]), ALU.subtract)\
                   .then_inc(S[stage + "_sub"], 1)

            def weights(w, stage, s):
                e = pr[:, s % 2, :].rearrange("p (h k) -> p h k", k=N)
                dve.wait_ge(S[stage + "_exp"], upto(stage + "_exp", w.b, s + 1))
                dve.tensor_reduce(psum[:, s % 2, :], e, AX.X, ALU.add).then_inc(S[stage + "_sum"], 1)
                dve.wait_ge(S[stage + "_sum"], upto(stage + "_sum", w.b, s + 1))
                dve.reciprocal(rec[:, s % 2, :], psum[:, s % 2, :]).then_inc(S[stage + "_rec"], 1)
                dve.wait_ge(S[stage + "_rec"], upto(stage + "_rec", w.b, s + 1))
                factor = rec
                if stage == "c":
                    dve.wait_ge(S["gates"], upto("gates", w.b))
                    dve.tensor_tensor(gr[:, s % 2, :], rec[:, s % 2, :], gates[:, s, :], ALU.mult)\
                       .then_inc(S["c_gr"], 1)
                    dve.wait_ge(S["c_gr"], upto("c_gr", w.b, s + 1))
                    factor = gr
                dve.tensor_tensor(e, e, factor[:, s % 2, :].unsqueeze(2).to_broadcast([N, NH, N]), ALU.mult)\
                   .then_inc(S[stage + "_w"], 1)

            def b_pr(w, tile):
                sum_and_norm(w, ("b_pr", tile), "x2_tm", xr, 2)

            def b_f2(w, tile):
                dve.wait_ge(S["hx"], upto("hx", w.b))
                sum_and_norm(w, ("b_f2", tile), "h2_tm", hx, 3)

            def c_g(w, _):
                dve.wait_ge(fill_sem(w, ("c_g", 0)), fill_count(w, ("c_g", 0)))
                t = slot(w, ("c_g", 0))[0:N, 0:GS * (EXPERTS + 4)].rearrange("p (s k) -> p s k", s=GS)
                step = [0]

                def ordered(ins):
                    ins.then_inc(S["g_step"], 1)
                    step[0] += 1
                    dve.wait_ge(S["g_step"], upto("g_step", w.b, step[0]))

                def rows(n, lo, hi):
                    return gsm[:, n, :, lo:hi]

                def spread(ap, k):
                    return ap.to_broadcast([N, GS, k])

                pairs = lambda n, at: gsm[:, n, :, at:at + 4].rearrange("p s (a b) -> p s a b", b=2)
                E_ = EXPERTS
                mx = rows(0, 0, 1)
                mx2 = gsm[:, 0, :, 1:3]
                ordered(dve.tensor_reduce(gsm[:, 0, :, 0], t[:, :, 0:E_], AX.X, ALU.max))
                ordered(dve.tensor_reduce(mx2, t[:, :, E_:E_ + 4].rearrange("p s (a b) -> p s a b", b=2), AX.X, ALU.max))
                ordered(dve.tensor_tensor(rows(1, 0, E_), t[:, :, 0:E_], spread(mx, E_), ALU.subtract))
                m = dve.tensor_tensor(pairs(1, E_), t[:, :, E_:E_ + 4].rearrange("p s (a b) -> p s a b", b=2),
                                      mx2.unsqueeze(3).to_broadcast([N, GS, 2, 2]), ALU.subtract)
                ordered(m)
                dve.wait_ge(S["g_exp"], upto("g_exp", w.b))
                e = rows(1, 0, E_)
                prio_b = w_prio[:, :].unsqueeze(1).to_broadcast([N, GS, E_])

                def first_of_largest(values, n):
                    top = gsm[:, n, :, 0:1]
                    ordered(dve.tensor_reduce(gsm[:, n, :, 0], values, AX.X, ALU.max))
                    ordered(dve.tensor_tensor(rows(n + 1, 0, E_), values, spread(top, E_), ALU.is_equal))
                    ordered(dve.tensor_tensor(rows(n + 1, 0, E_), rows(n + 1, 0, E_), prio_b, ALU.mult))
                    ordered(dve.tensor_reduce(gsm[:, n, :, 1], rows(n + 1, 0, E_), AX.X, ALU.max))
                    ordered(dve.tensor_tensor(rows(n + 2, 0, E_), rows(n + 1, 0, E_), spread(gsm[:, n, :, 1:2], E_),
                                              ALU.is_equal))

                first_of_largest(e, 2)
                ordered(dve.scalar_tensor_tensor(out=rows(5, 0, E_), in0=rows(4, 0, E_), scalar=-2.0, in1=e,
                                                 op0=ALU.mult, op1=ALU.add))
                first_of_largest(rows(5, 0, E_), 6)
                ordered(dve.tensor_tensor(rows(9, 0, E_), rows(4, 0, E_), rows(8, 0, E_), ALU.add))
                ordered(dve.tensor_tensor(rows(9, 0, E_), rows(9, 0, E_), e, ALU.mult))
                ordered(dve.tensor_reduce(gsm[:, 10, :, 0], rows(9, 0, E_), AX.X, ALU.add))
                ordered(dve.tensor_reduce(gsm[:, 10, :, 1:3], pairs(1, E_), AX.X, ALU.add))
                ordered(dve.reciprocal(gsm[:, 11, :, 0:3], gsm[:, 10, :, 0:3]))
                ordered(dve.tensor_tensor(gsm[:, 10, :, 4:6], rows(1, E_, E_ + 2), spread(gsm[:, 11, :, 1:2], 2),
                                          ALU.mult))
                ordered(dve.scalar_tensor_tensor(out=gsm[:, 10, :, 6], in0=gsm[:, 10, :, 4], scalar=4.0,
                                                 in1=gsm[:, 11, :, 2], op0=ALU.mult, op1=ALU.mult))
                ordered(dve.scalar_tensor_tensor(out=gsm[:, 10, :, 7], in0=gsm[:, 10, :, 5], scalar=4.0,
                                                 in1=gsm[:, 11, :, 0], op0=ALU.mult, op1=ALU.mult))
                dve.tensor_tensor(gates[:, :, 0:2], rows(1, E_ + 2, E_ + 4), spread(gsm[:, 10, :, 6:7], 2), ALU.mult)\
                   .then_inc(S["gates"], 1)
                dve.tensor_tensor(gates[:, :, 2:NH], rows(9, 0, E_), spread(gsm[:, 10, :, 7:8], E_), ALU.mult)\
                   .then_inc(S["gates"], 1)
                assert step[0] == PER_GROUP["g_step"], step[0]

            def c_qk(w, tile):
                dve.wait_ge(S["sq"], upto("sq", w.b, tile + 1))
                dve.tensor_reduce(ss[:, :], sq.rearrange("p (h d) -> p h d", d=HD2), AX.X, ALU.add)\
                   .then_inc(S["ss"], 1)
                dve.wait_ge(S["ss"], upto("ss", w.b, tile + 1))
                inverse_root(qk_root, 2 * NH, "qk_root", w.b, tile * ROOT_STEPS, [
                    lambda: dve.tensor_scalar(qk_root[:, 0, :], ss[:, :], 1.0 / HD2, EPS, ALU.mult, ALU.add)])
                dve.wait_ge(S["qk_raw"], upto("qk_raw", w.b, tile + 1))
                qk = qkn[tile % 2].rearrange("p (h d) -> p h d", d=HD2)
                dve.tensor_tensor(qk, qk, qk_root[:, 1, :].unsqueeze(2).to_broadcast([128, 2 * NH, HD2]), ALU.mult)\
                   .then_inc(S["qkn"], 1)

            def c_pr(w, tile):
                dve.wait_ge(S["h2b"], upto("h2b", w.b))
                residual(w, ("c_pr", tile), "out_tm", hx, h_tm)

            def centre_weights():
                dve.wait_ge(loads["cqkv"], 16 * n_loads["cqkv"])
                for kc, k in ((0, HC + 1), (1, HC)):
                    wv = w_cqkv[0:k, kc, 0:qkw].rearrange("p (h d) -> p h d", d=HD2)
                    dve.tensor_reduce(w_mean[0:k, kc, :], wv, AX.X, ALU.add).then_inc(s_mean, 1)
                    dve.wait_ge(s_mean, kc + 1)
                    dve.scalar_tensor_tensor(out=wv, in0=w_mean[0:k, kc, :].unsqueeze(2).to_broadcast([k, 2 * NH, HD2]),
                                             scalar=-1.0 / HD2, in1=wv, op0=ALU.mult, op1=ALU.add)\
                       .then_inc(s_centred, 1)

            sections(dve, {"a_en": a_en, "a_x0": a_x0, "a_f2": lambda w, j: a_f2_chunk(w, "a_f2", j, 0),
                           "a_h2": lambda w, j: a_f2_chunk(w, "a_h2", j, 1), "a_s": a_s, "a_o": a_o,
                           "a_pr": a_pr, "b_ht": b_ht, "b_u": b_u, "b_in": b_in, "b_out": b_out, "b_k": b_k,
                           "b_s": lambda w, s: less_max(w, "b", s), "b_n": lambda w, s: weights(w, "b", s),
                           "b_pr": b_pr, "b_f2": b_f2,
                           "c_g": c_g, "c_qk": c_qk, "c_s": lambda w, s: less_max(w, "c", s), 
                           "c_n": lambda w, s: weights(w, "c", s),
                           "c_pr": c_pr,
                           "a_f1": lambda w, j: centre_weights() if w.section == "first" and j == 1 else None})

        @block.gpsimd
        def _(pool):
            pool.wait_ge(loads["vec"], 16 * n_loads["vec"])

            def spread(out_ap, in_ap, k):
                return pool.tensor_tensor(out_ap, in_ap.unsqueeze(1).to_broadcast([HC, 6, k]),
                                          w_mask[:, :].unsqueeze(2).to_broadcast([HC, 6, k]), ALU.mult)

            def a_s(w, t2):
                if t2 == 1:
                    pool.wait_ge(fill_sem(w, ("a_s", 0)), fill_count(w, ("a_s", 0)))
                else:
                    pool.wait_ge(S["a_kT"], upto("a_kT", w.a))
                for c in range(2):
                    spread(a_kB[:, c], a_kT[:, c, t2 * 128:(t2 + 1) * 128], 128).then_inc(S["a_kB"], 1)

            def b_s(w, s):
                if s >= 2:
                    pool.wait_ge(fill_sem(w, ("b_s", s - 2)), fill_count(w, ("b_s", s - 2)))
                else:
                    pool.wait_ge(S["b_kT"], upto("b_kT", w.b))
                for c in range(2):
                    spread(b_kBv[:, s % 2, c], b_kT[:, c, s * N:(s + 1) * N], N).then_inc(S["b_kB"], 1)

            def b_pr(w, tile):
                if tile < TILES_B - 1:
                    return
                pool.wait_ge(S["x2_tm"], upto("x2_tm", w.b))
                pool.wait_ge(S["out_dma"], upto("out_dma", w.b))
                bias = w_ff2_b[:, :].unsqueeze(1).to_broadcast([128, TILES_B, D])
                pool.tensor_tensor(hx[:, :, :], xr[:, :, :], h_tm[:, :, :], ALU.add).then_inc(S["hx"], 1)
                pool.wait_ge(S["hx"], upto("hx", w.b, 1))
                pool.tensor_tensor(hx[:, :, :], hx[:, :, :], bias, ALU.add).then_inc(S["hx"], 1)

            def b_f2(w, tile):
                if tile < TILES_B - 1:
                    return
                pool.wait_ge(S["h2_tm"], upto("h2_tm", w.b))
                bias = w_cproj_b[:, :].unsqueeze(1).to_broadcast([128, TILES_B, D])
                pool.tensor_tensor(h_tm[:, :, :], hx[:, :, :], bias, ALU.add).then_inc(S["h2b"], 1)

            sections(pool, {"a_s": a_s, "b_s": b_s, "b_pr": b_pr, "b_f2": b_f2})



def positions():
    pos = np.arange(NI, dtype=np.float32)[:, None]
    i = np.arange(D // 2, dtype=np.float32)[None, :]
    ang = pos / np.power(np.float32(10000.0), np.float32(2.0) * i / np.float32(D))
    pe = np.zeros((NI, D), np.float32)
    pe[:, 0::2] = np.sin(ang)
    pe[:, 1::2] = np.cos(ang)
    return pe


def chunked(a, rows):
    return np.ascontiguousarray(a.reshape(-1, rows, a.shape[-1]).transpose(1, 0, 2))


def with_bias(a, b):
    row = np.stack([b, np.zeros_like(b)])[None]
    return np.ascontiguousarray(np.concatenate([chunked(a, HC), row], axis=0))


def kernel(**inputs):
    import concourse.bacc as _bacc
    from concourse.bass_utils import run_bass_kernel_spmd as _run

    v = {k: np.asarray(a) for k, a in inputs.items()}
    tok, att, ffn = (lambda n: v["L0_tok_" + n]), (lambda n: v["L0_attn_" + n]), (lambda n: v["L0_ffn_" + n])
    per96 = lambda b: b.reshape(2, HC).T
    rows = lambda b: np.ascontiguousarray(np.broadcast_to(b, (128, D)))
    pix = v["x"].reshape(NG, GS, CH, IMG // P, P, IMG // P, P).transpose(0, 2, 4, 6, 1, 3, 5)
    arrays = {
        "xT": pix.reshape(NG, KP, 128, TA).transpose(0, 2, 1, 3),
        "txtT": v["txt"].reshape(NG, GS, NT, 2, HC).transpose(0, 4, 3, 1, 2),
        "patchT": chunked(tok("patch_w").reshape(D, -1).T, 128),
        "ident": np.eye(128, dtype=np.float32),
        "peT": positions().T.reshape(2, HC, NI).transpose(1, 0, 2),
        "mask": (np.arange(HC)[:, None] // HD == np.arange(6)[None]).astype(np.float32),
        "prio": np.broadcast_to(np.arange(EXPERTS, 0, -1).astype(np.float32), (N, EXPERTS)),
        "vec96": np.concatenate([per96(tok("ln_g")), per96(tok("ff2_b"))] +
                                [per96(att(f"ln{n}_{k}")) for n in (1, 2, 3) for k in "gb"] +
                                [per96(tok("ln_b"))], axis=1),
        "vec128": np.concatenate([att("conv_w").reshape(3, 128, KC).transpose(1, 0, 2).reshape(128, 3 * KC),
                                  att("conv_b").reshape(3, 128).T] +
                                 [np.concatenate([ffn(n), ffn(n)])[:, None] for n in
                                  ("q_norm_w", "q_norm_b", "k_norm_w", "k_norm_b")], axis=1),
        "patch_b": rows(tok("patch_b")),
        "tok_ff1": with_bias(tok("ff1_w"), tok("ff1_b")),
        "tok_ff2": chunked(tok("ff2_w"), 128),
        "tok_qkv": with_bias(tok("qkv_w"), tok("qkv_b")),
        "tok_proj": with_bias(tok("proj_w"), tok("proj_b")),
        "in_proj": chunked(att("in_proj_w"), HC),
        "out_proj": chunked(att("out_proj_w"), 128),
        "qkv": with_bias(att("qkv_w"), att("qkv_b")),
        "attn_proj": with_bias(att("attn_proj_w"), att("attn_proj_b")),
        "ffn1": with_bias(att("ffn1_w"), att("ffn1_b")),
        "ffn2": chunked(att("ffn2_w"), 128),
        "ffn2_b": rows(att("ffn2_b")),
        "cqkv": with_bias(ffn("qkv_w"), ffn("qkv_b")),
        "cproj": chunked(ffn("proj_w"), 128),
        "cproj_b": rows(ffn("proj_b")),
        "cgate": chunked(np.concatenate([ffn("wg_w"), ffn("wg0_w"), ffn("wg1_w")], axis=1), HC),
    }
    arrays = {k: np.ascontiguousarray(a) for k, a in arrays.items()}
    nc = _bacc.Bacc("TRN2", target_bir_lowering=False, num_devices=1)
    args = {k: nc.dram_tensor(f"in_{k}", a.shape, mybir.dt.from_np(a.dtype), kind="ExternalInput").ap()
            for k, a in arrays.items()}
    res = nc.dram_tensor("out", (B * N, D), F32, kind="ExternalOutput").ap()
    program(nc, **args, out=res.rearrange("(g t p) d -> g p t d", g=NG, p=128))
    r = _run(nc, [{f"in_{k}": a for k, a in arrays.items()}], core_ids=[0])
    return r.results[0]["out"].reshape(B, N, D)
```
